# Optimizing a Trainium2 kernel written in Bass

```python
import numpy as np
import jax
import jax.numpy as jnp

def _softmax(x, axis=-1):
    return jax.nn.softmax(x, axis=axis)

def _gelu(x):
    return jax.nn.gelu(x, approximate=True)

def _silu(x):
    return jax.nn.silu(x)

def _sigmoid(x):
    return jax.nn.sigmoid(x)

def _layernorm(x, axis=-1, eps=1e-05):
    m = jnp.mean(x, axis=axis, keepdims=True)
    v = jnp.var(x, axis=axis, keepdims=True)
    return (x - m) / jnp.sqrt(v + eps)

def _scatter_add(tgt, idx, src, axis=0):
    return tgt.at[idx].add(src)

def _segment_sum(src, seg, n):
    return jax.ops.segment_sum(src, seg, n)
kernel_name = 'mk_xattn_ffn_d1_seqx_r2_6a9774'

def setup_inputs(seed: int=0):
    np.random.seed(seed)
    _w = jnp.asarray

    def _rec_inputs():
        import jax
        import jax.numpy as jnp
        _rk = jax.random.key(seed)
        x = -0.000125 + 0.9999 * jax.random.normal(jax.random.fold_in(_rk, 1), (8, 512, 2048), jnp.float32)
        _lenS = 512 - jax.random.randint(jax.random.fold_in(_rk, 7), (8,), 0, max(1, 512 // 4) + 1, jnp.int32)
        _lenS2 = 512 - jax.random.randint(jax.random.fold_in(_rk, 8), (8,), 0, max(1, 512 // 4) + 1, jnp.int32)
        _ctx_4096P = jax.random.normal(jax.random.fold_in(_rk, 11), (8, 16, 2048), jnp.float32)
        _ctx_4096c = jax.random.dirichlet(jax.random.fold_in(_rk, 511), 0.3 * jnp.ones((16,), jnp.float32), (8, 512))
        _ctx_4096t = jnp.einsum('bsk,bkd->bsd', _ctx_4096c, _ctx_4096P)
        _ctx_4096t = _ctx_4096t * jax.lax.rsqrt(jnp.mean(jnp.square(_ctx_4096t)) + 1e-12) * 0.953939
        ctx_4096 = -1.52775e-05 + 0.999936 * (_ctx_4096t + 0.3 * jax.random.normal(jax.random.fold_in(_rk, 611), (8, 512, 2048), jnp.float32))
        return (x, ctx_4096)
    x, ctx_4096 = _rec_inputs()

    def _L0_xattn_setup():
        import jax, jax.numpy as jnp
        import numpy as np
        H = 8
        C = 2

        def _autocorrelation(Q, K, V):
            B, L, D = Q.shape
            d = D // H
            q = Q.reshape(B, L, H, d).transpose(0, 2, 1, 3)
            k = K.reshape(B, L, H, d).transpose(0, 2, 1, 3)
            v = V.reshape(B, L, H, d).transpose(0, 2, 1, 3)
            qf = jnp.fft.fft(q, axis=2)
            kf = jnp.fft.fft(k, axis=2)
            corr = jnp.fft.ifft(qf * jnp.conj(kf), axis=2).real
            topk = int(C * np.log(L))
            w, idx = jax.lax.top_k(corr.transpose(0, 1, 3, 2), topk)
            w = jax.nn.softmax(w, axis=-1)
            pos = jnp.arange(L)[:, None]
            out = jnp.zeros_like(v)
            for i in range(topk):
                g = jnp.minimum(idx[:, :, None, :, i] + pos, L - 1)
                out = out + w[:, :, None, :, i] * jnp.take_along_axis(v, g, axis=2)
            return out.transpose(0, 2, 1, 3).reshape(B, L, D)
        key = jax.random.key(seed)
        k1, k2, k3 = jax.random.split(key, 3)
        B, L, D = (16, 256, 2048)
        Q = jax.random.normal(k1, (B, L, D), dtype=jnp.float32)
        K = jax.random.normal(k2, (B, L, D), dtype=jnp.float32)
        V = jax.random.normal(k3, (B, L, D), dtype=jnp.float32)
        return {'Q': Q, 'K': K, 'V': V}
    _L0_xattn_all = _L0_xattn_setup()
    _L0_xattn_in = {k: v for k, v in _L0_xattn_all.items() if k in ()}
    del _L0_xattn_all

    def _L0_ffn_setup():
        import jax, jax.numpy as jnp
        import numpy as np
        B, T, D_IN, D_OUT = (8, 1024, 2048, 2048)
        N_LORAS, RANK = (16, 32)
        SCALING = 1.0
        key = jax.random.key(seed)
        ks = jax.random.split(key, 8)
        std = 1.0 / D_IN ** 0.5
        x = jax.random.normal(ks[0], (B, T, D_IN), dtype=jnp.float32)
        idx = jax.random.randint(ks[1], (B,), 0, N_LORAS)
        gate = jax.nn.one_hot(idx, N_LORAS, dtype=jnp.float32)
        kernel = jax.random.normal(ks[2], (D_IN, D_OUT), dtype=jnp.float32) * std
        bias = jnp.zeros((D_OUT,), dtype=jnp.float32)
        lora_A = jax.random.normal(ks[3], (N_LORAS, RANK, D_IN), dtype=jnp.float32) * std
        lora_B = jax.random.normal(ks[4], (N_LORAS, D_OUT, RANK), dtype=jnp.float32) * 0.01
        lora_A_shared = jax.random.normal(ks[5], (RANK, D_IN), dtype=jnp.float32) * std
        lora_B_shared = jax.random.normal(ks[6], (D_OUT, RANK), dtype=jnp.float32) * 0.01
        return {'x': x, 'gate': gate, 'kernel': kernel, 'bias': bias, 'lora_A': lora_A, 'lora_B': lora_B, 'lora_A_shared': lora_A_shared, 'lora_B_shared': lora_B_shared}
    _L0_ffn_all = _L0_ffn_setup()
    _L0_ffn_in = {k: v for k, v in _L0_ffn_all.items() if k in ('gate', 'kernel', 'bias', 'lora_A', 'lora_B', 'lora_A_shared', 'lora_B_shared')}
    del _L0_ffn_all
    return {'x': x, 'ctx_4096': ctx_4096, 'L0_ffn_gate': _L0_ffn_in['gate'], 'L0_ffn_kernel': _L0_ffn_in['kernel'], 'L0_ffn_bias': _L0_ffn_in['bias'], 'L0_ffn_lora_A': _L0_ffn_in['lora_A'], 'L0_ffn_lora_B': _L0_ffn_in['lora_B'], 'L0_ffn_lora_A_shared': _L0_ffn_in['lora_A_shared'], 'L0_ffn_lora_B_shared': _L0_ffn_in['lora_B_shared']}

def reference(x, ctx_4096, L0_ffn_gate, L0_ffn_kernel, L0_ffn_bias, L0_ffn_lora_A, L0_ffn_lora_B, L0_ffn_lora_A_shared, L0_ffn_lora_B_shared):
    import jax
    import jax.numpy as jnp

    def _L0_xattn_ref(Q, K, V):
        import jax, jax.numpy as jnp
        import numpy as np
        H = 8
        C = 2

        def _autocorrelation(Q, K, V):
            B, L, D = Q.shape
            d = D // H
            q = Q.reshape(B, L, H, d).transpose(0, 2, 1, 3)
            k = K.reshape(B, L, H, d).transpose(0, 2, 1, 3)
            v = V.reshape(B, L, H, d).transpose(0, 2, 1, 3)
            qf = jnp.fft.fft(q, axis=2)
            kf = jnp.fft.fft(k, axis=2)
            corr = jnp.fft.ifft(qf * jnp.conj(kf), axis=2).real
            topk = int(C * np.log(L))
            w, idx = jax.lax.top_k(corr.transpose(0, 1, 3, 2), topk)
            w = jax.nn.softmax(w, axis=-1)
            pos = jnp.arange(L)[:, None]
            out = jnp.zeros_like(v)
            for i in range(topk):
                g = jnp.minimum(idx[:, :, None, :, i] + pos, L - 1)
                out = out + w[:, :, None, :, i] * jnp.take_along_axis(v, g, axis=2)
            return out.transpose(0, 2, 1, 3).reshape(B, L, D)
        return _autocorrelation(Q, K, V)

    def _L0_ffn_ref(x, gate, kernel, bias, lora_A, lora_B, lora_A_shared, lora_B_shared):
        import jax, jax.numpy as jnp
        import numpy as np
        B, T, D_IN, D_OUT = (8, 1024, 2048, 2048)
        N_LORAS, RANK = (16, 32)
        SCALING = 1.0
        base_out = jnp.matmul(x, kernel) + bias
        b = gate.shape[0]
        x_flat = x.reshape(b, -1, x.shape[-1])
        A_eff = jnp.einsum('bn,nri->bri', gate, lora_A)
        B_eff = jnp.einsum('bn,nor->bor', gate, lora_B)
        Ax = jnp.einsum('bri,bti->btr', A_eff, x_flat)
        delta_flat = jnp.einsum('bor,btr->bto', B_eff, Ax)
        Ax_s = jnp.einsum('ri,bti->btr', lora_A_shared, x_flat)
        delta_flat = delta_flat + jnp.einsum('or,btr->bto', lora_B_shared, Ax_s)
        delta = delta_flat.reshape(x.shape[:-1] + (kernel.shape[-1],))
        return base_out + (SCALING * delta).astype(base_out.dtype)
    x = x + _L0_xattn_ref(_layernorm(x, axis=-1), ctx_4096, ctx_4096)
    x = x + _L0_ffn_ref(_layernorm(x, axis=-1), L0_ffn_gate, L0_ffn_kernel, L0_ffn_bias, L0_ffn_lora_A, L0_ffn_lora_B, L0_ffn_lora_A_shared, L0_ffn_lora_B_shared)
    return x

_drawn_inputs = setup_inputs


def setup_inputs(seed=0):
    import zlib

    import numpy as np

    out = dict(_drawn_inputs(seed))
    spreads = {'L0_ffn_bias': (0.0, 0.1)}
    factors = {}
    for name, (base, spread) in spreads.items():
        noise = np.random.default_rng([zlib.crc32(name.encode()), seed]).standard_normal(out[name].shape)
        drawn = base * np.exp(spread * noise) if base else spread * noise
        out[name] = jnp.asarray(drawn.astype(out[name].dtype))
    for name, factor in factors.items():
        out[name] = (out[name] * factor).astype(out[name].dtype)
    return out
```

```python
from contextlib import ExitStack

import concourse.bass as bass
import numpy as np
from concourse import mybir

FP32 = mybir.dt.float32
FP16 = mybir.dt.float16
U32 = mybir.dt.uint32
ALU = mybir.AluOpType
ACT = mybir.ActivationFunctionType
AXX = mybir.AxisListType.X

P = 128
B, L, D = 8, 512, 2048
TT = L // P
GC = 512
GPB = D // GC
NG = B * GPB
CT = GC // P
HALF = L // 2
TOPK = int(2 * np.log(L))
NT = B * TT
KT = D // P
NL, RANK = 16, 32
NLT = NL * RANK // P
EPS = 1e-5
NEG = float(np.float32(-3.0e38))
HSCALE = 1024.0
ER, EI, OR, OI = range(4)
assert TT == 4 and GPB == 4 and CT == 4 and 8 < TOPK <= 16


def dft_tables():
    n = np.arange(HALF)[:, None].astype(np.float64)
    f = np.arange(P)[None, :].astype(np.float64)
    even = 2 * np.pi * n * f / HALF
    odd = 2 * np.pi * n * (2 * f + 1) / L
    alt = (-1.0) ** np.arange(HALF)
    fwd = np.zeros((HALF, 5, P))
    fwd[:, ER], fwd[:, EI], fwd[:, OR], fwd[:, OI] = np.cos(even), -np.sin(even), np.cos(odd), -np.sin(odd)
    fwd[:, EI, 0] = alt
    fwd[:, 4] = -np.sin(even)
    fwd[:, 4, 0] = -alt
    inv = np.zeros((P, 4, HALF))
    inv[:, ER], inv[:, EI] = 2 * np.cos(even).T / L, -2 * np.sin(even).T / L
    inv[:, OR], inv[:, OI] = 2 * np.cos(odd).T / L, -2 * np.sin(odd).T / L
    inv[0, ER] = 1.0 / L
    inv[0, EI] = alt / L
    fwd = fwd.reshape(2, P, 5, P).transpose(1, 0, 2, 3)
    return np.ascontiguousarray(fwd, dtype=np.float32), np.ascontiguousarray(inv, dtype=np.float32)


def ahead(b, g, k):
    c = (g + k) // GPB
    return (b + c if c else b), (g + k) % GPB


def later(b, i):
    return not (isinstance(b, int) and b == 0 and i == 0)


def build(nc, x, ctx, gateT, w, bias, lora_a, lora_bT, lora_as, lora_bsT, fwd_tab, inv_tab, eye, rank_sel, nyq_mask, out):
    x2 = nc.dram_tensor("x2_scratch", [B, L, D + 1024], FP32).ap()[:, :, 0:D]
    beff = nc.dram_tensor("beff_scratch", [B * RANK, D], FP32).ap()
    a_pair = nc.dram_tensor("a_pair_scratch", [2, P, KT * (B + 1) * RANK], FP16).ap()
    x_g = x.rearrange("b (t p) c -> b p t c", p=P)
    ctx_g = ctx.rearrange("b (t p) c -> b p t c", p=P)
    x2_g = x2.rearrange("b (t p) c -> b p t c", p=P)
    w_t = w.rearrange("(k p) o -> k p o", p=P)

    with ExitStack() as outer:
        def sb(name, shape, dt=FP32, where=outer):
            return where.enter_context(nc.sbuf_tensor(name, shape, dt))

        def sem(name, where=outer):
            return where.enter_context(nc.semaphore(name))

        ident = sb("ident", [P, P])
        rs1 = sb("rs1", [P, NT])
        nb1 = sb("nb1", [P, NT])
        half = sb("half", [P, NT])
        w_scale = sb("w_scale", [P, 1])
        w_back = sb("w_back", [P, 1])
        ax_fix = sb("ax_fix", [P, 1])
        ps = outer.enter_context(nc.psum_tensor("ps", [P, 8, 512], FP32))

        with ExitStack() as st:
            xs = sb("xs", [P, TT, D], FP32, st)
            ws = sb("ws", [P, 2, D], FP32, st)
            bn = sb("bn", [P, TT, TT, 6], FP32, st)
            bn_all = sb("bn_all", [P, TT, TT * 6], FP32, st)
            mv4 = sb("mv4", [P, TT, 2], FP32, st)
            mv = sb("mv", [P, NT, 2], FP32, st)
            var_eps = sb("var_eps", [P, NT], FP32, st)
            negmean = sb("negmean", [P, NT], FP32, st)
            la = sb("la", [P, NLT, D], FP32, st)
            lb = sb("lb", [P, NLT, D], FP32, st)
            las = sb("las", [RANK, D], FP32, st)
            rsel = sb("rsel", [P, RANK], FP32, st)
            gcol = sb("gcol", [P, NLT, B], FP32, st)
            gsel = sb("gsel", [P, NLT, B, RANK], FP32, st)
            a_t = sb("a_t", [P, KT, B + 1, RANK], FP32, st)
            b_t = sb("b_t", [P, 2, D], FP32, st)
            a_hi = sb("a_hi1", [P, KT, B + 1, RANK], FP16, st)
            a_lo = sb("a_lo1", [P, KT, B + 1, RANK], FP16, st)
            wmax = sb("wmax", [P, KT], FP32, st)
            top = sb("top", [P, 2], FP32, st)
            topall = sb("topall", [P, 2], FP32, st)
            pow2 = sb("pow2", [P, 2], FP32, st)
            rpow = sb("rpow", [P, 2], FP32, st)
            scl = sb("scl", [P, 2], FP32, st)

            s_tab = sem("s_tab", st)
            s_lora = sem("s_lora", st)
            s_xs = [sem(f"s_xs{k}", st) for k in range(TT)]
            s_xs_used = sem("s_xs_used", st)
            s_ws = [sem(f"s_ws{k}", st) for k in range(2)]
            s_ws_used = sem("s_ws_used", st)
            s_gcol = sem("s_gcol", st)
            s_chain = sem("s_chain", st)
            s_var = sem("s_var", st)
            s_rs = sem("s_rs", st)
            s_gsel = sem("s_gsel", st)
            s_at = sem("s_at", st)
            s_at_out = sem("s_at_out", st)
            s_bt = sem("s_bt", st)
            s_bt_out = sem("s_bt_out", st)
            s_top = sem("s_top", st)
            s_topall = sem("s_topall", st)
            s_scale = sem("s_scale", st)
            s_ahi = sem("s_ahi", st)
            s_alo = sem("s_alo", st)
            s_store = sem("s_store", st)

            with nc.Block() as block:
                @block.sync
                def _(sp):
                    sp.dma_start(ident[:, :], eye).then_inc(s_tab, 16)
                    sp.dma_start(rsel[:, :], rank_sel).then_inc(s_tab, 16)
                    for k in range(TT):
                        sp.dma_start(xs[:, k, :], x_g[0, :, k, :]).then_inc(s_xs[k], 16)
                    with sp.Fori(1, B) as b:
                        for k in range(TT):
                            sp.wait_ge(s_xs_used, TT * b - TT + k + 1)
                            sp.dma_start(xs[:, k, :], x_g[b, :, k, :]).then_inc(s_xs[k], 16)
                    for k in range(KT):
                        if k >= 2:
                            sp.wait_ge(s_ws_used, k - 1)
                        sp.dma_start(ws[:, k % 2, :], w_t[k]).then_inc(s_ws[k % 2], 16)
                    sp.wait_ge(s_bt_out, 8)
                    sp.dma_start(beff.rearrange("(m p) o -> p m o", p=P), b_t[:, :, :]).then_inc(s_store, 16)
                    sp.wait_ge(s_ahi, 1)
                    sp.dma_start(a_pair[0], a_hi[:, :, :, :].rearrange("p k b r -> p (k b r)")).then_inc(s_store, 16)
                    sp.wait_ge(s_alo, 1)
                    sp.dma_start(a_pair[1], a_lo[:, :, :, :].rearrange("p k b r -> p (k b r)")).then_inc(s_store, 16)
                    sp.wait_ge(s_store, 48)

                @block.gpsimd
                def _(pool):
                    for n in range(P // RANK):
                        src = gateT.rearrange("(k n) b -> n k b", n=P // RANK)[n].partition_broadcast(RANK)
                        pool.dma_start(gcol[n * RANK:(n + 1) * RANK, :, :], src).then_inc(s_gcol, 16)
                    nc.gpsimd.memset(half[:, :], -0.5).then_inc(s_chain, 1)
                    pool.wait_ge(s_chain, 1)
                    pool.wait_ge(s_var, 1)
                    nc.gpsimd.tensor_tensor(rs1[:, :], var_eps[:, :], half[:, :], ALU.pow).then_inc(s_rs, 1)
                    pool.wait_ge(s_rs, 1)
                    nc.gpsimd.tensor_tensor(nb1[:, :], negmean[:, :], rs1[:, :], ALU.mult).then_inc(s_rs, 1)
                    pool.wait_ge(s_top, 2)
                    nc.gpsimd.partition_all_reduce(topall[:, :], top[:, :], P, bass.bass_isa.ReduceOp.max).then_inc(s_topall, 1)

                @block.scalar
                def _(act):
                    act.dma_start(la[:, :, :], lora_a.rearrange("(k p) i -> p k i", p=P)).then_inc(s_lora, 16)
                    act.dma_start(lb[:, :, :], lora_bT.rearrange("(k p) o -> p k o", p=P)).then_inc(s_lora, 16)
                    act.dma_start(las[:, :], lora_as).then_inc(s_lora, 16)
                    for i in range(KT):
                        act.wait_ge(s_at, i + 1)
                        nc.scalar.activation(a_t[:, i, :, :], ps[:, i % 4, 0:(B + 1) * RANK].rearrange("p (b r) -> p b r", r=RANK),
                                             ACT.Copy).then_inc(s_at_out, 1)
                    for i in range(8):
                        act.wait_ge(s_bt, i + 1)
                        nc.scalar.activation(b_t[:, i // 4, (i % 4) * 512:(i % 4 + 1) * 512], ps[:, 4 + i % 4, :],
                                             ACT.Copy).then_inc(s_bt_out, 1)
                    act.wait_ge(s_scale, 1)
                    nc.scalar.activation(a_hi[:, :, :, :], a_t[:, :, :, :], ACT.Copy, scale=scl[:, 1:2]).then_inc(s_ahi, 1)

                @block.tensor
                def _(pe):
                    pe.wait_ge(s_lora, 48)
                    pe.wait_ge(s_tab, 32)
                    pe.wait_ge(s_gsel, 1)
                    for i in range(KT):
                        if i >= 4:
                            pe.wait_ge(s_at_out, i - 3)
                        for k in range(NLT):
                            nc.tensor.matmul(ps[:, i % 4, 0:B * RANK], la[:, k, i * P:(i + 1) * P],
                                             gsel[:, k, :, :].rearrange("p b r -> p (b r)"), start=(k == 0), stop=(k == NLT - 1))
                        nc.tensor.matmul(ps[:, i % 4, B * RANK:(B + 1) * RANK], las[:, i * P:(i + 1) * P],
                                         ident[0:RANK, 0:RANK], start=True, stop=True).then_inc(s_at, 1)
                    for i in range(8):
                        if i >= 4:
                            pe.wait_ge(s_bt_out, i - 3)
                        for k in range(NLT):
                            last = nc.tensor.matmul(ps[:, 4 + i % 4, :],
                                                    gsel[:, k, 4 * (i // 4):4 * (i // 4) + 4, :].rearrange("p b r -> p (b r)"),
                                                    lb[:, k, (i % 4) * 512:(i % 4 + 1) * 512],
                                                    start=(k == 0), stop=(k == NLT - 1))
                        last.then_inc(s_bt, 1)

                @block.vector
                def _(dve):
                    chain = [0]

                    def link(ins):
                        chain[0] += 1
                        ins.then_inc(s_mine, 1)
                        dve.wait_ge(s_mine, chain[0])

                    s_mine = sem("s_mine", st)
                    dve.wait_ge(s_tab, 32)
                    dve.wait_ge(s_gcol, 16 * (P // RANK))
                    nc.vector.tensor_tensor(gsel[:, :, :, :].rearrange("p k b r -> p (k b) r"),
                                            gcol[:, :, :].rearrange("p k b -> p (k b)").unsqueeze(2).broadcast_to([P, NLT * B, RANK]),
                                            rsel[:, :].unsqueeze(1).broadcast_to([P, NLT * B, RANK]), ALU.mult).then_inc(s_gsel, 1)
                    s_own = sem("s_own", st)
                    s_mv = sem("s_mv", st)
                    with dve.Fori(0, B) as b:
                        for k in range(TT):
                            dve.wait_ge(s_xs[k], 16 * b + 16)
                            for c in range(TT):
                                last = nc.vector.bn_stats(bn[:, k, c, :], xs[:, k, c * 512:(c + 1) * 512])
                            last.then_inc(s_xs_used, 1)
                        dve.sem_clear(s_own)
                        dve.wait_ge(s_xs_used, TT * b + TT)
                        nc.vector.tensor_copy(bn_all[:, :, :], bn[:, :, :, :].rearrange("p k c s -> p k (c s)")).then_inc(s_own, 1)
                        dve.wait_ge(s_own, 1)
                        for k in range(TT):
                            last = nc.vector.bn_aggr(mv4[:, k, :], bn_all[:, k, :])
                        last.then_inc(s_own, 1)
                        dve.wait_ge(s_own, 2)
                        nc.vector.tensor_copy(mv[:, bass.ts(b, TT), :], mv4[:, :, :]).then_inc(s_mv, 1)
                    dve.wait_ge(s_mv, B)
                    nc.vector.tensor_scalar(negmean[:, :], mv[:, :, 0], -1.0, None, ALU.mult)
                    nc.vector.tensor_scalar(var_eps[:, :], mv[:, :, 1], EPS, None, ALU.add).then_inc(s_var, 1)
                    for k in range(KT):
                        dve.wait_ge(s_ws[k % 2], 16 * (k // 2 + 1))
                        nc.vector.tensor_reduce(wmax[:, k:k + 1], ws[:, k % 2, :], AXX, ALU.max,
                                                apply_absolute_value=True).then_inc(s_ws_used, 1)
                    dve.wait_ge(s_ws_used, KT)
                    nc.vector.tensor_reduce(top[:, 0:1], wmax[:, :], AXX, ALU.max).then_inc(s_top, 1)
                    dve.wait_ge(s_at_out, KT)
                    nc.vector.tensor_reduce(top[:, 1:2], a_t[:, :, :, :].rearrange("p k b r -> p (k b r)"), AXX, ALU.max,
                                            apply_absolute_value=True).then_inc(s_top, 1)
                    dve.wait_ge(s_topall, 1)
                    link(nc.vector.tensor_scalar(pow2[:, :], topall[:, :], 1e-30, None, ALU.max))
                    link(nc.vector.tensor_scalar(pow2[:, :].bitcast(U32), pow2[:, :].bitcast(U32), 0x7F800000, None, ALU.bitwise_and))
                    link(nc.vector.reciprocal(rpow[:, :], pow2[:, :]))
                    link(nc.vector.tensor_scalar(scl[:, :], rpow[:, :], 16384.0, None, ALU.mult))
                    nc.vector.tensor_copy(w_scale[:, :], scl[:, 0:1]).then_inc(s_scale, 1)
                    link(nc.vector.tensor_scalar(w_back[:, :], pow2[:, 0:1], 1.0 / (16384.0 * HSCALE), None, ALU.mult))
                    link(nc.vector.tensor_scalar(ax_fix[:, :], scl[:, 0:1], pow2[:, 1:2], 1.0 / 16384.0, ALU.mult, ALU.mult))
                    dve.wait_ge(s_ahi, 1)
                    nc.vector.scalar_tensor_tensor(out=a_lo[:, :, :, :].rearrange("p k b r -> p (k b r)"),
                                                   in0=a_t[:, :, :, :].rearrange("p k b r -> p (k b r)"), scalar=scl[:, 1:2],
                                                   in1=a_hi[:, :, :, :].rearrange("p k b r -> p (k b r)"),
                                                   op0=ALU.mult, op1=ALU.subtract).then_inc(s_alo, 1)

        with ExitStack() as st:
            ft = sb("ft", [P, 2, 5, P], FP32, st)
            it = sb("it", [P, 4, HALF], FP32, st)
            nyq = sb("nyq", [P, 1], FP32, st)
            xg = sb("xg", [P, 2, TT, GC], FP32, st)
            qa = sb("qa", [P, 2, 2, GC], FP32, st)
            cg = sb("cg", [P, 2, TT, GC], FP32, st)
            ua = sb("ua", [P, 2, 2, GC], FP32, st)
            vrow = sb("vrow", [P, 4, GC], FP32, st)
            xv = sb("xv", [P, 2, TT, GC], FP32, st)
            spe = sb("spe", [P, 2, 2, 3, GC], FP32, st)
            spo = sb("spo", [P, 2, 2, 2, GC], FP32, st)
            mr = sb("mr", [P, 4, GC], FP32, st)
            mi = sb("mi", [P, 4, GC], FP32, st)
            mhr = sb("mhr", [P, 2, GC], FP32, st)
            mhi = sb("mhi", [P, 2, GC], FP32, st)
            cp = sb("cp", [P, 4, GC], FP32, st)
            op = sb("op", [P, 2, 4, GC], FP32, st)
            eo = sb("eo", [P, CT, L], FP32, st)
            cr = sb("cr", [P, CT, L], FP32, st)
            wd = sb("wd", [P, CT, L], FP32, st)
            wt = sb("wt", [P, 4, GC], FP32, st)
            rsb = sb("rsb", [P, TT], FP32, st)
            nbb = sb("nbb", [P, TT], FP32, st)
            m16 = sb("m16", [P, CT, 16], FP32, st)
            nmax = sb("nmax", [P, CT], FP32, st)
            zsum = sb("zsum", [P, CT], FP32, st)
            rz = sb("rz", [P, CT], FP32, st)

            s_tabs = sem("s_tabs", st)
            s_x = [sem(f"s_x{k}", st) for k in range(2)]
            s_c = [sem(f"s_c{k}", st) for k in range(2)]
            s_v = [sem(f"s_v{k}", st) for k in range(2)]
            s_xr = [sem(f"s_xr{k}", st) for k in range(2)]
            s_st = [sem(f"s_st{k}", st) for k in range(2)]
            cols_ok = sem("cols_ok", st)
            q_norm = sem("q_norm", st)
            u_sub = sem("u_sub", st)
            u_fold = sem("u_fold", st)
            q_fold = sem("q_fold", st)
            xv_sum = sem("xv_sum", st)
            fwd_spec = sem("fwd_spec", st)
            spec_out = sem("spec_out", st)
            cprod = sem("cprod", st)
            cp_sum = sem("cp_sum", st)
            corr_spec = sem("corr_spec", st)
            corr_out = sem("corr_out", st)
            own = sem("own", st)
            nmax_ok = sem("nmax_ok", st)
            exp_ok = sem("exp_ok", st)
            w_ready = sem("w_ready", st)
            wt_spec = sem("wt_spec", st)
            wt_out = sem("wt_out", st)
            w_spec = sem("w_spec", st)
            oprod = sem("oprod", st)
            pair_sum = sem("pair_sum", st)
            op_sum = sem("op_sum", st)
            out_spec = sem("out_spec", st)
            out_add = sem("out_add", st)

            with nc.Block() as block:
                @block.sync
                def _(sp):
                    def load(b, g):
                        cols = slice(g * GC, (g + 1) * GC)
                        sp.dma_start(xg[:, g % 2, :, :], x_g[b, :, :, cols]).then_inc(s_x[g % 2], 16)
                        sp.dma_start(cg[:, g % 2, :, :], ctx_g[b, :, :, cols]).then_inc(s_c[g % 2], 16)
                        sp.dma_start(vrow[:, g, :], ctx[b, L - 1, cols].partition_broadcast(P)).then_inc(s_v[g % 2], 16)

                    def load_residual(b, g):
                        cols = slice(g * GC, (g + 1) * GC)
                        sp.dma_start(xv[:, g % 2, :, :], x_g[b, :, :, cols]).then_inc(s_xr[g % 2], 16)

                    def step(b, g, more, lead):
                        n = GPB * b + g
                        if more:
                            sp.wait_ge(fwd_spec, 12 * n + 24)
                            if later(b, g):
                                sp.wait_ge(xv_sum, n)
                            load(*ahead(b, g, 3))
                        if lead:
                            if g % 2 == 1:
                                sp.wait_ge(s_st[0], 16 * (2 * b + g // 2 + 1))
                            elif later(b, g):
                                sp.wait_ge(s_st[1], 16 * (2 * b + g // 2))
                            load_residual(*ahead(b, g, 1))
                        sp.wait_ge(out_add, 4 * n + 4)
                        sp.dma_start(x2_g[b, :, :, g * GC:(g + 1) * GC], xv[:, g % 2, :, :]).then_inc(s_st[g % 2], 16)

                    load(0, 0)
                    sp.dma_start(ft[:, :, :, :], fwd_tab).then_inc(s_tabs, 16)
                    sp.dma_start(it[:, :, :], inv_tab).then_inc(s_tabs, 16)
                    sp.dma_start(nyq[:, :], nyq_mask).then_inc(s_tabs, 16)
                    load(0, 1)
                    load_residual(0, 0)
                    sp.wait_ge(fwd_spec, 12)
                    load(0, 2)
                    for g in range(GPB):
                        step(0, g, True, True)
                    with sp.Fori(1, B - 1) as b:
                        for g in range(GPB):
                            step(b, g, True, True)
                    for g in range(GPB):
                        step(B - 1, g, g + 3 < GPB, g + 1 < GPB)
                    for k in range(2):
                        sp.wait_ge(s_st[k], 16 * NG // 2)

                @block.gpsimd
                def _(pool):
                    def prepare_u(b, g, free):
                        m, k = GPB * b + g, g % 2
                        seen = 16 * (2 * b + g // 2 + 1)
                        pool.wait_ge(s_c[k], seen)
                        pool.wait_ge(s_v[k], seen)
                        nc.gpsimd.tensor_tensor(cg[:, k, :, :], cg[:, k, :, :],
                                                vrow[:, g, :].unsqueeze(1).broadcast_to([P, TT, GC]),
                                                ALU.subtract).then_inc(u_sub, 1)
                        pool.wait_ge(u_sub, m + 1)
                        if free:
                            pool.wait_ge(fwd_spec, 12 * m - 12)
                        nc.gpsimd.tensor_tensor(ua[:, k, :, :], cg[:, k, 0:2, :], cg[:, k, 2:4, :], ALU.add).then_inc(u_fold, 1)
                        nc.gpsimd.tensor_tensor(cg[:, k, 0:2, :], cg[:, k, 0:2, :], cg[:, k, 2:4, :], ALU.subtract).then_inc(u_fold, 1)

                    def prepare_q(b, g):
                        m, k = GPB * b + g, g % 2
                        pool.wait_ge(q_norm, 4 * m + 4)
                        nc.gpsimd.tensor_tensor(qa[:, k, :, :], xg[:, k, 0:2, :], xg[:, k, 2:4, :], ALU.add).then_inc(q_fold, 1)
                        nc.gpsimd.tensor_tensor(xg[:, k, 0:2, :], xg[:, k, 0:2, :], xg[:, k, 2:4, :], ALU.subtract).then_inc(q_fold, 1)

                    def corr_sums(b, g):
                        m = GPB * b + g
                        if later(b, g):
                            pool.wait_ge(corr_spec, 4 * m)
                        pool.wait_ge(cprod, 4 * m + 4)
                        nc.gpsimd.tensor_tensor(cp[:, 0::2, :], mr[:, 0::2, :], mr[:, 1::2, :], ALU.add).then_inc(cp_sum, 1)
                        nc.gpsimd.tensor_tensor(cp[:, 1::2, :], mi[:, 1::2, :], mi[:, 0::2, :], ALU.subtract).then_inc(cp_sum, 1)

                    def residual(b, g):
                        pool.wait_ge(s_xr[g % 2], 16 * (2 * b + g // 2 + 1))
                        nc.gpsimd.tensor_tensor(xv[:, g % 2, :, :], xv[:, g % 2, :, :],
                                                vrow[:, g, :].unsqueeze(1).broadcast_to([P, TT, GC]), ALU.add).then_inc(xv_sum, 1)

                    def out_sums(b, g):
                        n = GPB * b + g
                        if later(b, g):
                            pool.wait_ge(out_spec, 4 * n)
                        for h in range(2):
                            r, i = 2 * h, 2 * h + 1
                            pool.wait_ge(oprod, 8 * n + 4 * h + 1)
                            nc.gpsimd.tensor_tensor(mr[:, 0:2, :], mr[:, 0:2, :], mr[:, 2:4, :], ALU.add).then_inc(pair_sum, 1)
                            pool.wait_ge(oprod, 8 * n + 4 * h + 2)
                            nc.gpsimd.tensor_tensor(mi[:, 0:2, :], mi[:, 0:2, :], mi[:, 2:4, :], ALU.add).then_inc(pair_sum, 1)
                            pool.wait_ge(pair_sum, 4 * n + 2 * h + 1)
                            nc.gpsimd.tensor_tensor(op[:, 0, r, :], mr[:, 0, :], mr[:, 1, :], ALU.add).then_inc(op_sum, 1)
                            pool.wait_ge(pair_sum, 4 * n + 2 * h + 2)
                            nc.gpsimd.tensor_tensor(op[:, 0, i, :], mi[:, 0, :], mi[:, 1, :], ALU.subtract).then_inc(op_sum, 1)
                            pool.wait_ge(oprod, 8 * n + 4 * h + 4)
                            nc.gpsimd.tensor_tensor(op[:, 1, r, :], mhr[:, 0, :], mhr[:, 1, :], ALU.add).then_inc(op_sum, 1)
                            nc.gpsimd.tensor_tensor(op[:, 1, i, :], mhi[:, 0, :], mhi[:, 1, :], ALU.subtract).then_inc(op_sum, 1)

                    def step(b, g, prepare, lead):
                        residual(b, g)
                        if prepare:
                            prepare_u(*ahead(b, g, 2), True)
                            prepare_q(*ahead(b, g, 2))
                        if lead:
                            corr_sums(*ahead(b, g, 1))
                        out_sums(b, g)

                    for g in range(2):
                        prepare_u(0, g, False)
                        prepare_q(0, g)
                        if g == 0:
                            pass
                    corr_sums(0, 0)
                    for g in range(GPB):
                        step(0, g, True, True)
                    with pool.Fori(1, B - 1) as b:
                        for g in range(GPB):
                            step(b, g, True, True)
                    for g in range(GPB):
                        step(B - 1, g, g + 2 < GPB, g + 1 < GPB)

                @block.scalar
                def _(act):
                    def normalise(b, g):
                        k = g % 2
                        if g == 0:
                            cols = bass.ts(b, TT)
                            nc.scalar.activation(rsb[:, :], rs1[:, cols], ACT.Copy).then_inc(cols_ok, 1)
                            nc.scalar.activation(nbb[:, :], nb1[:, cols], ACT.Copy).then_inc(cols_ok, 1)
                            act.wait_ge(cols_ok, 2 * b + 2)
                        act.wait_ge(s_x[k], 16 * (2 * b + g // 2 + 1))
                        for t in range(TT):
                            nc.scalar.activation(xg[:, k, t, :], xg[:, k, t, :], ACT.Identity,
                                                 bias=nbb[:, t:t + 1], scale=rsb[:, t:t + 1]).then_inc(q_norm, 1)

                    def store_spectrum(b, g, which):
                        m, k, bank = GPB * b + g, g % 2, 4 * which
                        act.wait_ge(fwd_spec, 12 * m + 4 * which + 1)
                        nc.scalar.activation(spe[:, k, which, 0::2, :], ps[:, bank, :].unsqueeze(1).broadcast_to([P, 2, GC]),
                                             ACT.Copy).then_inc(spec_out, 1)
                        act.wait_ge(fwd_spec, 12 * m + 4 * which + 2)
                        nc.scalar.activation(spe[:, k, which, 1, :], ps[:, bank + 1, :], ACT.Copy, scale=nyq[:, 0:1]).then_inc(spec_out, 1)
                        act.wait_ge(spec_out, 8 * m + 4 * which + 1)
                        nc.scalar.activation(spe[0:1, k, which, 2, :], ps[0:1, bank + 1, :], ACT.Copy).then_inc(spec_out, 1)
                        act.wait_ge(fwd_spec, 12 * m + 4 * which + 4)
                        nc.scalar.activation(spo[:, k, which, :, :], ps[:, bank + 2:bank + 4, :], ACT.Copy).then_inc(spec_out, 1)

                    def corr_and_exp(b, g):
                        m = GPB * b + g
                        if later(b, g):
                            act.wait_ge(w_ready, 4 * m)
                        for j in range(CT):
                            act.wait_ge(corr_spec, 4 * m + j + 1)
                            nc.scalar.activation(eo[:, j, :], ps[:, j, :], ACT.Copy).then_inc(corr_out, 1)
                        act.wait_ge(nmax_ok, m + 1)
                        if later(b, g):
                            act.wait_ge(wt_spec, 4 * m)
                        for j in range(CT):
                            nc.scalar.activation(wd[:, j, :], cr[:, j, :], ACT.Exp, bias=nmax[:, j:j + 1]).then_inc(exp_ok, 1)

                    def transposed_out(b, g):
                        n = GPB * b + g
                        if later(b, g):
                            act.wait_ge(w_spec, 8 * n)
                        for k in range(4):
                            act.wait_ge(wt_spec, 4 * n + k + 1)
                            nc.scalar.activation(wt[:, k, :], ps[:, 4 + k, :], ACT.Copy).then_inc(wt_out, 1)

                    def step(b, g, prepare, lead):
                        n = GPB * b + g
                        nxt = ahead(b, g, 1)
                        if lead:
                            if later(b, g):
                                act.wait_ge(oprod, 8 * n)
                            store_spectrum(*nxt, 0)
                            store_spectrum(*nxt, 1)
                        if prepare:
                            normalise(*ahead(b, g, 2))
                        transposed_out(b, g)
                        if lead:
                            corr_and_exp(*nxt)

                    normalise(0, 0)
                    normalise(0, 1)
                    act.wait_ge(s_tabs, 48)
                    store_spectrum(0, 0, 0)
                    store_spectrum(0, 0, 1)
                    corr_and_exp(0, 0)
                    for g in range(GPB):
                        step(0, g, True, True)
                    with act.Fori(1, B - 1) as b:
                        for g in range(GPB):
                            step(b, g, True, True)
                    for g in range(GPB):
                        step(B - 1, g, g + 2 < GPB, g + 1 < GPB)

                @block.tensor
                def _(pe):
                    def forward(bank, kind, src):
                        for k in range(2):
                            last = nc.tensor.matmul(ps[:, bank, :], ft[:, k, kind, :], src[k], start=(k == 0), stop=(k == 1))
                        return last

                    def input_spectra(b, g):
                        m, k = GPB * b + g, g % 2
                        first, second = (lambda s: [s[:, k, t, :] for t in (0, 1)]), (lambda s: [s[:, k, t, :] for t in (2, 3)])
                        pe.wait_ge(u_fold, 2 * m + 2)
                        for i in range(4):
                            if later(b, g):
                                pe.wait_ge(corr_out, 4 * m - 3 + i)
                            forward(i, i, first(ua if i < 2 else cg)).then_inc(fwd_spec, 1)
                        if later(b, g) and later(b, g - 1):
                            pe.wait_ge(out_add, 4 * m - 4)
                        for i in range(4):
                            forward(4 + i, i, second(cg)).then_inc(fwd_spec, 1)
                        pe.wait_ge(q_fold, 2 * m + 2)
                        for i in range(4):
                            pe.wait_ge(spec_out, 8 * m + (1, 3, 4, 4)[i])
                            forward(i, i, first(qa if i < 2 else xg)).then_inc(fwd_spec, 1)

                    def weight_spectra(b, g, lead):
                        n = GPB * b + g
                        pe.wait_ge(w_ready, 4 * n + 4)
                        for k in range(4):
                            if lead:
                                pe.wait_ge(spec_out, 8 * n + 8 + (5, 7, 8, 8)[k])
                            else:
                                pe.wait_ge(out_add, 4 * n)
                            for j in range(CT):
                                last = nc.tensor.transpose(ps[:, 4 + k, j * P:(j + 1) * P], wd[:, j, k * P:(k + 1) * P], ident[:, :])
                            last.then_inc(wt_spec, 1)
                        for i in range(4):
                            if lead:
                                pe.wait_ge(cprod, 4 * n + 4 + (2, 2, 4, 4)[i])
                            pe.wait_ge(wt_out, 4 * n + (2, 2, 4, 4)[i])
                            src = [wt[:, 2 * (i // 2) + k, :] for k in range(2)]
                            forward(i, (ER, 4)[i % 2], src).then_inc(w_spec, 1)
                        for i in range(4):
                            src = [wt[:, 2 * (i // 2) + k, :] for k in range(2)]
                            forward(4 + i, (OR, OI)[i % 2], src).then_inc(w_spec, 1)

                    def correlation(b, g):
                        m = GPB * b + g
                        if later(b, g):
                            pe.wait_ge(oprod, 8 * m - 4)
                        pe.wait_ge(cp_sum, 2 * m + 2)
                        for j in range(CT):
                            for h in range(2):
                                for i in range(2):
                                    s = 2 * h + i
                                    last = nc.tensor.matmul(ps[:, j, h * HALF:(h + 1) * HALF], cp[:, s, j * P:(j + 1) * P],
                                                            it[:, s, :], start=(i == 0), stop=(i == 1))
                            last.then_inc(corr_spec, 1)

                    def output(b, g):
                        n = GPB * b + g
                        pe.wait_ge(oprod, 8 * n + 8)
                        pe.wait_ge(op_sum, 8 * n + 8)
                        for t in range(TT):
                            for s in range(4):
                                last = nc.tensor.matmul(ps[:, 4 + t, :], it[:, s, (t % 2) * P:(t % 2 + 1) * P], op[:, t // 2, s, :],
                                                        start=(s == 0), stop=(s == 3))
                            last.then_inc(out_spec, 1)

                    def step(b, g, lead):
                        nxt = ahead(b, g, 1)
                        if lead:
                            input_spectra(*nxt)
                        weight_spectra(b, g, lead)
                        if lead:
                            correlation(*nxt)
                        output(b, g)

                    pe.wait_ge(s_tabs, 48)
                    input_spectra(0, 0)
                    correlation(0, 0)
                    for g in range(GPB):
                        step(0, g, True)
                    with pe.Fori(1, B - 1) as b:
                        for g in range(GPB):
                            step(b, g, True)
                    for g in range(GPB):
                        step(B - 1, g, g + 1 < GPB)

                @block.vector
                def _(dve):
                    def swapped(t, k, which):
                        return t[:, k, which, ::-1, :]

                    def corr_products(b, g):
                        m, k = GPB * b + g, g % 2
                        if later(b, g) and later(b, g - 1):
                            dve.wait_ge(op_sum, 8 * m - 8)
                        dve.wait_ge(spec_out, 8 * m + 4)
                        dve.wait_ge(fwd_spec, 12 * m + 10)
                        nc.vector.tensor_tensor(mr[:, 0:2, :], ps[:, 0:2, :], spe[:, k, 0, 0:2, :], ALU.mult).then_inc(cprod, 1)
                        nc.vector.tensor_tensor(mi[:, 0:2, :], ps[:, 0:2, :], spe[:, k, 0, 1:3, :], ALU.mult).then_inc(cprod, 1)
                        dve.wait_ge(fwd_spec, 12 * m + 12)
                        nc.vector.tensor_tensor(mr[:, 2:4, :], ps[:, 2:4, :], spo[:, k, 0, :, :], ALU.mult).then_inc(cprod, 1)
                        nc.vector.tensor_tensor(mi[:, 2:4, :], ps[:, 2:4, :], swapped(spo, k, 0), ALU.mult).then_inc(cprod, 1)

                    def out_products(b, g, lead):
                        n, k = GPB * b + g, g % 2
                        dve.wait_ge(spec_out, 8 * n + 8)
                        for h in range(2):
                            if h == 0:
                                dve.wait_ge(cp_sum, 2 * n + (4 if lead else 2))
                                if later(b, g):
                                    dve.wait_ge(op_sum, 8 * n)
                            else:
                                dve.wait_ge(op_sum, 8 * n + 4)
                            dve.wait_ge(w_spec, 8 * n + 4 * h + 4)
                            wl, wlh = ps[:, 4 * h:4 * h + 2, :], ps[:, 4 * h:4 * h + 4, :].rearrange("p (a r) c -> p a r c", a=2)
                            if h == 0:
                                v_r, v_i, vh_r, vh_i = spe[:, k, :, 0:2, :], spe[:, k, :, 1:3, :], spe[:, k, 1, 0:2, :], spe[:, k, 1, 1:3, :]
                            else:
                                v_r, v_i, vh_r, vh_i = spo[:, k, :, :, :], spo[:, k, :, ::-1, :], spo[:, k, 1, :, :], swapped(spo, k, 1)
                            split = "p (a r) c -> p a r c"
                            nc.vector.tensor_tensor(mr[:, :, :].rearrange(split, a=2), wlh, v_r, ALU.mult).then_inc(oprod, 1)
                            nc.vector.tensor_tensor(mi[:, :, :].rearrange(split, a=2), wlh, v_i, ALU.mult).then_inc(oprod, 1)
                            nc.vector.tensor_tensor(mhr[:, :, :], wl, vh_r, ALU.mult).then_inc(oprod, 1)
                            nc.vector.tensor_tensor(mhi[:, :, :], wl, vh_i, ALU.mult).then_inc(oprod, 1)

                    def top_lags(b, g):
                        m = GPB * b + g
                        dve.sem_clear(own)
                        if later(b, g):
                            dve.wait_ge(exp_ok, 4 * m)
                        for j in range(CT):
                            dve.wait_ge(corr_out, 4 * m + j + 1)
                            nc.vector.tensor_tensor(cr[:, j, 0:HALF], eo[:, j, 0:HALF], eo[:, j, HALF:L], ALU.add)
                            nc.vector.tensor_tensor(cr[:, j, HALF:L], eo[:, j, 0:HALF], eo[:, j, HALF:L], ALU.subtract).then_inc(own, 1)
                        for j in range(CT):
                            dve.wait_ge(own, j + 1)
                            nc.vector.max(m16[:, j, 0:8], cr[:, j, :]).then_inc(own, 1)
                        dve.wait_ge(own, 2 * CT)
                        nc.vector.tensor_scalar(nmax[:, :], m16[:, :, 0], -1.0, None, ALU.mult).then_inc(nmax_ok, 1)
                        for j in range(CT):
                            nc.vector.match_replace(eo[:, j, :], m16[:, j, 0:8], cr[:, j, :], NEG).then_inc(own, 1)
                        for j in range(CT):
                            dve.wait_ge(own, 2 * CT + j + 1)
                            nc.vector.max(m16[:, j, 8:16], eo[:, j, :]).then_inc(own, 1)
                        dve.wait_ge(own, 4 * CT)
                        nc.vector.memset(m16[:, :, TOPK:16], NEG).then_inc(own, 1)
                        dve.wait_ge(own, 4 * CT + 1)
                        for j in range(CT):
                            nc.vector.match_replace(eo[:, j, :], m16[:, j, 8:16], eo[:, j, :], NEG).then_inc(own, 1)
                        dve.wait_ge(exp_ok, 4 * m + 4)
                        for j in range(CT):
                            dve.wait_ge(own, 4 * CT + j + 2)
                            nc.vector.scalar_tensor_tensor(out=wd[:, j, :], in0=eo[:, j, :], scalar=NEG, in1=wd[:, j, :],
                                                           op0=ALU.is_le, op1=ALU.mult, accum_out=zsum[:, j:j + 1]).then_inc(own, 1)
                        dve.wait_ge(own, 6 * CT + 1)
                        nc.vector.reciprocal(rz[:, :], zsum[:, :]).then_inc(own, 1)
                        dve.wait_ge(own, 6 * CT + 2)
                        for j in range(CT):
                            nc.vector.tensor_scalar(wd[:, j, :], wd[:, j, :], rz[:, j:j + 1], None, ALU.mult).then_inc(w_ready, 1)

                    def add_output(b, g):
                        n = GPB * b + g
                        dve.wait_ge(xv_sum, n + 1)
                        for t in range(TT):
                            dve.wait_ge(out_spec, 4 * n + t + 1)
                            nc.vector.tensor_tensor(xv[:, g % 2, t, :], ps[:, 4 + t, :], xv[:, g % 2, t, :], ALU.add).then_inc(out_add, 1)

                    def step(b, g, lead):
                        nxt = ahead(b, g, 1)
                        if lead:
                            corr_products(*nxt)
                        out_products(b, g, lead)
                        if lead:
                            top_lags(*nxt)
                        add_output(b, g)

                    corr_products(0, 0)
                    top_lags(0, 0)
                    for g in range(GPB):
                        step(0, g, True)
                    with dve.Fori(1, B - 1) as b:
                        for g in range(GPB):
                            step(b, g, True)
                    for g in range(GPB):
                        step(B - 1, g, g + 1 < GPB)

        with ExitStack() as st:
            w_hi = sb("w_hi", [P, KT, D], FP16, st)
            w_lo = sb("w_lo", [P, KT, D], FP16, st)
            a_hi = sb("a_hi", [P, KT, B + 1, RANK], FP16, st)
            a_lo = sb("a_lo", [P, KT, B + 1, RANK], FP16, st)
            xt = sb("xt", [P, 2, D], FP32, st)
            h = sb("h", [P, D], FP32, st)
            h_hi = sb("h_hi", [P, 2, KT, P], FP16, st)
            h_lo = sb("h_lo", [P, 2, KT, P], FP16, st)
            bcat = sb("bcat", [2 * RANK, D], FP32, st)
            brow = sb("brow", [P, D], FP32, st)
            bn2 = sb("bn2", [P, 4, 6], FP32, st)
            mv2 = sb("mv2", [P, 2], FP32, st)
            ve2 = sb("ve2", [P, 1], FP32, st)
            rp2 = sb("rp2", [P, 1], FP32, st)
            rs2 = sb("rs2", [P, 1], FP32, st)
            nb2 = sb("nb2", [P, 1], FP32, st)
            ax = sb("ax", [P, 2 * RANK], FP32, st)
            axT = sb("axT", [2 * RANK, P], FP32, st)

            s_row = sem("s_row", st)
            s_b = sem("s_b", st)
            s_wl = [sem(f"s_wl{k}", st) for k in range(2)]
            wh_ok = sem("wh_ok", st)
            wl_ok = sem("wl_ok", st)
            s_xt = [sem(f"s_xt{k}", st) for k in range(2)]
            s_out = [sem(f"s_out{k}", st) for k in range(2)]
            own2 = sem("own2", st)
            ve_ok = sem("ve_ok", st)
            rp_ok = sem("rp_ok", st)
            nb_ok = sem("nb_ok", st)
            h_ok = sem("h_ok", st)
            bias_ok = sem("bias_ok", st)
            ht_spec = sem("ht_spec", st)
            hi_ok = sem("hi_ok", st)
            lo_ok = sem("lo_ok", st)
            ax_spec = sem("ax_spec", st)
            ax_ok = sem("ax_ok", st)
            axt_spec = sem("axt_spec", st)
            axt_ok = sem("axt_ok", st)
            y_spec = sem("y_spec", st)
            y_ok = sem("y_ok", st)

            with nc.Block() as block:
                out_t = out.rearrange("b (t p) c -> b p t c", p=P)

                @block.sync
                def _(sp):
                    def load(b, t):
                        sp.dma_start(xt[:, t % 2, :], x2_g[b, :, t, :]).then_inc(s_xt[t % 2], 16)

                    def load_b(b):
                        sp.dma_start(bcat[0:RANK, :], beff[bass.ts(b, RANK), :]).then_inc(s_b, 16)

                    sp.dma_start(brow[:, :], bias.partition_broadcast(P)).then_inc(s_row, 16)
                    sp.dma_start(bcat[RANK:2 * RANK, :], lora_bsT).then_inc(s_row, 16)
                    sp.dma_start(a_hi[:, :, :, :].rearrange("p k b r -> p (k b r)"), a_pair[0]).then_inc(s_row, 16)
                    sp.dma_start(a_lo[:, :, :, :].rearrange("p k b r -> p (k b r)"), a_pair[1]).then_inc(s_row, 16)
                    for k in range(KT):
                        if k >= 2:
                            sp.wait_ge(wl_ok, k - 1)
                        sp.dma_start(xt[:, k % 2, :], w_t[k]).then_inc(s_wl[k % 2], 16)
                    load_b(0)
                    for t in range(2):
                        sp.wait_ge(wl_ok, KT - 1 + t)
                        load(0, t)

                    def step(b, t, more):
                        n = TT * b + t
                        sp.wait_ge(y_ok, 4 * n + 4)
                        sp.dma_start(out_t[b, :, t, :], xt[:, t % 2, :]).then_inc(s_out[t % 2], 16)
                        if more:
                            if t == TT - 1:
                                load_b(b + 1)
                            sp.wait_ge(s_out[t % 2], 16 * (2 * b + t // 2 + 1))
                            load(*ahead(b, t, 2))

                    for t in range(TT):
                        step(0, t, True)
                    with sp.Fori(1, B - 1) as b:
                        for t in range(TT):
                            step(b, t, True)
                    for t in range(TT):
                        step(B - 1, t, t + 2 < TT)
                    for k in range(2):
                        sp.wait_ge(s_out[k], 16 * NT // 2)

                @block.gpsimd
                def _(pool):
                    def prepare(b, t):
                        n = TT * b + t
                        pool.wait_ge(ve_ok, n + 1)
                        nc.gpsimd.tensor_tensor(rp2[:, :], ve2[:, :], half[:, 0:1], ALU.pow).then_inc(rp_ok, 1)
                        pool.wait_ge(h_ok, n + 1)
                        nc.gpsimd.tensor_tensor(xt[:, t % 2, :], xt[:, t % 2, :], brow[:, :], ALU.add).then_inc(bias_ok, 1)

                    pool.wait_ge(s_row, 64)
                    with pool.Fori(0, B) as b:
                        for t in range(TT):
                            prepare(b, t)

                @block.scalar
                def _(act):
                    for k in range(KT):
                        act.wait_ge(s_wl[k % 2], 16 * (k // 2 + 1))
                        nc.scalar.activation(w_hi[:, k, :], xt[:, k % 2, :], ACT.Copy, scale=w_scale[:, 0:1]).then_inc(wh_ok, 1)

                    def prepare(b, t):
                        n, k = TT * b + t, t % 2
                        act.wait_ge(s_xt[k], 16 * (2 * b + t // 2 + 1))
                        act.wait_ge(nb_ok, n + 1)
                        if later(b, t):
                            act.wait_ge(ht_spec, 4 * n)
                        nc.scalar.activation(h[:, :], xt[:, k, :], ACT.Identity, bias=nb2[:, 0:1], scale=rs2[:, 0:1]).then_inc(h_ok, 1)
                        if later(b, t) and later(b, t - 1):
                            act.wait_ge(y_spec, 4 * n - 4)
                        for q in range(4):
                            act.wait_ge(ht_spec, 4 * n + q + 1)
                            nc.scalar.activation(h_hi[:, k, 4 * q:4 * q + 4, :], ps[:, 4 + q, :].rearrange("p (c t) -> p c t", t=P),
                                                 ACT.Copy).then_inc(hi_ok, 1)
                        act.wait_ge(axt_spec, n + 1)
                        if later(b, t):
                            act.wait_ge(y_spec, 4 * n)
                        nc.scalar.activation(axT[:, :], ps[0:2 * RANK, 5, 0:P], ACT.Copy).then_inc(axt_ok, 1)

                    for t in range(TT):
                        prepare(0, t)
                    with act.Fori(1, B) as b:
                        for t in range(TT):
                            prepare(b, t)

                @block.tensor
                def _(pe):
                    def transposes(b, t):
                        n = TT * b + t
                        pe.wait_ge(h_ok, n + 1)
                        if later(b, t):
                            pe.wait_ge(axt_ok, n)
                        for q in range(4):
                            for c in range(4):
                                i = 4 * q + c
                                last = nc.tensor.transpose(ps[:, 4 + q, c * P:(c + 1) * P], h[:, i * P:(i + 1) * P], ident[:, :])
                            last.then_inc(ht_spec, 1)

                    def adapter_in(b, t):
                        n, k = TT * b + t, t % 2
                        pe.wait_ge(hi_ok, 4 * n + 4)
                        pe.wait_ge(lo_ok, 4 * n + 4)
                        bank = ps[:, 4, 0:2 * RANK]
                        for s, own in enumerate((True, False)):
                            dst = bank[:, s * RANK:(s + 1) * RANK]
                            for i in range(KT):
                                def a_of(a):
                                    return a[:, i, bass.ds(b, 1), :].squeeze(1) if own else a[:, i, B, :]
                                nc.tensor.matmul(dst, h_hi[:, k, i, :], a_of(a_hi), start=(i == 0), stop=False)
                                nc.tensor.matmul(dst, h_hi[:, k, i, :], a_of(a_lo), start=False, stop=False)
                                last = nc.tensor.matmul(dst, h_lo[:, k, i, :], a_of(a_hi), start=False, stop=(i == KT - 1))
                        last.then_inc(ax_spec, 1)

                    def chunk(b, t, c):
                        n, k = TT * b + t, t % 2
                        if later(b, t):
                            pe.wait_ge(y_ok, 4 * n)
                        cols = slice(c * 512, (c + 1) * 512)
                        for i in range(KT):
                            nc.tensor.matmul(ps[:, c, :], h_hi[:, k, i, :], w_hi[:, i, cols], start=(i == 0), stop=False)
                            nc.tensor.matmul(ps[:, c, :], h_hi[:, k, i, :], w_lo[:, i, cols], start=False, stop=False)
                            nc.tensor.matmul(ps[:, c, :], h_lo[:, k, i, :], w_hi[:, i, cols], start=False, stop=False)
                        if c == 0:
                            pe.wait_ge(ax_ok, n + 1)
                            nc.tensor.matmul(ps[0:2 * RANK, 5, 0:P], ax[:, :], ident[:, :], start=True, stop=True).then_inc(axt_spec, 1)
                            pe.wait_ge(axt_ok, n + 1)
                            pe.wait_ge(s_b, 16 * b + 16)
                        nc.tensor.matmul(ps[:, c, :], axT[:, :], bcat[:, cols], start=False, stop=True).then_inc(y_spec, 1)

                    def step(b, t, more):
                        nxt = ahead(b, t, 1)
                        chunk(b, t, 0)
                        chunk(b, t, 1)
                        if more:
                            transposes(*nxt)
                        chunk(b, t, 2)
                        chunk(b, t, 3)
                        if more:
                            adapter_in(*nxt)

                    transposes(0, 0)
                    pe.wait_ge(s_row, 64)
                    adapter_in(0, 0)
                    pe.wait_ge(wh_ok, KT)
                    pe.wait_ge(wl_ok, KT)
                    for t in range(TT):
                        step(0, t, True)
                    with pe.Fori(1, B - 1) as b:
                        for t in range(TT):
                            step(b, t, True)
                    for t in range(TT):
                        step(B - 1, t, t + 1 < TT)

                @block.vector
                def _(dve):
                    for k in range(KT):
                        dve.wait_ge(wh_ok, k + 1)
                        nc.vector.scalar_tensor_tensor(out=w_lo[:, k, :], in0=xt[:, k % 2, :], scalar=w_scale[:, 0:1],
                                                       in1=w_hi[:, k, :], op0=ALU.mult, op1=ALU.subtract).then_inc(wl_ok, 1)

                    def statistics(b, t):
                        n, k = TT * b + t, t % 2
                        dve.sem_clear(own2)
                        dve.wait_ge(s_xt[k], 16 * (2 * b + t // 2 + 1))
                        for c in range(4):
                            last = nc.vector.bn_stats(bn2[:, c, :], xt[:, k, c * 512:(c + 1) * 512])
                        last.then_inc(own2, 1)
                        dve.wait_ge(own2, 1)
                        nc.vector.bn_aggr(mv2[:, :], bn2[:, :, :].rearrange("p c s -> p (c s)")).then_inc(own2, 1)
                        dve.wait_ge(own2, 2)
                        nc.vector.tensor_scalar(ve2[:, :], mv2[:, 1:2], EPS, None, ALU.add).then_inc(ve_ok, 1)
                        dve.wait_ge(rp_ok, n + 1)
                        if later(b, t):
                            dve.wait_ge(h_ok, n)
                        nc.vector.tensor_scalar(rs2[:, :], rp2[:, :], HSCALE, None, ALU.mult).then_inc(own2, 1)
                        dve.wait_ge(own2, 3)
                        nc.vector.tensor_scalar(nb2[:, :], mv2[:, 0:1], rs2[:, 0:1], -1.0, ALU.mult, ALU.mult).then_inc(nb_ok, 1)

                    def rest_of_h(b, t):
                        n, k = TT * b + t, t % 2
                        for q in range(4):
                            dve.wait_ge(hi_ok, 4 * n + q + 1)
                            nc.vector.tensor_tensor(h_lo[:, k, 4 * q:4 * q + 4, :], ps[:, 4 + q, :].rearrange("p (c t) -> p c t", t=P),
                                                    h_hi[:, k, 4 * q:4 * q + 4, :], ALU.subtract).then_inc(lo_ok, 1)

                    def adapter(b, t):
                        n = TT * b + t
                        dve.wait_ge(ax_spec, n + 1)
                        if later(b, t):
                            dve.wait_ge(axt_spec, n)
                        nc.vector.tensor_scalar(ax[:, :], ps[:, 4, 0:2 * RANK], ax_fix[:, 0:1], None, ALU.mult).then_inc(ax_ok, 1)

                    def finish(b, t, c):
                        n, k = TT * b + t, t % 2
                        if c == 0:
                            dve.wait_ge(bias_ok, n + 1)
                        dve.wait_ge(y_spec, 4 * n + c + 1)
                        cols = slice(c * 512, (c + 1) * 512)
                        nc.vector.scalar_tensor_tensor(out=xt[:, k, cols], in0=ps[:, c, :], scalar=w_back[:, 0:1], in1=xt[:, k, cols],
                                                       op0=ALU.mult, op1=ALU.add).then_inc(y_ok, 1)

                    def step(b, t, more):
                        nxt = ahead(b, t, 1)
                        if more:
                            statistics(*nxt)
                        finish(b, t, 0)
                        finish(b, t, 1)
                        if more:
                            rest_of_h(*nxt)
                        finish(b, t, 2)
                        finish(b, t, 3)
                        if more:
                            adapter(*nxt)

                    statistics(0, 0)
                    rest_of_h(0, 0)
                    adapter(0, 0)
                    for t in range(TT):
                        step(0, t, True)
                    with dve.Fori(1, B - 1) as b:
                        for t in range(TT):
                            step(b, t, True)
                    for t in range(TT):
                        step(B - 1, t, t + 1 < TT)


def kernel(x, ctx_4096, L0_ffn_gate, L0_ffn_kernel, L0_ffn_bias, L0_ffn_lora_A, L0_ffn_lora_B,
           L0_ffn_lora_A_shared, L0_ffn_lora_B_shared):
    import concourse.bacc as bacc
    from concourse.bass_utils import run_bass_kernel_spmd

    fwd_tab, inv_tab = dft_tables()
    nyq_mask = np.ones((P, 1), np.float32)
    nyq_mask[0] = 0.0
    arrays = {
        "x": np.ascontiguousarray(x),
        "ctx": np.ascontiguousarray(ctx_4096),
        "gateT": np.ascontiguousarray(np.asarray(L0_ffn_gate).T),
        "w": np.ascontiguousarray(L0_ffn_kernel),
        "bias": np.ascontiguousarray(L0_ffn_bias),
        "lora_a": np.ascontiguousarray(np.asarray(L0_ffn_lora_A).reshape(NL * RANK, D)),
        "lora_bT": np.ascontiguousarray(np.asarray(L0_ffn_lora_B).transpose(0, 2, 1).reshape(NL * RANK, D)),
        "lora_as": np.ascontiguousarray(L0_ffn_lora_A_shared),
        "lora_bsT": np.ascontiguousarray(np.asarray(L0_ffn_lora_B_shared).T),
        "fwd_tab": fwd_tab,
        "inv_tab": inv_tab,
        "eye": np.eye(P, dtype=np.float32),
        "rank_sel": np.ascontiguousarray(np.tile(np.eye(RANK, dtype=np.float32), (P // RANK, 1))),
        "nyq_mask": nyq_mask,
    }
    nc = bacc.Bacc("TRN2", target_bir_lowering=False, num_devices=1)
    args = [nc.dram_tensor(name, a.shape, mybir.dt.from_np(a.dtype), kind="ExternalInput").ap() for name, a in arrays.items()]
    args.append(nc.dram_tensor("out", (B, L, D), FP32, kind="ExternalOutput").ap())
    build(nc, *args)
    r = run_bass_kernel_spmd(nc, [arrays], core_ids=[0])
    return r.results[0]["out"]
```

```python
from contextlib import ExitStack

import concourse.bass as bass
import numpy as np
from concourse import mybir

FP32 = mybir.dt.float32
FP16 = mybir.dt.float16
U32 = mybir.dt.uint32
ALU = mybir.AluOpType
ACT = mybir.ActivationFunctionType
AXX = mybir.AxisListType.X

P = 128
B, L, D = 8, 512, 2048
TT = L // P
GC = 512
GPB = D // GC
NG = B * GPB
CT = GC // P
HALF = L // 2
TOPK = int(2 * np.log(L))
NT = B * TT
KT = D // P
NL, RANK = 16, 32
NLT = NL * RANK // P
EPS = 1e-5
NEG = float(np.float32(-3.0e38))
WSCALE = 2.0 ** 14
TSCALE = 2.0 ** 10
HSCALE = 1024.0
ER, EI, OR, OI = range(4)
TURN = (2, 3, 0, 1)
assert TT == 4 and GPB == 4 and CT == 4 and 8 < TOPK <= 16


def dft_tables():
    n = np.arange(HALF)[:, None].astype(np.float64)
    f = np.arange(P)[None, :].astype(np.float64)
    even = 2 * np.pi * n * f / HALF
    odd = 2 * np.pi * n * (2 * f + 1) / L
    alt = (-1.0) ** np.arange(HALF)
    fwd = np.zeros((HALF, 4, P))
    fwd[:, ER], fwd[:, EI], fwd[:, OR], fwd[:, OI] = np.cos(even), -np.sin(even), np.cos(odd), -np.sin(odd)
    fwd_w = fwd * TSCALE
    fwd[:, EI, 0] = alt
    fwd_w[:, EI, 0] = -alt * TSCALE
    inv = np.zeros((P, 4, HALF))
    inv[:, ER], inv[:, EI] = 2 * np.cos(even).T / L, -2 * np.sin(even).T / L
    inv[:, OR], inv[:, OI] = 2 * np.cos(odd).T / L, -2 * np.sin(odd).T / L
    inv[0, ER] = 1.0 / L
    inv[0, EI] = alt / L

    def lay(a, dt):
        return np.ascontiguousarray(a.reshape(2, P, 4, P).transpose(1, 0, 2, 3), dtype=dt)

    high = fwd_w.astype(np.float16).astype(np.float64)
    pair = np.stack([lay(high, np.float16), lay(fwd_w - high, np.float16)], axis=1)
    return lay(fwd, np.float32), pair, np.ascontiguousarray(inv, dtype=np.float32)


def ahead(b, g, k):
    c = (g + k) // GPB
    return (b + c if c else b), (g + k) % GPB


def later(b, i):
    return not (isinstance(b, int) and b == 0 and i == 0)


def build(nc, x, ctx, gateT, w, bias, lora_a, lora_bT, lora_as, lora_bsT, fwd_tab, inv_tab, eye, rank_sel, nyq_mask, fwd_pair, out):
    x2 = nc.dram_tensor("x2_scratch", [B, L, D + 1024], FP32).ap()[:, :, 0:D]
    beff = nc.dram_tensor("beff_scratch", [B * RANK, D], FP32).ap()
    w_pair = nc.dram_tensor("w_pair_scratch", [2, KT, P, D + 1024], FP16).ap()[:, :, :, 0:D]
    a_pair = nc.dram_tensor("a_pair_scratch", [2, P, KT * (B + 1) * RANK], FP16).ap()
    x_g = x.rearrange("b (t p) c -> b p t c", p=P)
    ctx_g = ctx.rearrange("b (t p) c -> b p t c", p=P)
    x2_g = x2.rearrange("b (t p) c -> b p t c", p=P)
    w_t = w.rearrange("(k p) o -> k p o", p=P)
    w_b = w.rearrange("(b k p) o -> b k p o", p=P, b=B)
    w_pair_b = w_pair.rearrange("a (b k) p o -> a b k p o", b=B)

    with ExitStack() as outer:
        def sb(name, shape, dt=FP32, where=outer):
            return where.enter_context(nc.sbuf_tensor(name, shape, dt))

        def sem(name, where=outer):
            return where.enter_context(nc.semaphore(name))

        ident = sb("ident", [P, P])
        rsb = sb("rsb", [P, TT])
        nbb = sb("nbb", [P, TT])
        rsn = sb("rsn", [P, TT])
        nbn = sb("nbn", [P, TT])
        half = sb("half", [P, TT])
        w_scale = sb("w_scale", [P, 1])
        w_back = sb("w_back", [P, 1])
        ax_fix = sb("ax_fix", [P, 1])
        ps = outer.enter_context(nc.psum_tensor("ps", [P, 8, 512], FP32))

        with ExitStack() as st:
            xs = sb("xs", [P, TT, D], FP32, st)
            ws = sb("ws", [P, 4, D], FP32, st)
            bn = sb("bn", [P, 2 * TT, TT * 6], FP32, st)
            mv = sb("mv", [P, 2 * TT, 2], FP32, st)
            var_eps = sb("var_eps", [P, 2 * TT], FP32, st)
            negmean = sb("negmean", [P, 2 * TT], FP32, st)
            la = sb("la", [P, NLT, D], FP32, st)
            lb = sb("lb", [P, NLT, D], FP32, st)
            las = sb("las", [RANK, D], FP32, st)
            rsel = sb("rsel", [P, RANK], FP32, st)
            gcol = sb("gcol", [P, NLT, B], FP32, st)
            gsel = sb("gsel", [P, NLT, B, RANK], FP32, st)
            a_t = sb("a_t", [P, KT, B + 1, RANK], FP32, st)
            b_t = sb("b_t", [P, 2, D], FP32, st)
            a_hi = sb("a_hi1", [P, KT, B + 1, RANK], FP16, st)
            a_lo = sb("a_lo1", [P, KT, B + 1, RANK], FP16, st)
            wmax = sb("wmax", [P, KT], FP32, st)
            top = sb("top", [P, 2], FP32, st)
            topall = sb("topall", [P, 2], FP32, st)
            pow2 = sb("pow2", [P, 2], FP32, st)
            rpow = sb("rpow", [P, 2], FP32, st)
            scl = sb("scl", [P, 2], FP32, st)

            s_tab = sem("s_tab", st)
            s_lora = sem("s_lora", st)
            s_xs = [sem(f"s_xs{k}", st) for k in range(TT)]
            s_xs_used = sem("s_xs_used", st)
            s_ws = [sem(f"s_ws{k}", st) for k in range(4)]
            s_ws_used = sem("s_ws_used", st)
            s_gcol = sem("s_gcol", st)
            s_chain = sem("s_chain", st)
            s_var = sem("s_var", st)
            s_rs = sem("s_rs", st)
            s_gsel = sem("s_gsel", st)
            s_at = sem("s_at", st)
            s_at_out = sem("s_at_out", st)
            s_bt = sem("s_bt", st)
            s_bt_out = sem("s_bt_out", st)
            s_top = sem("s_top", st)
            s_topall = sem("s_topall", st)
            s_scale = sem("s_scale", st)
            s_ahi = sem("s_ahi", st)
            s_alo = sem("s_alo", st)
            s_store = sem("s_store", st)

            with nc.Block() as block:
                @block.sync
                def _(sp):
                    sp.dma_start(ident[:, :], eye).then_inc(s_tab, 16)
                    sp.dma_start(rsel[:, :], rank_sel).then_inc(s_tab, 16)
                    for b in range(2):
                        for k in range(TT):
                            if b:
                                sp.wait_ge(s_xs_used, k + 1)
                            sp.dma_start(xs[:, k, :], x_g[b, :, k, :]).then_inc(s_xs[k], 16)
                    for k in range(KT):
                        if k >= 4:
                            sp.wait_ge(s_ws_used, k - 3)
                        sp.dma_start(ws[:, k % 4, :], w_t[k]).then_inc(s_ws[k % 4], 16)
                    sp.wait_ge(s_bt_out, 8)
                    sp.dma_start(beff.rearrange("(m p) o -> p m o", p=P), b_t[:, :, :]).then_inc(s_store, 16)
                    sp.wait_ge(s_ahi, 1)
                    sp.dma_start(a_pair[0], a_hi[:, :, :, :].rearrange("p k b r -> p (k b r)")).then_inc(s_store, 16)
                    sp.wait_ge(s_alo, 1)
                    sp.dma_start(a_pair[1], a_lo[:, :, :, :].rearrange("p k b r -> p (k b r)")).then_inc(s_store, 16)
                    sp.wait_ge(s_store, 48)

                @block.gpsimd
                def _(pool):
                    for n in range(P // RANK):
                        src = gateT.rearrange("(k n) b -> n k b", n=P // RANK)[n].partition_broadcast(RANK)
                        pool.dma_start(gcol[n * RANK:(n + 1) * RANK, :, :], src).then_inc(s_gcol, 16)
                    nc.gpsimd.memset(half[:, :], -0.5).then_inc(s_chain, 1)
                    pool.wait_ge(s_chain, 1)
                    pool.wait_ge(s_var, 1)
                    for b, (rs, nb) in enumerate(((rsb, nbb), (rsn, nbn))):
                        cols = slice(b * TT, (b + 1) * TT)
                        nc.gpsimd.tensor_tensor(rs[:, :], var_eps[:, cols], half[:, :], ALU.pow).then_inc(s_rs, 1)
                        pool.wait_ge(s_rs, b + 1)
                        nc.gpsimd.tensor_tensor(nb[:, :], negmean[:, cols], rs[:, :], ALU.mult)
                    pool.wait_ge(s_top, 2)
                    nc.gpsimd.partition_all_reduce(topall[:, :], top[:, :], P, bass.bass_isa.ReduceOp.max).then_inc(s_topall, 1)

                @block.scalar
                def _(act):
                    act.dma_start(la[:, :, :], lora_a.rearrange("(k p) i -> p k i", p=P)).then_inc(s_lora, 16)
                    act.dma_start(lb[:, :, :], lora_bT.rearrange("(k p) o -> p k o", p=P)).then_inc(s_lora, 16)
                    act.dma_start(las[:, :], lora_as).then_inc(s_lora, 16)
                    for i in range(KT):
                        act.wait_ge(s_at, i + 1)
                        nc.scalar.activation(a_t[:, i, :, :], ps[:, i % 4, 0:(B + 1) * RANK].rearrange("p (b r) -> p b r", r=RANK),
                                             ACT.Copy).then_inc(s_at_out, 1)
                    for i in range(8):
                        act.wait_ge(s_bt, i + 1)
                        nc.scalar.activation(b_t[:, i // 4, (i % 4) * 512:(i % 4 + 1) * 512], ps[:, 4 + i % 4, :],
                                             ACT.Copy).then_inc(s_bt_out, 1)
                    act.wait_ge(s_scale, 1)
                    nc.scalar.activation(a_hi[:, :, :, :], a_t[:, :, :, :], ACT.Copy, scale=scl[:, 1:2]).then_inc(s_ahi, 1)

                @block.tensor
                def _(pe):
                    pe.wait_ge(s_lora, 48)
                    pe.wait_ge(s_tab, 32)
                    pe.wait_ge(s_gsel, 1)
                    for i in range(KT):
                        if i >= 4:
                            pe.wait_ge(s_at_out, i - 3)
                        for k in range(NLT):
                            nc.tensor.matmul(ps[:, i % 4, 0:B * RANK], la[:, k, i * P:(i + 1) * P],
                                             gsel[:, k, :, :].rearrange("p b r -> p (b r)"), start=(k == 0), stop=(k == NLT - 1))
                        nc.tensor.matmul(ps[:, i % 4, B * RANK:(B + 1) * RANK], las[:, i * P:(i + 1) * P],
                                         ident[0:RANK, 0:RANK], start=True, stop=True).then_inc(s_at, 1)
                    for i in range(8):
                        if i >= 4:
                            pe.wait_ge(s_bt_out, i - 3)
                        for k in range(NLT):
                            last = nc.tensor.matmul(ps[:, 4 + i % 4, :],
                                                    gsel[:, k, 4 * (i // 4):4 * (i // 4) + 4, :].rearrange("p b r -> p (b r)"),
                                                    lb[:, k, (i % 4) * 512:(i % 4 + 1) * 512],
                                                    start=(k == 0), stop=(k == NLT - 1))
                        last.then_inc(s_bt, 1)

                @block.vector
                def _(dve):
                    chain = [0]

                    def link(ins):
                        chain[0] += 1
                        ins.then_inc(s_mine, 1)
                        dve.wait_ge(s_mine, chain[0])

                    s_mine = sem("s_mine", st)
                    s_mv = sem("s_mv", st)
                    dve.wait_ge(s_tab, 32)
                    dve.wait_ge(s_gcol, 16 * (P // RANK))
                    nc.vector.tensor_tensor(gsel[:, :, :, :].rearrange("p k b r -> p (k b) r"),
                                            gcol[:, :, :].rearrange("p k b -> p (k b)").unsqueeze(2).broadcast_to([P, NLT * B, RANK]),
                                            rsel[:, :].unsqueeze(1).broadcast_to([P, NLT * B, RANK]), ALU.mult).then_inc(s_gsel, 1)
                    for t in range(2 * TT):
                        dve.wait_ge(s_xs[t % TT], 16 * (t // TT + 1))
                        for c in range(TT):
                            last = nc.vector.bn_stats(bn[:, t, 6 * c:6 * c + 6], xs[:, t % TT, c * 512:(c + 1) * 512])
                        last.then_inc(s_xs_used, 1)
                    dve.wait_ge(s_xs_used, 2 * TT)
                    for t in range(2 * TT):
                        last = nc.vector.bn_aggr(mv[:, t, :], bn[:, t, :])
                    last.then_inc(s_mv, 1)
                    dve.wait_ge(s_mv, 1)
                    nc.vector.tensor_scalar(negmean[:, :], mv[:, :, 0], -1.0, None, ALU.mult)
                    nc.vector.tensor_scalar(var_eps[:, :], mv[:, :, 1], EPS, None, ALU.add).then_inc(s_var, 1)
                    for k in range(KT):
                        dve.wait_ge(s_ws[k % 4], 16 * (k // 4 + 1))
                        nc.vector.tensor_reduce(wmax[:, k:k + 1], ws[:, k % 4, :], AXX, ALU.max,
                                                apply_absolute_value=True).then_inc(s_ws_used, 1)
                    dve.wait_ge(s_ws_used, KT)
                    nc.vector.tensor_reduce(top[:, 0:1], wmax[:, :], AXX, ALU.max).then_inc(s_top, 1)
                    dve.wait_ge(s_at_out, KT)
                    nc.vector.tensor_reduce(top[:, 1:2], a_t[:, :, :, :].rearrange("p k b r -> p (k b r)"), AXX, ALU.max,
                                            apply_absolute_value=True).then_inc(s_top, 1)
                    dve.wait_ge(s_topall, 1)
                    link(nc.vector.tensor_scalar(pow2[:, :], topall[:, :], 1e-30, None, ALU.max))
                    link(nc.vector.tensor_scalar(pow2[:, :].bitcast(U32), pow2[:, :].bitcast(U32), 0x7F800000, None, ALU.bitwise_and))
                    link(nc.vector.reciprocal(rpow[:, :], pow2[:, :]))
                    link(nc.vector.tensor_scalar(scl[:, :], rpow[:, :], 16384.0, None, ALU.mult))
                    nc.vector.tensor_copy(w_scale[:, :], scl[:, 0:1]).then_inc(s_scale, 1)
                    link(nc.vector.tensor_scalar(w_back[:, :], pow2[:, 0:1], 1.0 / (16384.0 * HSCALE), None, ALU.mult))
                    link(nc.vector.tensor_scalar(ax_fix[:, :], scl[:, 0:1], pow2[:, 1:2], 1.0 / 16384.0, ALU.mult, ALU.mult))
                    dve.wait_ge(s_ahi, 1)
                    nc.vector.scalar_tensor_tensor(out=a_lo[:, :, :, :].rearrange("p k b r -> p (k b r)"),
                                                   in0=a_t[:, :, :, :].rearrange("p k b r -> p (k b r)"), scalar=scl[:, 1:2],
                                                   in1=a_hi[:, :, :, :].rearrange("p k b r -> p (k b r)"),
                                                   op0=ALU.mult, op1=ALU.subtract).then_inc(s_alo, 1)

        with ExitStack() as st:
            ft = sb("ft", [P, 2, 4, P], FP32, st)
            fp = sb("fp", [P, 2, 2, 4, P], FP16, st)
            it = sb("it", [P, 4, HALF], FP32, st)
            nyq = sb("nyq", [P, 1], FP32, st)
            xg = sb("xg", [P, 2, TT, GC], FP32, st)
            qa = sb("qa", [P, 2, GC], FP32, st)
            cg = sb("cg", [P, 2, TT, GC], FP32, st)
            va = sb("va", [P, 2, GC], FP32, st)
            zs = sb("zs", [P, 2, 2, GC], FP32, st)
            vrow = sb("vrow", [P, GC], FP32, st)
            xv = sb("xv", [P, TT, GC], FP32, st)
            vlast = sb("vlast", [1, GC], FP32, st)
            spe = sb("spe", [P, 2, 2, 3, GC], FP32, st)
            spo = sb("spo", [P, 2, 2, 2, GC], FP32, st)
            mr = sb("mr", [P, 4, GC], FP32, st)
            mi = sb("mi", [P, 4, GC], FP32, st)
            mhr = sb("mhr", [P, 2, GC], FP32, st)
            mhi = sb("mhi", [P, 2, GC], FP32, st)
            cp = sb("cp", [P, 4, GC], FP32, st)
            op = sb("op", [P, 2, 4, GC], FP32, st)
            eo = sb("eo", [P, CT, L], FP32, st)
            cr = sb("cr", [P, CT, L], FP32, st)
            wd = sb("wd", [P, CT, L], FP32, st)
            wt = sb("wt", [P, 2, 4, GC], FP16, st)
            m16 = sb("m16", [P, CT, 16], FP32, st)
            nmax = sb("nmax", [P, CT], FP32, st)
            zsum = sb("zsum", [P, CT], FP32, st)
            rz = sb("rz", [P, CT], FP32, st)
            xrow = sb("xrow", [P, D], FP32, st)
            bn1 = sb("bn1", [P, TT * 6], FP32, st)
            mv1 = sb("mv1", [P, TT, 2], FP32, st)
            ve1 = sb("ve1", [P, TT], FP32, st)
            nm1 = sb("nm1", [P, TT], FP32, st)
            wc = sb("wc", [P, D // 2], FP32, st)
            wch = sb("wch", [P, D // 2], FP16, st)
            wcl = wc[:, :].bitcast(FP16)[:, 0:D // 2]

            s_tabs = sem("s_tabs", st)
            s_x = [sem(f"s_x{k}", st) for k in range(2)]
            s_c = [sem(f"s_c{k}", st) for k in range(2)]
            s_v = sem("s_v", st)
            s_xr = sem("s_xr", st)
            s_st = sem("s_st", st)
            s_xrow = sem("s_xrow", st)
            s_wc = sem("s_wc", st)
            s_wst = sem("s_wst", st)
            q_norm = sem("q_norm", st)
            cols_ok = sem("cols_ok", st)
            v_fold = sem("v_fold", st)
            q_fold = sem("q_fold", st)
            v_spec = sem("v_spec", st)
            q_spec = sem("q_spec", st)
            z_spec = sem("z_spec", st)
            v_out = sem("v_out", st)
            z_out = sem("z_out", st)
            cprod = sem("cprod", st)
            cp_sum = sem("cp_sum", st)
            corr_spec = sem("corr_spec", st)
            corr_out = sem("corr_out", st)
            own = sem("own", st)
            nmax_ok = sem("nmax_ok", st)
            exp_ok = sem("exp_ok", st)
            w_ready = sem("w_ready", st)
            wt_spec = sem("wt_spec", st)
            wt_hi = sem("wt_hi", st)
            wt_lo = sem("wt_lo", st)
            w_spec = sem("w_spec", st)
            oprod = sem("oprod", st)
            pair_sum = sem("pair_sum", st)
            op_sum = sem("op_sum", st)
            hi_sum = sem("hi_sum", st)
            rz_ok = sem("rz_ok", st)
            out_spec = sem("out_spec", st)
            out_add = sem("out_add", st)
            row_used = sem("row_used", st)
            ve_ok = sem("ve_ok", st)
            rsn_ok = sem("rsn_ok", st)
            wch_ok = sem("wch_ok", st)
            wcl_ok = sem("wcl_ok", st)

            with nc.Block() as block:
                @block.sync
                def _(sp):
                    def load(b, g):
                        cols = slice(g * GC, (g + 1) * GC)
                        sp.dma_start(cg[:, g % 2, :, :], ctx_g[b, :, :, cols]).then_inc(s_c[g % 2], 16)
                        sp.dma_start(xg[:, g % 2, :, :], x_g[b, :, :, cols]).then_inc(s_x[g % 2], 16)
                        if later(b, g):
                            sp.wait_ge(v_fold, 4 * (GPB * b + g))
                        sp.dma_start(vrow[:, :], ctx[b, L - 1, cols].partition_broadcast(P)).then_inc(s_v, 16)

                    def load_residual(b, g):
                        sp.dma_start(xv[:, :, :], x_g[b, :, :, g * GC:(g + 1) * GC]).then_inc(s_xr, 16)
                        sp.dma_start(vlast[:, :], ctx[b, L - 1, g * GC:(g + 1) * GC].unsqueeze(0)).then_inc(s_xr, 16)

                    def load_weights(b, g):
                        sp.dma_start(wc[:, :], w_b[b, g // 2, :, (g % 2) * (D // 2):(g % 2 + 1) * (D // 2)]).then_inc(s_wc, 16)

                    def step(b, g, more, lead, rows):
                        n = GPB * b + g
                        if more:
                            sp.wait_ge(z_spec, 4 * n + 8)
                            load(*ahead(b, g, 3))
                        sp.wait_ge(wch_ok, n + 1)
                        sp.wait_ge(wcl_ok, n + 1)
                        half_cols = slice((g % 2) * (D // 2), (g % 2 + 1) * (D // 2))
                        sp.dma_start(w_pair_b[0, b, g // 2, :, half_cols], wch[:, :]).then_inc(s_wst, 16)
                        sp.dma_start(w_pair_b[1, b, g // 2, :, half_cols], wcl).then_inc(s_wst, 16)
                        if lead:
                            sp.wait_ge(s_wst, 32 * n + 32)
                            load_weights(*ahead(b, g, 1))
                        if rows:
                            sp.wait_ge(row_used, n + 1)
                            nb, nt = ahead(b, g, 1)
                            sp.dma_start(xrow[:, :], x_g[nb + 2, :, nt, :]).then_inc(s_xrow, 16)
                        sp.wait_ge(out_add, 4 * n + 4)
                        sp.dma_start(x2_g[b, :, :, g * GC:(g + 1) * GC], xv[:, :, :]).then_inc(s_st, 16)
                        if lead:
                            sp.wait_ge(s_st, 16 * n + 16)
                            load_residual(*ahead(b, g, 1))

                    load(0, 0)
                    sp.dma_start(ft[:, :, :, :], fwd_tab).then_inc(s_tabs, 16)
                    sp.dma_start(it[:, :, :], inv_tab).then_inc(s_tabs, 16)
                    sp.dma_start(nyq[:, :], nyq_mask).then_inc(s_tabs, 16)
                    sp.dma_start(fp[:, :, :, :, :], fwd_pair).then_inc(s_tabs, 16)
                    load(0, 1)
                    load_residual(0, 0)
                    load_weights(0, 0)
                    sp.dma_start(xrow[:, :], x_g[2, :, 0, :]).then_inc(s_xrow, 16)
                    sp.wait_ge(z_spec, 4)
                    load(0, 2)
                    for g in range(GPB):
                        step(0, g, True, True, True)
                    with sp.Fori(1, B - 3) as b:
                        for g in range(GPB):
                            step(b, g, True, True, True)
                    for g in range(GPB):
                        step(B - 3, g, True, True, g < GPB - 1)
                    for g in range(GPB):
                        step(B - 2, g, True, True, False)
                    for g in range(GPB):
                        step(B - 1, g, g + 3 < GPB, g + 1 < GPB, False)
                    sp.wait_ge(s_st, 16 * NG)
                    sp.wait_ge(s_wst, 32 * NG)

                @block.gpsimd
                def _(pool):
                    def prepare(b, g):
                        m, k = GPB * b + g, g % 2
                        seen = 16 * (2 * b + g // 2 + 1)
                        pool.wait_ge(s_c[k], seen)
                        pool.wait_ge(s_v, 16 * m + 16)
                        row = vrow[:, :].unsqueeze(1).broadcast_to([P, 2, GC])
                        if later(b, g):
                            pool.wait_ge(v_spec, 4 * m)
                        nc.gpsimd.tensor_tensor(va[:, :, :], cg[:, k, 0:2, :], cg[:, k, 2:4, :], ALU.add).then_inc(v_fold, 1)
                        nc.gpsimd.tensor_tensor(cg[:, k, 0:2, :], cg[:, k, 0:2, :], cg[:, k, 2:4, :], ALU.subtract).then_inc(v_fold, 1)
                        nc.gpsimd.tensor_tensor(zs[:, k, :, :], cg[:, k, 2:4, :], row, ALU.add).then_inc(v_fold, 1)
                        nc.gpsimd.tensor_tensor(cg[:, k, 2:4, :], cg[:, k, 2:4, :], row, ALU.subtract).then_inc(v_fold, 1)
                        if later(b, g):
                            pool.wait_ge(q_spec, 4 * m)
                        pool.wait_ge(q_norm, 4 * m + 4)
                        nc.gpsimd.tensor_tensor(qa[:, :, :], xg[:, k, 0:2, :], xg[:, k, 2:4, :], ALU.add).then_inc(q_fold, 1)
                        nc.gpsimd.tensor_tensor(xg[:, k, 0:2, :], xg[:, k, 0:2, :], xg[:, k, 2:4, :], ALU.subtract).then_inc(q_fold, 1)

                    def corr_sums(b, g):
                        m = GPB * b + g
                        if later(b, g):
                            pool.wait_ge(corr_spec, 4 * m)
                        pool.wait_ge(cprod, 4 * m + 4)
                        nc.gpsimd.tensor_tensor(cp[:, 0::2, :], mr[:, 0::2, :], mr[:, 1::2, :], ALU.add).then_inc(cp_sum, 1)
                        nc.gpsimd.tensor_tensor(cp[:, 1::2, :], mi[:, 1::2, :], mi[:, 0::2, :], ALU.subtract).then_inc(cp_sum, 1)

                    def out_sums(b, g):
                        n = GPB * b + g
                        if later(b, g):
                            pool.wait_ge(out_spec, 4 * n)
                        for h in range(2):
                            r, i = 2 * h, 2 * h + 1
                            pool.wait_ge(oprod, 9 * n + 5 * h + 1)
                            nc.gpsimd.tensor_tensor(mr[:, 0:2, :], mr[:, 0:2, :], mr[:, 2:4, :], ALU.add).then_inc(pair_sum, 1)
                            pool.wait_ge(oprod, 9 * n + 5 * h + 2)
                            nc.gpsimd.tensor_tensor(mi[:, 0:2, :], mi[:, 0:2, :], mi[:, 2:4, :], ALU.add).then_inc(pair_sum, 1)
                            pool.wait_ge(pair_sum, 4 * n + 2 * h + 1)
                            nc.gpsimd.tensor_tensor(op[:, 0, r, :], mr[:, 0, :], mr[:, 1, :], ALU.add).then_inc(op_sum, 1)
                            pool.wait_ge(pair_sum, 4 * n + 2 * h + 2)
                            nc.gpsimd.tensor_tensor(op[:, 0, i, :], mi[:, 0, :], mi[:, 1, :], ALU.subtract).then_inc(op_sum, 1)
                            if h == 0:
                                pool.wait_ge(oprod, 9 * n + 5)
                                nc.gpsimd.tensor_tensor(op[:, 1, r, :], mhr[:, 0, :], mhr[:, 1, :], ALU.add).then_inc(op_sum, 1)
                                nc.gpsimd.tensor_tensor(op[:, 1, i, :], mhi[:, 0, :], mhi[:, 1, :], ALU.subtract).then_inc(op_sum, 1)

                    def next_rows(b):
                        pool.wait_ge(ve_ok, b + 1)
                        pool.wait_ge(cols_ok, 2 * b + 2)
                        nc.gpsimd.tensor_tensor(rsn[:, :], ve1[:, :], half[:, :], ALU.pow).then_inc(rsn_ok, 1)
                        pool.wait_ge(rsn_ok, 2 * b + 1)
                        nc.gpsimd.tensor_tensor(nbn[:, :], nm1[:, :], rsn[:, :], ALU.mult).then_inc(rsn_ok, 1)

                    def step(b, g, more, lead, rows):
                        if more:
                            prepare(*ahead(b, g, 2))
                        if lead:
                            corr_sums(*ahead(b, g, 1))
                        out_sums(b, g)
                        if rows and g == GPB - 1:
                            next_rows(b)

                    prepare(0, 0)
                    prepare(0, 1)
                    corr_sums(0, 0)
                    for g in range(GPB):
                        step(0, g, True, True, True)
                    with pool.Fori(1, B - 2) as b:
                        for g in range(GPB):
                            step(b, g, True, True, True)
                    for g in range(GPB):
                        step(B - 2, g, True, True, False)
                    for g in range(GPB):
                        step(B - 1, g, g + 2 < GPB, g + 1 < GPB, False)

                @block.scalar
                def _(act):
                    def normalise(b, g):
                        k = g % 2
                        if g == 0 and later(b, g):
                            if not isinstance(b, int) or b > 1:
                                act.wait_ge(rsn_ok, 2 * b - 2)
                            nc.scalar.activation(rsb[:, :], rsn[:, :], ACT.Copy).then_inc(cols_ok, 1)
                            nc.scalar.activation(nbb[:, :], nbn[:, :], ACT.Copy).then_inc(cols_ok, 1)
                            act.wait_ge(cols_ok, 2 * b)
                        act.wait_ge(s_x[k], 16 * (2 * b + g // 2 + 1))
                        for t in range(TT):
                            nc.scalar.activation(xg[:, k, t, :], xg[:, k, t, :], ACT.Identity,
                                                 bias=nbb[:, t:t + 1], scale=rsb[:, t:t + 1]).then_inc(q_norm, 1)

                    def store_spectrum(b, g, which):
                        m, k, even, odd = GPB * b + g, g % 2, 4 * which + TURN[0], 4 * which + TURN[2]
                        spec, kept = ((v_spec, v_out), (z_spec, z_out))[which]
                        act.wait_ge(spec, 4 * m + 1)
                        nc.scalar.activation(spe[:, k, which, 0::2, :], ps[:, even, :].unsqueeze(1).broadcast_to([P, 2, GC]),
                                             ACT.Copy).then_inc(kept, 1)
                        act.wait_ge(spec, 4 * m + 2)
                        nc.scalar.activation(spe[:, k, which, 1, :], ps[:, even + 1, :], ACT.Copy, scale=nyq[:, 0:1]).then_inc(kept, 1)
                        act.wait_ge(kept, 4 * m + 1)
                        nc.scalar.activation(spe[0:1, k, which, 2, :], ps[0:1, even + 1, :], ACT.Copy).then_inc(kept, 1)
                        act.wait_ge(spec, 4 * m + 4)
                        nc.scalar.activation(spo[:, k, which, :, :], ps[:, odd:odd + 2, :], ACT.Copy).then_inc(kept, 1)

                    def corr_to_sbuf(b, g):
                        m = GPB * b + g
                        if later(b, g):
                            act.wait_ge(w_ready, 4 * m)
                        for j in range(CT):
                            act.wait_ge(corr_spec, 4 * m + j + 1)
                            nc.scalar.activation(eo[:, j, :], ps[:, TURN[j], :], ACT.Copy).then_inc(corr_out, 1)

                    def exponentials(b, g):
                        m = GPB * b + g
                        if later(b, g):
                            act.wait_ge(wt_spec, 4 * m)
                        act.wait_ge(nmax_ok, m + 1)
                        for j in range(CT):
                            nc.scalar.activation(wd[:, j, :], cr[:, j, :], ACT.Exp, bias=nmax[:, j:j + 1]).then_inc(exp_ok, 1)

                    def divide_w(b, g):
                        m = GPB * b + g
                        act.wait_ge(rz_ok, m + 1)
                        for j in range(CT):
                            nc.scalar.activation(wd[:, j, :], wd[:, j, :], ACT.Copy, scale=rz[:, j:j + 1]).then_inc(w_ready, 1)

                    def transposed_out(b, g):
                        n = GPB * b + g
                        if later(b, g):
                            act.wait_ge(w_spec, 8 * n)
                        for k in range(4):
                            act.wait_ge(wt_spec, 4 * n + k + 1)
                            nc.scalar.activation(wt[:, 0, k, :], ps[:, 4 + TURN[k], :], ACT.Copy, scale=WSCALE).then_inc(wt_hi, 1)

                    def weights_high(b, g):
                        n = GPB * b + g
                        if later(b, g):
                            act.wait_ge(s_wst, 32 * n)
                        act.wait_ge(s_wc, 16 * n + 16)
                        nc.scalar.activation(wch[:, :], wc[:, :], ACT.Copy, scale=w_scale[:, 0:1]).then_inc(wch_ok, 1)

                    def step(b, g, more, lead, far):
                        n = GPB * b + g
                        transposed_out(b, g)
                        if lead:
                            store_spectrum(*ahead(b, g, 1), 1)
                        weights_high(b, g)
                        if lead:
                            corr_to_sbuf(*ahead(b, g, 1))
                        if more:
                            act.wait_ge(oprod, 9 * n + 9)
                            store_spectrum(*ahead(b, g, 2), 0)
                        if lead:
                            exponentials(*ahead(b, g, 1))
                        if far:
                            normalise(*ahead(b, g, 3))
                        if lead:
                            divide_w(*ahead(b, g, 1))

                    normalise(0, 0)
                    normalise(0, 1)
                    act.wait_ge(s_tabs, 64)
                    store_spectrum(0, 0, 0)
                    store_spectrum(0, 0, 1)
                    corr_to_sbuf(0, 0)
                    store_spectrum(0, 1, 0)
                    exponentials(0, 0)
                    normalise(0, 2)
                    divide_w(0, 0)
                    for g in range(GPB):
                        step(0, g, True, True, True)
                    with act.Fori(1, B - 1) as b:
                        for g in range(GPB):
                            step(b, g, True, True, True)
                    for g in range(GPB):
                        step(B - 1, g, g + 2 < GPB, g + 1 < GPB, g + 3 < GPB)

                @block.tensor
                def _(pe):
                    def forward(bank, kind, src):
                        for k in range(2):
                            last = nc.tensor.matmul(ps[:, bank, :], ft[:, k, kind, :], src[k], start=(k == 0), stop=(k == 1))
                        return last

                    def forward_w(bank, kind, part):
                        for k in range(2):
                            for i, (tab, val) in enumerate(((0, 0), (1, 0), (0, 1))):
                                last = nc.tensor.matmul(ps[:, bank, :], fp[:, tab, k, kind, :], wt[:, val, 2 * part + k, :],
                                                        start=(k == 0 and i == 0), stop=(k == 1 and i == 2))
                        return last

                    def v_spectrum(b, g):
                        m, k = GPB * b + g, g % 2
                        pe.wait_ge(v_fold, 4 * m + 2)
                        for i in range(4):
                            if later(b, g):
                                pe.wait_ge(corr_out, 4 * m - 3 + i)
                            src = (va[:, 0, :], va[:, 1, :]) if i < 2 else (cg[:, k, 0, :], cg[:, k, 1, :])
                            forward(TURN[i], i, src).then_inc(v_spec, 1)

                    def q_spectrum(b, g):
                        m, k = GPB * b + g, g % 2
                        pe.wait_ge(q_fold, 2 * m + 2)
                        pe.wait_ge(v_out, 4 * m + 4)
                        for i in range(4):
                            src = (qa[:, 0, :], qa[:, 1, :]) if i < 2 else (xg[:, k, 0, :], xg[:, k, 1, :])
                            forward(i, i, src).then_inc(q_spec, 1)

                    def z_spectrum(b, g):
                        m, k = GPB * b + g, g % 2
                        pe.wait_ge(v_fold, 4 * m + 4)
                        for i in range(4):
                            if later(b, g):
                                pe.wait_ge(wt_lo, 4 * m - 3 + i)
                            src = (zs[:, k, 0, :], zs[:, k, 1, :]) if i < 2 else (cg[:, k, 2, :], cg[:, k, 3, :])
                            forward(4 + TURN[i], i, src).then_inc(z_spec, 1)

                    def transpose_w(b, g):
                        n = GPB * b + g
                        pe.wait_ge(w_ready, 4 * n + 4)
                        for k in range(4):
                            if later(b, g):
                                pe.wait_ge(out_add, 4 * n - 3 + k)
                            for j in range(CT):
                                last = nc.tensor.transpose(ps[:, 4 + TURN[k], j * P:(j + 1) * P], wd[:, j, k * P:(k + 1) * P], ident[:, :])
                            last.then_inc(wt_spec, 1)

                    def weight_spectra(b, g, lead):
                        n = GPB * b + g
                        if lead:
                            pe.wait_ge(cprod, 4 * n + 8)
                        pe.wait_ge(wt_lo, 4 * n + 4)
                        for i in range(4):
                            forward_w(i, (ER, EI)[i % 2], i // 2).then_inc(w_spec, 1)
                        if lead:
                            pe.wait_ge(z_out, 4 * n + 8)
                        for i in range(4):
                            forward_w(4 + i, (OR, OI)[i % 2], i // 2).then_inc(w_spec, 1)

                    def correlation(b, g):
                        m = GPB * b + g
                        pe.wait_ge(cp_sum, 2 * m + 2)
                        for j in range(CT):
                            if later(b, g):
                                pe.wait_ge(oprod, 9 * m - (6 if j < 2 else 4))
                            for h in range(2):
                                for i in range(2):
                                    s = 2 * h + i
                                    last = nc.tensor.matmul(ps[:, TURN[j], h * HALF:(h + 1) * HALF], cp[:, s, j * P:(j + 1) * P],
                                                            it[:, s, :], start=(i == 0), stop=(i == 1))
                            last.then_inc(corr_spec, 1)

                    def output(b, g):
                        n = GPB * b + g
                        pe.wait_ge(oprod, 9 * n + 9)
                        pe.wait_ge(hi_sum, 3 * n + 3)
                        for t in TURN:
                            if t == 0:
                                pe.wait_ge(op_sum, 6 * n + 6)
                            for s in range(4):
                                last = nc.tensor.matmul(ps[:, 4 + t, :], it[:, s, (t % 2) * P:(t % 2 + 1) * P], op[:, t // 2, s, :],
                                                        start=(s == 0), stop=(s == 3))
                            last.then_inc(out_spec, 1)

                    def step(b, g, more, lead):
                        if lead:
                            q_spectrum(*ahead(b, g, 1))
                        transpose_w(b, g)
                        if lead:
                            z_spectrum(*ahead(b, g, 1))
                        weight_spectra(b, g, lead)
                        if lead:
                            correlation(*ahead(b, g, 1))
                        if more:
                            v_spectrum(*ahead(b, g, 2))
                        output(b, g)

                    pe.wait_ge(s_tabs, 64)
                    v_spectrum(0, 0)
                    q_spectrum(0, 0)
                    z_spectrum(0, 0)
                    correlation(0, 0)
                    v_spectrum(0, 1)
                    for g in range(GPB):
                        step(0, g, True, True)
                    with pe.Fori(1, B - 1) as b:
                        for g in range(GPB):
                            step(b, g, True, True)
                    for g in range(GPB):
                        step(B - 1, g, g + 2 < GPB, g + 1 < GPB)

                @block.vector
                def _(dve):
                    def corr_products_even(b, g):
                        m, k = GPB * b + g, g % 2
                        if later(b, g) and later(b, g - 1):
                            dve.wait_ge(op_sum, 6 * m - 6)
                        dve.wait_ge(v_out, 4 * m + 4)
                        dve.wait_ge(q_spec, 4 * m + 2)
                        nc.vector.tensor_tensor(mr[:, 0:2, :], ps[:, 0:2, :], spe[:, k, 0, 0:2, :], ALU.mult).then_inc(cprod, 1)
                        nc.vector.tensor_tensor(mi[:, 0:2, :], ps[:, 0:2, :], spe[:, k, 0, 1:3, :], ALU.mult).then_inc(cprod, 1)

                    def corr_products_odd(b, g):
                        m, k = GPB * b + g, g % 2
                        dve.wait_ge(q_spec, 4 * m + 4)
                        nc.vector.tensor_tensor(mr[:, 2:4, :], ps[:, 2:4, :], spo[:, k, 0, :, :], ALU.mult).then_inc(cprod, 1)
                        nc.vector.tensor_tensor(mi[:, 2:4, :], ps[:, 2:4, :], spo[:, k, 0, ::-1, :], ALU.mult).then_inc(cprod, 1)

                    def weights_rest(b, g):
                        n = GPB * b + g
                        dve.wait_ge(wch_ok, n + 1)
                        nc.vector.scalar_tensor_tensor(out=wcl, in0=wc[:, :], scalar=w_scale[:, 0:1], in1=wch[:, :],
                                                       op0=ALU.mult, op1=ALU.subtract).then_inc(wcl_ok, 1)

                    def row_statistics(b, g):
                        n = GPB * b + g
                        dve.sem_clear(own)
                        dve.wait_ge(s_xrow, 16 * n + 16)
                        for c in range(4):
                            nc.vector.bn_stats(bn1[:, 6 * c:6 * c + 6], xrow[:, c * 512:(c + 1) * 512]).then_inc(own, 1)
                        dve.wait_ge(own, 4)
                        nc.vector.bn_aggr(mv1[:, g, :], bn1[:, :]).then_inc(row_used, 1)
                        if g == GPB - 1:
                            dve.wait_ge(row_used, n + 1)
                            if later(b, 0):
                                dve.wait_ge(rsn_ok, 2 * b)
                            nc.vector.tensor_scalar(nm1[:, :], mv1[:, :, 0], -1.0, None, ALU.mult)
                            nc.vector.tensor_scalar(ve1[:, :], mv1[:, :, 1], EPS, None, ALU.add).then_inc(ve_ok, 1)

                    def w_rest(b, g):
                        n = GPB * b + g
                        if later(b, g):
                            dve.wait_ge(w_spec, 8 * n)
                        for k in range(4):
                            dve.wait_ge(wt_hi, 4 * n + k + 1)
                            nc.vector.scalar_tensor_tensor(out=wt[:, 1, k, :], in0=ps[:, 4 + TURN[k], :], scalar=WSCALE, in1=wt[:, 0, k, :],
                                                           op0=ALU.mult, op1=ALU.subtract).then_inc(wt_lo, 1)

                    def out_products(b, g, lead):
                        n, k = GPB * b + g, g % 2
                        dve.wait_ge(z_out, 4 * n + 4)
                        for h in range(2):
                            if h == 0:
                                dve.wait_ge(cp_sum, 2 * n + (4 if lead else 2))
                            else:
                                dve.wait_ge(op_sum, 6 * n + 1)
                            dve.wait_ge(w_spec, 8 * n + 4 * h + 4)
                            split = "p (a r) c -> p a r c"
                            wl, wlh = ps[:, 4 * h:4 * h + 2, :], ps[:, 4 * h:4 * h + 4, :].rearrange(split, a=2)
                            if h == 0:
                                v_r, v_i, z_r, z_i = spe[:, k, :, 0:2, :], spe[:, k, :, 1:3, :], spe[:, k, 1, 0:2, :], spe[:, k, 1, 1:3, :]
                            else:
                                v_r, v_i, z_r, z_i = spo[:, k, :, :, :], spo[:, k, :, ::-1, :], spo[:, k, 1, :, :], spo[:, k, 1, ::-1, :]
                            nc.vector.tensor_tensor(mr[:, :, :].rearrange(split, a=2), wlh, v_r, ALU.mult).then_inc(oprod, 1)
                            if h == 1:
                                dve.wait_ge(op_sum, 6 * n + 2)
                            nc.vector.tensor_tensor(mi[:, :, :].rearrange(split, a=2), wlh, v_i, ALU.mult).then_inc(oprod, 1)
                            if h == 0:
                                dve.wait_ge(s_xr, 32 * n + 32)
                                nc.vector.scalar_tensor_tensor(out=vlast[:, :], in0=ps[0:1, 2, :], scalar=float(L), in1=vlast[:, :],
                                                               op0=ALU.mult, op1=ALU.mult).then_inc(oprod, 1)
                            else:
                                dve.wait_ge(op_sum, 6 * n + 4)
                            nc.vector.tensor_tensor(mhr[:, :, :], wl, z_r, ALU.mult).then_inc(oprod, 1)
                            nc.vector.tensor_tensor(mhi[:, :, :], wl, z_i, ALU.mult).then_inc(oprod, 1)
                        nc.vector.tensor_tensor(op[0:1, 1, ER, :], op[0:1, 1, ER, :], vlast[:, :], ALU.add).then_inc(hi_sum, 1)
                        dve.wait_ge(oprod, 9 * n + 8)
                        nc.vector.tensor_tensor(op[:, 1, OR, :], mhr[:, 0, :], mhr[:, 1, :], ALU.add).then_inc(hi_sum, 1)
                        dve.wait_ge(oprod, 9 * n + 9)
                        nc.vector.tensor_tensor(op[:, 1, OI, :], mhi[:, 0, :], mhi[:, 1, :], ALU.subtract).then_inc(hi_sum, 1)

                    def top_lags(b, g):
                        m = GPB * b + g
                        dve.sem_clear(own)
                        if later(b, g):
                            dve.wait_ge(exp_ok, 4 * m)
                        for j in range(CT):
                            dve.wait_ge(corr_out, 4 * m + j + 1)
                            nc.vector.tensor_tensor(cr[:, j, 0:HALF], eo[:, j, 0:HALF], eo[:, j, HALF:L], ALU.add)
                            nc.vector.tensor_tensor(cr[:, j, HALF:L], eo[:, j, 0:HALF], eo[:, j, HALF:L], ALU.subtract).then_inc(own, 1)
                        for j in range(CT):
                            dve.wait_ge(own, j + 1)
                            nc.vector.max(m16[:, j, 0:8], cr[:, j, :]).then_inc(own, 1)
                        dve.wait_ge(own, 2 * CT)
                        nc.vector.tensor_scalar(nmax[:, :], m16[:, :, 0], -1.0, None, ALU.mult).then_inc(nmax_ok, 1)
                        for j in range(CT):
                            nc.vector.match_replace(eo[:, j, :], m16[:, j, 0:8], cr[:, j, :], NEG).then_inc(own, 1)
                        for j in range(CT):
                            dve.wait_ge(own, 2 * CT + j + 1)
                            nc.vector.max(m16[:, j, 8:16], eo[:, j, :]).then_inc(own, 1)
                        dve.wait_ge(own, 4 * CT)
                        nc.vector.memset(m16[:, :, TOPK:16], NEG).then_inc(own, 1)
                        dve.wait_ge(own, 4 * CT + 1)
                        for j in range(CT):
                            nc.vector.match_replace(eo[:, j, :], m16[:, j, 8:16], eo[:, j, :], NEG).then_inc(own, 1)
                        dve.wait_ge(exp_ok, 4 * m + 4)
                        for j in range(CT):
                            dve.wait_ge(own, 4 * CT + j + 2)
                            nc.vector.scalar_tensor_tensor(out=wd[:, j, :], in0=eo[:, j, :], scalar=NEG, in1=wd[:, j, :],
                                                           op0=ALU.is_le, op1=ALU.mult, accum_out=zsum[:, j:j + 1]).then_inc(own, 1)
                        dve.wait_ge(own, 6 * CT + 1)
                        if later(b, g):
                            dve.wait_ge(w_ready, 4 * m)
                        nc.vector.reciprocal(rz[:, :], zsum[:, :]).then_inc(rz_ok, 1)

                    def add_output(b, g):
                        n = GPB * b + g
                        for i, t in enumerate(TURN):
                            dve.wait_ge(out_spec, 4 * n + i + 1)
                            nc.vector.scalar_tensor_tensor(out=xv[:, t, :], in0=ps[:, 4 + t, :], scalar=1.0 / (WSCALE * TSCALE),
                                                           in1=xv[:, t, :], op0=ALU.mult, op1=ALU.add).then_inc(out_add, 1)

                    def step(b, g, lead, rows):
                        if lead:
                            corr_products_even(*ahead(b, g, 1))
                        w_rest(b, g)
                        if lead:
                            corr_products_odd(*ahead(b, g, 1))
                        if rows:
                            row_statistics(b, g)
                        weights_rest(b, g)
                        out_products(b, g, lead)
                        if lead:
                            top_lags(*ahead(b, g, 1))
                        add_output(b, g)

                    corr_products_even(0, 0)
                    corr_products_odd(0, 0)
                    top_lags(0, 0)
                    for g in range(GPB):
                        step(0, g, True, True)
                    with dve.Fori(1, B - 2) as b:
                        for g in range(GPB):
                            step(b, g, True, True)
                    for g in range(GPB):
                        step(B - 2, g, True, False)
                    for g in range(GPB):
                        step(B - 1, g, g + 1 < GPB, False)

        with ExitStack() as st:
            w_hi = sb("w_hi", [P, KT, D], FP16, st)
            w_lo = sb("w_lo", [P, KT, D], FP16, st)
            a_hi = sb("a_hi", [P, KT, B + 1, RANK], FP16, st)
            a_lo = sb("a_lo", [P, KT, B + 1, RANK], FP16, st)
            xt = sb("xt", [P, 2, D], FP32, st)
            h = sb("h", [P, D], FP32, st)
            h_hi = sb("h_hi", [P, 2, KT, P], FP16, st)
            h_lo = sb("h_lo", [P, 2, KT, P], FP16, st)
            bcat = sb("bcat", [2 * RANK, D], FP32, st)
            brow = sb("brow", [P, D], FP32, st)
            bn2 = sb("bn2", [P, 4, 6], FP32, st)
            mv2 = sb("mv2", [P, 2], FP32, st)
            ve2 = sb("ve2", [P, 1], FP32, st)
            rp2 = sb("rp2", [P, 1], FP32, st)
            rs2 = sb("rs2", [P, 1], FP32, st)
            nb2 = sb("nb2", [P, 1], FP32, st)
            ax = sb("ax", [P, 2 * RANK], FP32, st)
            axT = sb("axT", [2 * RANK, P], FP32, st)

            s_row = sem("s_row", st)
            s_b = sem("s_b", st)
            s_w = [sem(f"s_w{k}", st) for k in range(4)]
            s_xt = [sem(f"s_xt{k}", st) for k in range(2)]
            s_out = [sem(f"s_out{k}", st) for k in range(2)]
            own2 = sem("own2", st)
            ve_ok = sem("ve_ok", st)
            rp_ok = sem("rp_ok", st)
            nb_ok = sem("nb_ok", st)
            h_ok = sem("h_ok", st)
            bias_ok = sem("bias_ok", st)
            ht_spec = sem("ht_spec", st)
            hi_ok = sem("hi_ok", st)
            lo_ok = sem("lo_ok", st)
            ax_spec = sem("ax_spec", st)
            ax_ok = sem("ax_ok", st)
            axt_spec = sem("axt_spec", st)
            axt_ok = sem("axt_ok", st)
            y_spec = sem("y_spec", st)
            y_ok = sem("y_ok", st)

            with nc.Block() as block:
                out_t = out.rearrange("b (t p) c -> b p t c", p=P)

                @block.sync
                def _(sp):
                    def load(b, t):
                        sp.dma_start(xt[:, t % 2, :], x2_g[b, :, t, :]).then_inc(s_xt[t % 2], 16)

                    def load_b(b):
                        sp.dma_start(bcat[0:RANK, :], beff[bass.ts(b, RANK), :]).then_inc(s_b, 16)

                    load(0, 0)
                    load(0, 1)
                    sp.dma_start(brow[:, :], bias.partition_broadcast(P)).then_inc(s_row, 16)
                    sp.dma_start(bcat[RANK:2 * RANK, :], lora_bsT).then_inc(s_row, 16)
                    sp.dma_start(a_hi[:, :, :, :].rearrange("p k b r -> p (k b r)"), a_pair[0]).then_inc(s_row, 16)
                    sp.dma_start(a_lo[:, :, :, :].rearrange("p k b r -> p (k b r)"), a_pair[1]).then_inc(s_row, 16)
                    load_b(0)
                    for c in range(4):
                        cols = slice(c * 512, (c + 1) * 512)
                        sp.dma_start(w_hi[:, :, cols], w_pair[0, :, :, cols].rearrange("k p o -> p k o")).then_inc(s_w[c], 16)
                        sp.dma_start(w_lo[:, :, cols], w_pair[1, :, :, cols].rearrange("k p o -> p k o")).then_inc(s_w[c], 16)

                    def step(b, t, more):
                        n = TT * b + t
                        sp.wait_ge(y_ok, 4 * n + 4)
                        sp.dma_start(out_t[b, :, t, :], xt[:, t % 2, :]).then_inc(s_out[t % 2], 16)
                        if more:
                            if t == TT - 1:
                                load_b(b + 1)
                            sp.wait_ge(s_out[t % 2], 16 * (2 * b + t // 2 + 1))
                            load(*ahead(b, t, 2))

                    for t in range(TT):
                        step(0, t, True)
                    with sp.Fori(1, B - 1) as b:
                        for t in range(TT):
                            step(b, t, True)
                    for t in range(TT):
                        step(B - 1, t, t + 2 < TT)
                    for k in range(2):
                        sp.wait_ge(s_out[k], 16 * NT // 2)

                @block.gpsimd
                def _(pool):
                    def prepare(b, t):
                        n = TT * b + t
                        pool.wait_ge(ve_ok, n + 1)
                        nc.gpsimd.tensor_tensor(rp2[:, :], ve2[:, :], half[:, 0:1], ALU.pow).then_inc(rp_ok, 1)
                        pool.wait_ge(h_ok, n + 1)
                        nc.gpsimd.tensor_tensor(xt[:, t % 2, :], xt[:, t % 2, :], brow[:, :], ALU.add).then_inc(bias_ok, 1)

                    pool.wait_ge(s_row, 64)
                    with pool.Fori(0, B) as b:
                        for t in range(TT):
                            prepare(b, t)

                @block.scalar
                def _(act):
                    def prepare(b, t):
                        n, k = TT * b + t, t % 2
                        act.wait_ge(s_xt[k], 16 * (2 * b + t // 2 + 1))
                        act.wait_ge(nb_ok, n + 1)
                        if later(b, t):
                            act.wait_ge(ht_spec, 4 * n)
                        nc.scalar.activation(h[:, :], xt[:, k, :], ACT.Identity, bias=nb2[:, 0:1], scale=rs2[:, 0:1]).then_inc(h_ok, 1)
                        if later(b, t) and later(b, t - 1):
                            act.wait_ge(y_spec, 4 * n - 4)
                        for q in range(4):
                            act.wait_ge(ht_spec, 4 * n + q + 1)
                            nc.scalar.activation(h_hi[:, k, 4 * q:4 * q + 4, :], ps[:, 4 + q, :].rearrange("p (c t) -> p c t", t=P),
                                                 ACT.Copy).then_inc(hi_ok, 1)
                        act.wait_ge(axt_spec, n + 1)
                        if later(b, t):
                            act.wait_ge(y_spec, 4 * n)
                        nc.scalar.activation(axT[:, :], ps[0:2 * RANK, 5, 0:P], ACT.Copy).then_inc(axt_ok, 1)

                    for t in range(TT):
                        prepare(0, t)
                    with act.Fori(1, B) as b:
                        for t in range(TT):
                            prepare(b, t)

                @block.tensor
                def _(pe):
                    def transposes(b, t):
                        n = TT * b + t
                        pe.wait_ge(h_ok, n + 1)
                        if later(b, t):
                            pe.wait_ge(axt_ok, n)
                        for q in range(4):
                            for c in range(4):
                                i = 4 * q + c
                                last = nc.tensor.transpose(ps[:, 4 + q, c * P:(c + 1) * P], h[:, i * P:(i + 1) * P], ident[:, :])
                            last.then_inc(ht_spec, 1)

                    def adapter_in(b, t):
                        n, k = TT * b + t, t % 2
                        pe.wait_ge(hi_ok, 4 * n + 4)
                        pe.wait_ge(lo_ok, 4 * n + 4)
                        bank = ps[:, 4, 0:2 * RANK]
                        for s, own in enumerate((True, False)):
                            dst = bank[:, s * RANK:(s + 1) * RANK]
                            for i in range(KT):
                                def a_of(a):
                                    return a[:, i, bass.ds(b, 1), :].squeeze(1) if own else a[:, i, B, :]
                                nc.tensor.matmul(dst, h_hi[:, k, i, :], a_of(a_hi), start=(i == 0), stop=False)
                                nc.tensor.matmul(dst, h_hi[:, k, i, :], a_of(a_lo), start=False, stop=False)
                                last = nc.tensor.matmul(dst, h_lo[:, k, i, :], a_of(a_hi), start=False, stop=(i == KT - 1))
                        last.then_inc(ax_spec, 1)

                    def chunk(b, t, c):
                        n, k = TT * b + t, t % 2
                        if later(b, t):
                            pe.wait_ge(y_ok, 4 * n)
                        else:
                            pe.wait_ge(s_w[c], 32)
                        cols = slice(c * 512, (c + 1) * 512)
                        for i in range(KT):
                            nc.tensor.matmul(ps[:, c, :], h_hi[:, k, i, :], w_hi[:, i, cols], start=(i == 0), stop=False)
                            nc.tensor.matmul(ps[:, c, :], h_hi[:, k, i, :], w_lo[:, i, cols], start=False, stop=False)
                            nc.tensor.matmul(ps[:, c, :], h_lo[:, k, i, :], w_hi[:, i, cols], start=False, stop=False)
                        if c == 0:
                            pe.wait_ge(ax_ok, n + 1)
                            nc.tensor.matmul(ps[0:2 * RANK, 5, 0:P], ax[:, :], ident[:, :], start=True, stop=True).then_inc(axt_spec, 1)
                            pe.wait_ge(axt_ok, n + 1)
                            pe.wait_ge(s_b, 16 * b + 16)
                        nc.tensor.matmul(ps[:, c, :], axT[:, :], bcat[:, cols], start=False, stop=True).then_inc(y_spec, 1)

                    def step(b, t, more):
                        nxt = ahead(b, t, 1)
                        chunk(b, t, 0)
                        chunk(b, t, 1)
                        if more:
                            transposes(*nxt)
                        chunk(b, t, 2)
                        chunk(b, t, 3)
                        if more:
                            adapter_in(*nxt)

                    transposes(0, 0)
                    pe.wait_ge(s_row, 64)
                    adapter_in(0, 0)
                    for t in range(TT):
                        step(0, t, True)
                    with pe.Fori(1, B - 1) as b:
                        for t in range(TT):
                            step(b, t, True)
                    for t in range(TT):
                        step(B - 1, t, t + 1 < TT)

                @block.vector
                def _(dve):
                    def statistics(b, t):
                        n, k = TT * b + t, t % 2
                        dve.sem_clear(own2)
                        dve.wait_ge(s_xt[k], 16 * (2 * b + t // 2 + 1))
                        for c in range(4):
                            last = nc.vector.bn_stats(bn2[:, c, :], xt[:, k, c * 512:(c + 1) * 512])
                        last.then_inc(own2, 1)
                        dve.wait_ge(own2, 1)
                        nc.vector.bn_aggr(mv2[:, :], bn2[:, :, :].rearrange("p c s -> p (c s)")).then_inc(own2, 1)
                        dve.wait_ge(own2, 2)
                        nc.vector.tensor_scalar(ve2[:, :], mv2[:, 1:2], EPS, None, ALU.add).then_inc(ve_ok, 1)
                        dve.wait_ge(rp_ok, n + 1)
                        if later(b, t):
                            dve.wait_ge(h_ok, n)
                        nc.vector.tensor_scalar(rs2[:, :], rp2[:, :], HSCALE, None, ALU.mult).then_inc(own2, 1)
                        dve.wait_ge(own2, 3)
                        nc.vector.tensor_scalar(nb2[:, :], mv2[:, 0:1], rs2[:, 0:1], -1.0, ALU.mult, ALU.mult).then_inc(nb_ok, 1)

                    def rest_of_h(b, t):
                        n, k = TT * b + t, t % 2
                        for q in range(4):
                            dve.wait_ge(hi_ok, 4 * n + q + 1)
                            nc.vector.tensor_tensor(h_lo[:, k, 4 * q:4 * q + 4, :], ps[:, 4 + q, :].rearrange("p (c t) -> p c t", t=P),
                                                    h_hi[:, k, 4 * q:4 * q + 4, :], ALU.subtract).then_inc(lo_ok, 1)

                    def adapter(b, t):
                        n = TT * b + t
                        dve.wait_ge(ax_spec, n + 1)
                        if later(b, t):
                            dve.wait_ge(axt_spec, n)
                        nc.vector.tensor_scalar(ax[:, :], ps[:, 4, 0:2 * RANK], ax_fix[:, 0:1], None, ALU.mult).then_inc(ax_ok, 1)

                    def finish(b, t, c):
                        n, k = TT * b + t, t % 2
                        if c == 0:
                            dve.wait_ge(bias_ok, n + 1)
                        dve.wait_ge(y_spec, 4 * n + c + 1)
                        cols = slice(c * 512, (c + 1) * 512)
                        nc.vector.scalar_tensor_tensor(out=xt[:, k, cols], in0=ps[:, c, :], scalar=w_back[:, 0:1], in1=xt[:, k, cols],
                                                       op0=ALU.mult, op1=ALU.add).then_inc(y_ok, 1)

                    def step(b, t, more):
                        nxt = ahead(b, t, 1)
                        if more:
                            statistics(*nxt)
                        finish(b, t, 0)
                        finish(b, t, 1)
                        if more:
                            rest_of_h(*nxt)
                        finish(b, t, 2)
                        finish(b, t, 3)
                        if more:
                            adapter(*nxt)

                    statistics(0, 0)
                    rest_of_h(0, 0)
                    adapter(0, 0)
                    for t in range(TT):
                        step(0, t, True)
                    with dve.Fori(1, B - 1) as b:
                        for t in range(TT):
                            step(b, t, True)
                    for t in range(TT):
                        step(B - 1, t, t + 1 < TT)


def kernel(x, ctx_4096, L0_ffn_gate, L0_ffn_kernel, L0_ffn_bias, L0_ffn_lora_A, L0_ffn_lora_B,
           L0_ffn_lora_A_shared, L0_ffn_lora_B_shared):
    import concourse.bacc as bacc
    from concourse.bass_utils import run_bass_kernel_spmd

    fwd_tab, fwd_pair, inv_tab = dft_tables()
    nyq_mask = np.ones((P, 1), np.float32)
    nyq_mask[0] = 0.0
    arrays = {
        "x": np.ascontiguousarray(x),
        "ctx": np.ascontiguousarray(ctx_4096),
        "gateT": np.ascontiguousarray(np.asarray(L0_ffn_gate).T),
        "w": np.ascontiguousarray(L0_ffn_kernel),
        "bias": np.ascontiguousarray(L0_ffn_bias),
        "lora_a": np.ascontiguousarray(np.asarray(L0_ffn_lora_A).reshape(NL * RANK, D)),
        "lora_bT": np.ascontiguousarray(np.asarray(L0_ffn_lora_B).transpose(0, 2, 1).reshape(NL * RANK, D)),
        "lora_as": np.ascontiguousarray(L0_ffn_lora_A_shared),
        "lora_bsT": np.ascontiguousarray(np.asarray(L0_ffn_lora_B_shared).T),
        "fwd_tab": fwd_tab,
        "inv_tab": inv_tab,
        "eye": np.eye(P, dtype=np.float32),
        "rank_sel": np.ascontiguousarray(np.tile(np.eye(RANK, dtype=np.float32), (P // RANK, 1))),
        "nyq_mask": nyq_mask,
        "fwd_pair": fwd_pair,
    }
    nc = bacc.Bacc("TRN2", target_bir_lowering=False, num_devices=1)
    args = [nc.dram_tensor(name, a.shape, mybir.dt.from_np(a.dtype), kind="ExternalInput").ap() for name, a in arrays.items()]
    args.append(nc.dram_tensor("out", (B, L, D), FP32, kind="ExternalOutput").ap())
    build(nc, *args)
    r = run_bass_kernel_spmd(nc, [arrays], core_ids=[0])
    return r.results[0]["out"]
```

```python
from contextlib import ExitStack

import concourse.bass as bass
import numpy as np
from concourse import mybir

FP32 = mybir.dt.float32
FP16 = mybir.dt.float16
U32 = mybir.dt.uint32
ALU = mybir.AluOpType
ACT = mybir.ActivationFunctionType
AXX = mybir.AxisListType.X

P = 128
B, L, D = 8, 512, 2048
TT = L // P
GC = 512
GPB = D // GC
NG = B * GPB
CT = GC // P
HALF = L // 2
TOPK = int(2 * np.log(L))
NT = B * TT
KT = D // P
NL, RANK = 16, 32
NLT = NL * RANK // P
EPS = 1e-5
NEG = float(np.float32(-3.0e38))
WSCALE = 2.0 ** 14
TSCALE = 2.0 ** 10
QSCALE = 2.0 ** 9
HSCALE = 1024.0
AXSCALE = 2.0 ** -21
ER, EI, OR, OI = range(4)
TURN = (2, 3, 0, 1)
assert TT == 4 and GPB == 4 and CT == 4 and 8 < TOPK <= 16


def dft_tables():
    n = np.arange(HALF)[:, None].astype(np.float64)
    f = np.arange(P)[None, :].astype(np.float64)
    even = 2 * np.pi * n * f / HALF
    odd = 2 * np.pi * n * (2 * f + 1) / L
    alt = (-1.0) ** np.arange(HALF)
    fwd = np.zeros((HALF, 4, P))
    fwd[:, ER], fwd[:, EI], fwd[:, OR], fwd[:, OI] = np.cos(even), -np.sin(even), np.cos(odd), -np.sin(odd)
    fwd_w = fwd * TSCALE
    fwd[:, EI, 0] = alt
    fwd_w[:, EI, 0] = -alt * TSCALE
    inv = np.zeros((P, 4, HALF))
    inv[:, ER], inv[:, EI] = 2 * np.cos(even).T / L, -2 * np.sin(even).T / L
    inv[:, OR], inv[:, OI] = 2 * np.cos(odd).T / L, -2 * np.sin(odd).T / L
    inv[0, ER] = 1.0 / L
    inv[0, EI] = alt / L

    def lay(a, dt):
        return np.ascontiguousarray(a.reshape(2, P, 4, P).transpose(1, 0, 2, 3), dtype=dt)

    high = fwd_w.astype(np.float16).astype(np.float64)
    pair = np.stack([lay(high, np.float16), lay(fwd_w - high, np.float16)], axis=1)
    return lay(fwd, np.float32), pair, np.ascontiguousarray(inv, dtype=np.float32)


def ahead(b, g, k):
    c = (g + k) // GPB
    return (b + c if c else b), (g + k) % GPB


def piece(b, g, h):
    return 2 * GPB * b + 2 * g + h - GPB * B


def later(b, i):
    return not (isinstance(b, int) and b == 0 and i == 0)


def build(nc, x, ctx, gateT, w, bias, lora_a, lora_bT, lora_as, lora_bsT, fwd_tab, inv_tab, eye, rank_sel, nyq_mask, fwd_pair, out):
    x2 = nc.dram_tensor("x2_scratch", [B, L, D + 1024], FP32).ap()[:, :, 0:D]
    beff = nc.dram_tensor("beff_scratch", [B * RANK, D], FP32).ap()
    w_pair = nc.dram_tensor("w_pair_scratch", [2, KT, P, D + 1024], FP16).ap()[:, :, :, 0:D]
    aeff = nc.dram_tensor("aeff_scratch", [B + 1, P, KT * RANK], FP32).ap()
    x_g = x.rearrange("b (t p) c -> b p t c", p=P)
    ctx_g = ctx.rearrange("b (t p) c -> b p t c", p=P)
    x2_g = x2.rearrange("b (t p) c -> b p t c", p=P)
    w_t = w.rearrange("(k p) o -> k p o", p=P)
    w_b = w.rearrange("(b k p) o -> b k p o", p=P, b=B // 2)
    w_pair_b = w_pair.rearrange("a (b k) p o -> a b k p o", b=B // 2)

    with ExitStack() as outer:
        def sb(name, shape, dt=FP32, where=outer):
            return where.enter_context(nc.sbuf_tensor(name, shape, dt))

        def sem(name, where=outer):
            return where.enter_context(nc.semaphore(name))

        ident = sb("ident", [P, P])
        rsb = sb("rsb", [P, TT])
        nbb = sb("nbb", [P, TT])
        rsn = sb("rsn", [P, TT])
        nbn = sb("nbn", [P, TT])
        half = sb("half", [P, TT])
        w_scale = sb("w_scale", [P, 1])
        w_back = sb("w_back", [P, 1])
        a_scale = sb("a_scale", [P, 1])
        b_scale = sb("b_scale", [P, 1])
        d_back = sb("d_back", [P, 1])
        ps = outer.enter_context(nc.psum_tensor("ps", [P, 8, 512], FP32))

        mid = ExitStack()
        ft = sb("ft", [P, 2, 4, P], FP32, mid)
        fp = sb("fp", [P, 2, 2, 4, P], FP16, mid)
        it = sb("it", [P, 4, HALF], FP32, mid)
        nyq = sb("nyq", [P, 1], FP32, mid)
        xg = sb("xg", [P, 2, TT, GC], FP32, mid)
        cg = sb("cg", [P, 2, TT, GC], FP32, mid)
        vrow = sb("vrow", [P, GC], FP32, mid)
        s_tabs = sem("s_tabs", mid)
        s_x = [sem(f"s_x{k}", mid) for k in range(2)]
        s_c = [sem(f"s_c{k}", mid) for k in range(2)]
        s_v = sem("s_v", mid)

        def load_inputs(sp, b, g):
            cols = slice(g * GC, (g + 1) * GC)
            sp.dma_start(cg[:, g % 2, :, :], ctx_g[b, :, :, cols]).then_inc(s_c[g % 2], 16)
            sp.dma_start(xg[:, g % 2, :, :], x_g[b, :, :, cols]).then_inc(s_x[g % 2], 16)

        def load_v_row(sp, b, g):
            sp.dma_start(vrow[:, :], ctx[b, L - 1, g * GC:(g + 1) * GC].partition_broadcast(P)).then_inc(s_v, 16)

        with ExitStack() as st:
            xs = sb("xs", [P, TT, D], FP32, st)
            bn = sb("bn", [P, 2 * TT, TT * 6], FP32, st)
            mv = sb("mv", [P, 2 * TT, 2], FP32, st)
            var_eps = sb("var_eps", [P, 2 * TT], FP32, st)
            negmean = sb("negmean", [P, 2 * TT], FP32, st)
            la = sb("la", [P, NLT, D], FP32, st)
            lb = sb("lb", [P, NLT, D], FP32, st)
            las = sb("las", [RANK, D], FP32, st)
            rsel = sb("rsel", [P, RANK], FP32, st)
            gcol = sb("gcol", [P, NLT, B], FP32, st)
            gsel = sb("gsel", [P, NLT, B, RANK], FP32, st)
            bsh = sb("bsh", [RANK, D], FP32, st)
            a_t = sb("a_t", [P, B + 1, KT, RANK], FP32, st)
            b_t = sb("b_t", [P, 2, D], FP32, st)
            bmax = sb("bmax", [P, 8], FP32, st)
            top = sb("top", [P, 3], FP32, st)
            topall = sb("topall", [P, 3], FP32, st)
            pow2 = sb("pow2", [P, 3], FP32, st)
            rpow = sb("rpow", [P, 2], FP32, st)

            s_tab = sem("s_tab", st)
            s_lora = sem("s_lora", st)
            s_lorb = sem("s_lorb", st)
            s_bsh = sem("s_bsh", st)
            s_xs = [sem(f"s_xs{k}", st) for k in range(TT)]
            s_xs_used = sem("s_xs_used", st)
            s_gcol = sem("s_gcol", st)
            s_chain = sem("s_chain", st)
            s_var = sem("s_var", st)
            s_rs = sem("s_rs", st)
            s_gsel = sem("s_gsel", st)
            s_at = sem("s_at", st)
            s_at_out = sem("s_at_out", st)
            s_bt = sem("s_bt", st)
            s_bt_out = sem("s_bt_out", st)
            s_bmax = sem("s_bmax", st)
            s_top = sem("s_top", st)
            s_topall = sem("s_topall", st)
            s_store = sem("s_store", st)

            with nc.Block() as block:
                @block.sync
                def _(sp):
                    sp.dma_start(ident[:, :], eye).then_inc(s_tab, 16)
                    sp.dma_start(rsel[:, :], rank_sel).then_inc(s_tab, 16)
                    for n in range(P // RANK):
                        src = gateT.rearrange("(k n) b -> n k b", n=P // RANK)[n].partition_broadcast(RANK)
                        sp.dma_start(gcol[n * RANK:(n + 1) * RANK, :, :], src).then_inc(s_gcol, 16)
                    sp.dma_start(las[:, :], lora_as).then_inc(s_lora, 16)
                    sp.dma_start(la[:, :, :], lora_a.rearrange("(k p) i -> p k i", p=P)).then_inc(s_lora, 16)
                    for b in range(2):
                        if b:
                            sp.dma_start(lb[:, :, :], lora_bT.rearrange("(k p) o -> p k o", p=P)).then_inc(s_lorb, 16)
                            sp.dma_start(bsh[:, :], lora_bsT).then_inc(s_bsh, 16)
                        for k in range(TT):
                            if b:
                                sp.wait_ge(s_xs_used, k + 1)
                            sp.dma_start(xs[:, k, :], x_g[b, :, k, :]).then_inc(s_xs[k], 16)
                    for tab, src in ((ft, fwd_tab), (it, inv_tab), (nyq, nyq_mask), (fp, fwd_pair)):
                        sp.dma_start(tab[tuple(slice(None) for _ in tab.shape)], src).then_inc(s_tabs, 16)
                    load_inputs(sp, 0, 0)
                    load_v_row(sp, 0, 0)
                    load_inputs(sp, 0, 1)
                    sp.wait_ge(s_at_out, KT)
                    sp.dma_start(aeff.rearrange("b p f -> p b f"), a_t[:, :, :, :].rearrange("p b k r -> p b (k r)")).then_inc(s_store, 16)
                    sp.wait_ge(s_bt_out, 8)
                    sp.dma_start(beff.rearrange("(m p) o -> p m o", p=P), b_t[:, :, :]).then_inc(s_store, 16)
                    sp.wait_ge(s_store, 32)

                @block.gpsimd
                def _(pool):
                    nc.gpsimd.memset(half[:, :], -0.5).then_inc(s_chain, 1)
                    pool.wait_ge(s_chain, 1)
                    pool.wait_ge(s_var, 1)
                    for b, (rs, nb) in enumerate(((rsb, nbb), (rsn, nbn))):
                        cols = slice(b * TT, (b + 1) * TT)
                        nc.gpsimd.tensor_tensor(rs[:, :], var_eps[:, cols], half[:, :], ALU.pow).then_inc(s_rs, 1)
                        pool.wait_ge(s_rs, b + 1)
                        nc.gpsimd.tensor_tensor(nb[:, :], negmean[:, cols], rs[:, :], ALU.mult)
                    pool.wait_ge(s_top, 4)
                    nc.gpsimd.partition_all_reduce(topall[:, :], top[:, :], P, bass.bass_isa.ReduceOp.max).then_inc(s_topall, 1)

                @block.scalar
                def _(act):
                    for i in range(KT):
                        act.wait_ge(s_at, i + 1)
                        nc.scalar.activation(a_t[:, :, i, :], ps[:, i % 4, 0:(B + 1) * RANK].rearrange("p (b r) -> p b r", r=RANK),
                                             ACT.Copy).then_inc(s_at_out, 1)
                    for i in range(8):
                        act.wait_ge(s_bt, i + 1)
                        nc.scalar.activation(b_t[:, i // 4, (i % 4) * 512:(i % 4 + 1) * 512], ps[:, 4 + i % 4, :],
                                             ACT.Copy).then_inc(s_bt_out, 1)

                @block.tensor
                def _(pe):
                    pe.wait_ge(s_lora, 32)
                    pe.wait_ge(s_tab, 32)
                    pe.wait_ge(s_gsel, 1)
                    for i in range(KT):
                        if i >= 4:
                            pe.wait_ge(s_at_out, i - 3)
                        for k in range(NLT):
                            nc.tensor.matmul(ps[:, i % 4, 0:B * RANK], la[:, k, i * P:(i + 1) * P],
                                             gsel[:, k, :, :].rearrange("p b r -> p (b r)"), start=(k == 0), stop=(k == NLT - 1))
                        nc.tensor.matmul(ps[:, i % 4, B * RANK:(B + 1) * RANK], las[:, i * P:(i + 1) * P],
                                         ident[0:RANK, 0:RANK], start=True, stop=True).then_inc(s_at, 1)
                    pe.wait_ge(s_lorb, 16)
                    for i in range(8):
                        if i >= 4:
                            pe.wait_ge(s_bt_out, i - 3)
                        for k in range(NLT):
                            last = nc.tensor.matmul(ps[:, 4 + i % 4, :],
                                                    gsel[:, k, 4 * (i // 4):4 * (i // 4) + 4, :].rearrange("p b r -> p (b r)"),
                                                    lb[:, k, (i % 4) * 512:(i % 4 + 1) * 512],
                                                    start=(k == 0), stop=(k == NLT - 1))
                        last.then_inc(s_bt, 1)

                @block.vector
                def _(dve):
                    chain = [0]

                    def link(ins):
                        chain[0] += 1
                        ins.then_inc(s_mine, 1)
                        dve.wait_ge(s_mine, chain[0])

                    s_mine = sem("s_mine", st)
                    s_mv = sem("s_mv", st)
                    dve.wait_ge(s_tab, 32)
                    dve.wait_ge(s_gcol, 16 * (P // RANK))
                    nc.vector.tensor_tensor(gsel[:, :, :, :].rearrange("p k b r -> p (k b) r"),
                                            gcol[:, :, :].rearrange("p k b -> p (k b)").unsqueeze(2).broadcast_to([P, NLT * B, RANK]),
                                            rsel[:, :].unsqueeze(1).broadcast_to([P, NLT * B, RANK]), ALU.mult).then_inc(s_gsel, 1)
                    for t in range(2 * TT):
                        dve.wait_ge(s_xs[t % TT], 16 * (t // TT + 1))
                        for c in range(TT):
                            last = nc.vector.bn_stats(bn[:, t, 6 * c:6 * c + 6], xs[:, t % TT, c * 512:(c + 1) * 512])
                        last.then_inc(s_xs_used, 1)
                    dve.wait_ge(s_xs_used, 2 * TT)
                    for t in range(2 * TT):
                        last = nc.vector.bn_aggr(mv[:, t, :], bn[:, t, :])
                    last.then_inc(s_mv, 1)
                    dve.wait_ge(s_mv, 1)
                    nc.vector.tensor_scalar(negmean[:, :], mv[:, :, 0], -1.0, None, ALU.mult)
                    nc.vector.tensor_scalar(var_eps[:, :], mv[:, :, 1], EPS, QSCALE ** -2, ALU.add, ALU.mult).then_inc(s_var, 1)
                    nc.vector.memset(top[:, 2:3], 0.0).then_inc(s_top, 1)
                    dve.wait_ge(s_at_out, KT)
                    nc.vector.tensor_reduce(top[:, 0:1], a_t[:, :, :, :].rearrange("p b k r -> p (b k r)"), AXX, ALU.max,
                                            apply_absolute_value=True).then_inc(s_top, 1)
                    dve.wait_ge(s_bsh, 16)
                    dve.wait_ge(s_top, 1)
                    nc.vector.tensor_reduce(top[0:RANK, 2:3], bsh[:, :], AXX, ALU.max, apply_absolute_value=True).then_inc(s_top, 1)
                    for i in range(8):
                        dve.wait_ge(s_bt_out, i + 1)
                        nc.vector.tensor_reduce(bmax[:, i:i + 1], b_t[:, i // 4, (i % 4) * 512:(i % 4 + 1) * 512], AXX, ALU.max,
                                                apply_absolute_value=True).then_inc(s_bmax, 1)
                    dve.wait_ge(s_bmax, 8)
                    nc.vector.tensor_reduce(top[:, 1:2], bmax[:, :], AXX, ALU.max).then_inc(s_top, 1)
                    dve.wait_ge(s_topall, 1)
                    link(nc.vector.tensor_scalar(pow2[:, :], topall[:, :], 1e-30, None, ALU.max))
                    link(nc.vector.tensor_tensor(pow2[:, 1:2], pow2[:, 1:2], pow2[:, 2:3], ALU.max))
                    link(nc.vector.tensor_scalar(pow2[:, :].bitcast(U32), pow2[:, :].bitcast(U32), 0x7F800000, None, ALU.bitwise_and))
                    link(nc.vector.reciprocal(rpow[:, :], pow2[:, 0:2]))
                    for k, scale in enumerate((a_scale, b_scale)):
                        nc.vector.tensor_scalar(scale[:, :], rpow[:, k:k + 1], 16384.0, None, ALU.mult)
                    link(nc.vector.tensor_scalar(d_back[:, :], pow2[:, 0:1], pow2[:, 1:2], 1.0 / (16384.0 ** 2 * HSCALE * AXSCALE),
                                                 ALU.mult, ALU.mult))

        with ExitStack() as st:
            qa = sb("qa", [P, 2, GC], FP32, st)
            va = sb("va", [P, 2, GC], FP32, st)
            zs = sb("zs", [P, 2, GC], FP32, st)
            qh = sb("qh", [P, 4, GC], FP16, st)
            xv = sb("xv", [P, TT, GC], FP32, st)
            vlast = sb("vlast", [1, GC], FP32, st)
            spe = sb("spe", [P, 2, 2, 3, GC], FP32, st)
            spo = sb("spo", [P, 2, 2, 2, GC], FP32, st)
            mr = sb("mr", [P, 4, GC], FP32, st)
            mi = sb("mi", [P, 4, GC], FP32, st)
            mhr = sb("mhr", [P, 2, GC], FP32, st)
            mhi = sb("mhi", [P, 2, GC], FP32, st)
            cp = sb("cp", [P, 4, GC], FP32, st)
            op = sb("op", [P, 2, 4, GC], FP32, st)
            eo = sb("eo", [P, CT, L], FP32, st)
            cr = sb("cr", [P, CT, L], FP32, st)
            wd = sb("wd", [P, CT, L], FP32, st)
            wt = sb("wt", [P, 2, 4, GC], FP16, st)
            m16 = sb("m16", [P, CT, 16], FP32, st)
            nmax = sb("nmax", [P, CT], FP32, st)
            zsum = sb("zsum", [P, CT], FP32, st)
            rz = sb("rz", [P, CT], FP32, st)
            xrow = sb("xrow", [P, D], FP32, st)
            wmax = sb("wmax", [P, GPB], FP32, st)
            wnew = sb("wnew", [P, GPB], FP32, st)
            wtop = sb("wtop", [P, 4], FP32, st)
            bn1 = sb("bn1", [P, TT * 6], FP32, st)
            mv1 = sb("mv1", [P, TT, 2], FP32, st)
            ve1 = sb("ve1", [P, TT], FP32, st)
            nm1 = sb("nm1", [P, TT], FP32, st)
            wc = sb("wc", [P, D // 2], FP32, st)
            wch = sb("wch", [P, D // 2], FP16, st)
            ql = [xg[:, k, 2:4, :].rearrange("p t c -> p (t c)").bitcast(FP16).rearrange("p (t c) -> p t c", c=GC) for k in range(2)]
            wcl = wc[:, :].bitcast(FP16)[:, 0:D // 2]

            s_xr = sem("s_xr", st)
            s_st = sem("s_st", st)
            s_xrow = sem("s_xrow", st)
            s_wc = sem("s_wc", st)
            s_wst = sem("s_wst", st)
            q_norm = sem("q_norm", st)
            cols_ok = sem("cols_ok", st)
            v_fold = sem("v_fold", st)
            z_fold = sem("z_fold", st)
            q_fold = sem("q_fold", st)
            q_hi = sem("q_hi", st)
            q_lo = sem("q_lo", st)
            v_spec = sem("v_spec", st)
            q_spec = sem("q_spec", st)
            z_spec = sem("z_spec", st)
            v_out = sem("v_out", st)
            z_out = sem("z_out", st)
            cprod = sem("cprod", st)
            cp_sum = sem("cp_sum", st)
            cp_turn = sem("cp_turn", st)
            corr_spec = sem("corr_spec", st)
            corr_out = sem("corr_out", st)
            own = sem("own", st)
            nmax_ok = sem("nmax_ok", st)
            exp_ok = sem("exp_ok", st)
            w_ready = sem("w_ready", st)
            wt_spec = sem("wt_spec", st)
            wt_hi = sem("wt_hi", st)
            wt_lo = sem("wt_lo", st)
            w_spec = sem("w_spec", st)
            oprod = sem("oprod", st)
            pair_sum = sem("pair_sum", st)
            op_sum = sem("op_sum", st)
            hi_sum = sem("hi_sum", st)
            rz_ok = sem("rz_ok", st)
            out_spec = sem("out_spec", st)
            out_add = sem("out_add", st)
            row_used = sem("row_used", st)
            ve_ok = sem("ve_ok", st)
            rsn_ok = sem("rsn_ok", st)
            s_wx = sem("s_wx", st)
            wx_used = sem("wx_used", st)
            wmax_ok = sem("wmax_ok", st)
            top_ok = sem("top_ok", st)
            topall_ok = sem("topall_ok", st)
            scale_ok = sem("scale_ok", st)
            wch_ok = sem("wch_ok", st)
            wcl_ok = sem("wcl_ok", st)

            with nc.Block() as block:
                @block.sync
                def _(sp):
                    def load_row(b, g):
                        if later(b, g):
                            sp.wait_ge(z_fold, 2 * (GPB * b + g))
                        load_v_row(sp, b, g)

                    def load_residual(b, g):
                        sp.dma_start(xv[:, :, :], x_g[b, :, :, g * GC:(g + 1) * GC]).then_inc(s_xr, 16)
                        sp.dma_start(vlast[:, :], ctx[b, L - 1, g * GC:(g + 1) * GC].unsqueeze(0)).then_inc(s_xr, 16)

                    def load_weights(b, g, h):
                        sp.dma_start(wc[:, :], w_b[b - B // 2, g, :, h * (D // 2):(h + 1) * (D // 2)]).then_inc(s_wc, 16)

                    def step(b, g, more, lead, rows, convert):
                        n = GPB * b + g
                        if more:
                            sp.wait_ge(z_spec, 4 * n + 8)
                            load_inputs(sp, *ahead(b, g, 3))
                        if not convert:
                            sp.wait_ge(row_used, n + 1)
                            sp.dma_start(xrow[:, :], w_t[n]).then_inc(s_wx, 16)
                            sp.wait_ge(wx_used, n + 1)
                        if rows:
                            if convert:
                                sp.wait_ge(row_used, n + 1)
                            nb, nt = ahead(b, g, 1)
                            sp.dma_start(xrow[:, :], x_g[nb + 2, :, nt, :]).then_inc(s_xrow, 16)
                        if convert:
                            for h in range(2):
                                m = piece(b, g, h)
                                sp.wait_ge(wch_ok, m + 1)
                                sp.wait_ge(wcl_ok, m + 1)
                                half_cols = slice(h * (D // 2), (h + 1) * (D // 2))
                                sp.dma_start(w_pair_b[0, b - B // 2, g, :, half_cols], wch[:, :]).then_inc(s_wst, 16)
                                sp.dma_start(w_pair_b[1, b - B // 2, g, :, half_cols], wcl).then_inc(s_wst, 16)
                                if h == 0 or lead:
                                    sp.wait_ge(s_wst, 32 * m + 32)
                                    load_weights(*((b, g, 1) if h == 0 else (*ahead(b, g, 1), 0)))
                        if more:
                            load_row(*ahead(b, g, 3))
                        sp.wait_ge(out_add, 4 * n + 4)
                        sp.dma_start(x2_g[b, :, :, g * GC:(g + 1) * GC], xv[:, :, :]).then_inc(s_st, 16)
                        if lead:
                            sp.wait_ge(s_st, 16 * n + 16)
                            load_residual(*ahead(b, g, 1))

                    load_residual(0, 0)
                    sp.dma_start(xrow[:, :], x_g[2, :, 0, :]).then_inc(s_xrow, 16)
                    load_row(0, 1)
                    sp.wait_ge(z_spec, 4)
                    load_inputs(sp, 0, 2)
                    load_row(0, 2)
                    for g in range(GPB):
                        step(0, g, True, True, True, False)
                    with sp.Fori(1, B // 2) as b:
                        for g in range(GPB):
                            step(b, g, True, True, True, False)
                    load_weights(B // 2, 0, 0)
                    for g in range(GPB):
                        step(B // 2, g, True, True, True, True)
                    for g in range(GPB):
                        step(B - 3, g, True, True, g < GPB - 1, True)
                    for g in range(GPB):
                        step(B - 2, g, True, True, False, True)
                    for g in range(GPB):
                        step(B - 1, g, g + 3 < GPB, g + 1 < GPB, False, True)
                    sp.wait_ge(s_st, 16 * NG)
                    sp.wait_ge(s_wst, 32 * 2 * KT)

                @block.gpsimd
                def _(pool):
                    def fold_v(b, g):
                        m, k = GPB * b + g, g % 2
                        pool.wait_ge(s_c[k], 16 * (2 * b + g // 2 + 1))
                        if later(b, g):
                            pool.wait_ge(v_spec, 4 * m)
                        nc.gpsimd.tensor_tensor(va[:, :, :], cg[:, k, 0:2, :], cg[:, k, 2:4, :], ALU.add).then_inc(v_fold, 1)
                        nc.gpsimd.tensor_tensor(cg[:, k, 0:2, :], cg[:, k, 0:2, :], cg[:, k, 2:4, :], ALU.subtract).then_inc(v_fold, 1)

                    def fold_z(b, g):
                        m, k = GPB * b + g, g % 2
                        pool.wait_ge(s_v, 16 * m + 16)
                        row = vrow[:, :].unsqueeze(1).broadcast_to([P, 2, GC])
                        if later(b, g):
                            pool.wait_ge(z_spec, 4 * m)
                        nc.gpsimd.tensor_tensor(zs[:, :, :], cg[:, k, 2:4, :], row, ALU.add).then_inc(z_fold, 1)
                        pool.wait_ge(v_fold, 2 * m + 2)
                        nc.gpsimd.tensor_tensor(cg[:, k, 2:4, :], cg[:, k, 2:4, :], row, ALU.subtract).then_inc(z_fold, 1)

                    def fold_q(b, g):
                        m, k = GPB * b + g, g % 2
                        if later(b, g):
                            pool.wait_ge(q_lo, 2 * m)
                        pool.wait_ge(q_norm, 4 * m + 4)
                        nc.gpsimd.tensor_tensor(qa[:, :, :], xg[:, k, 0:2, :], xg[:, k, 2:4, :], ALU.add).then_inc(q_fold, 1)
                        nc.gpsimd.tensor_tensor(xg[:, k, 0:2, :], xg[:, k, 0:2, :], xg[:, k, 2:4, :], ALU.subtract).then_inc(q_fold, 1)

                    def rest_of_q(b, g):
                        m, k = GPB * b + g, g % 2
                        pool.wait_ge(q_fold, 2 * m + 2)
                        for h, src in enumerate((qa[:, :, :], xg[:, k, 0:2, :])):
                            pool.wait_ge(q_hi, 2 * m + h + 1)
                            nc.gpsimd.tensor_tensor(ql[k][:, 2 * h:2 * h + 2, :], src, qh[:, 2 * h:2 * h + 2, :], ALU.subtract).then_inc(q_lo, 1)

                    def corr_sums(b, g):
                        m = GPB * b + g
                        if later(b, g):
                            pool.wait_ge(corr_spec, 4 * m)
                        pool.wait_ge(cprod, 4 * m + 4)
                        nc.gpsimd.tensor_tensor(cp[:, 0::2, :], mr[:, 0::2, :], mr[:, 1::2, :], ALU.add).then_inc(cp_sum, 1)
                        nc.gpsimd.tensor_tensor(cp[:, 1::2, :], mi[:, 1::2, :], mi[:, 0::2, :], ALU.subtract).then_inc(cp_sum, 1)

                    def out_sums(b, g):
                        n = GPB * b + g
                        if later(b, g):
                            pool.wait_ge(out_spec, 4 * n)
                        for h in range(2):
                            r, i = 2 * h, 2 * h + 1
                            pool.wait_ge(oprod, 9 * n + 5 * h + 1)
                            nc.gpsimd.tensor_tensor(mr[:, 0:2, :], mr[:, 0:2, :], mr[:, 2:4, :], ALU.add).then_inc(pair_sum, 1)
                            pool.wait_ge(oprod, 9 * n + 5 * h + 2)
                            nc.gpsimd.tensor_tensor(mi[:, 0:2, :], mi[:, 0:2, :], mi[:, 2:4, :], ALU.add).then_inc(pair_sum, 1)
                            pool.wait_ge(pair_sum, 4 * n + 2 * h + 1)
                            nc.gpsimd.tensor_tensor(op[:, 0, r, :], mr[:, 0, :], mr[:, 1, :], ALU.add).then_inc(op_sum, 1)
                            pool.wait_ge(pair_sum, 4 * n + 2 * h + 2)
                            nc.gpsimd.tensor_tensor(op[:, 0, i, :], mi[:, 0, :], mi[:, 1, :], ALU.subtract).then_inc(op_sum, 1)
                            if h == 0:
                                pool.wait_ge(oprod, 9 * n + 5)
                                nc.gpsimd.tensor_tensor(op[:, 1, r, :], mhr[:, 0, :], mhr[:, 1, :], ALU.add).then_inc(op_sum, 1)
                                nc.gpsimd.tensor_tensor(op[:, 1, i, :], mhi[:, 0, :], mhi[:, 1, :], ALU.subtract).then_inc(op_sum, 1)

                    def next_rows(b):
                        pool.wait_ge(ve_ok, b + 1)
                        pool.wait_ge(cols_ok, 2 * b + 2)
                        nc.gpsimd.tensor_tensor(rsn[:, :], ve1[:, :], half[:, :], ALU.pow).then_inc(rsn_ok, 1)
                        pool.wait_ge(rsn_ok, 2 * b + 1)
                        nc.gpsimd.tensor_tensor(nbn[:, :], nm1[:, :], rsn[:, :], ALU.mult).then_inc(rsn_ok, 1)

                    def step(b, g, more, lead, rows):
                        if more:
                            fold_v(*ahead(b, g, 2))
                            fold_q(*ahead(b, g, 2))
                            rest_of_q(*ahead(b, g, 2))
                        if lead:
                            corr_sums(*ahead(b, g, 1))
                        out_sums(b, g)
                        if more:
                            fold_z(*ahead(b, g, 2))
                        if rows and g == GPB - 1:
                            next_rows(b)

                    fold_v(0, 0)
                    fold_q(0, 0)
                    fold_z(0, 0)
                    rest_of_q(0, 0)
                    fold_v(0, 1)
                    fold_q(0, 1)
                    corr_sums(0, 0)
                    rest_of_q(0, 1)
                    fold_z(0, 1)
                    for g in range(GPB):
                        step(0, g, True, True, True)
                    with pool.Fori(1, B // 2) as b:
                        for g in range(GPB):
                            step(b, g, True, True, True)
                    pool.wait_ge(top_ok, 1)
                    nc.gpsimd.partition_all_reduce(wtop[:, 1:2], wtop[:, 0:1], P, bass.bass_isa.ReduceOp.max).then_inc(topall_ok, 1)
                    with pool.Fori(B // 2, B - 2) as b:
                        for g in range(GPB):
                            step(b, g, True, True, True)
                    for g in range(GPB):
                        step(B - 2, g, True, True, False)
                    for g in range(GPB):
                        step(B - 1, g, g + 2 < GPB, g + 1 < GPB, False)

                @block.scalar
                def _(act):
                    def normalise(b, g):
                        k = g % 2
                        if g == 0 and later(b, g):
                            if not isinstance(b, int) or b > 1:
                                act.wait_ge(rsn_ok, 2 * b - 2)
                            nc.scalar.activation(rsb[:, :], rsn[:, :], ACT.Copy).then_inc(cols_ok, 1)
                            nc.scalar.activation(nbb[:, :], nbn[:, :], ACT.Copy).then_inc(cols_ok, 1)
                            act.wait_ge(cols_ok, 2 * b)
                        act.wait_ge(s_x[k], 16 * (2 * b + g // 2 + 1))
                        for t in range(TT):
                            nc.scalar.activation(xg[:, k, t, :], xg[:, k, t, :], ACT.Identity,
                                                 bias=nbb[:, t:t + 1], scale=rsb[:, t:t + 1]).then_inc(q_norm, 1)

                    def high_of_q(b, g):
                        m, k = GPB * b + g, g % 2
                        if later(b, g):
                            act.wait_ge(q_spec, 4 * m)
                        for h, src in enumerate((qa[:, :, :], xg[:, k, 0:2, :])):
                            act.wait_ge(q_fold, 2 * m + h + 1)
                            nc.scalar.activation(qh[:, 2 * h:2 * h + 2, :], src, ACT.Copy).then_inc(q_hi, 1)

                    def turn_row(b, g):
                        m = GPB * b + g
                        act.wait_ge(cp_sum, 2 * m + 2)
                        nc.scalar.activation(cp[0:1, EI, :], cp[0:1, EI, :], ACT.Copy, scale=-1.0).then_inc(cp_turn, 1)

                    def store_spectrum(b, g, which):
                        m, k, even, odd = GPB * b + g, g % 2, 4 * which + TURN[0], 4 * which + TURN[2]
                        spec, kept = ((v_spec, v_out), (z_spec, z_out))[which]
                        act.wait_ge(spec, 4 * m + 1)
                        nc.scalar.activation(spe[:, k, which, 0::2, :], ps[:, even, :].unsqueeze(1).broadcast_to([P, 2, GC]),
                                             ACT.Copy).then_inc(kept, 1)
                        act.wait_ge(spec, 4 * m + 2)
                        nc.scalar.activation(spe[:, k, which, 1, :], ps[:, even + 1, :], ACT.Copy, scale=nyq[:, 0:1]).then_inc(kept, 1)
                        act.wait_ge(kept, 4 * m + 1)
                        nc.scalar.activation(spe[0:1, k, which, 2, :], ps[0:1, even + 1, :], ACT.Copy).then_inc(kept, 1)
                        act.wait_ge(spec, 4 * m + 4)
                        nc.scalar.activation(spo[:, k, which, :, :], ps[:, odd:odd + 2, :], ACT.Copy).then_inc(kept, 1)

                    def corr_to_sbuf(b, g):
                        m = GPB * b + g
                        if later(b, g):
                            act.wait_ge(w_ready, 4 * m)
                        for j in range(CT):
                            act.wait_ge(corr_spec, 4 * m + j + 1)
                            nc.scalar.activation(eo[:, j, :], ps[:, TURN[j], :], ACT.Copy).then_inc(corr_out, 1)

                    def exponentials(b, g):
                        m = GPB * b + g
                        if later(b, g):
                            act.wait_ge(wt_spec, 4 * m)
                        act.wait_ge(nmax_ok, m + 1)
                        for j in range(CT):
                            nc.scalar.activation(wd[:, j, :], cr[:, j, :], ACT.Exp, bias=nmax[:, j:j + 1],
                                                 scale=1.0 / (QSCALE * TSCALE)).then_inc(exp_ok, 1)

                    def divide_w(b, g):
                        m = GPB * b + g
                        act.wait_ge(rz_ok, m + 1)
                        for j in range(CT):
                            nc.scalar.activation(wd[:, j, :], wd[:, j, :], ACT.Copy, scale=rz[:, j:j + 1]).then_inc(w_ready, 1)

                    def transposed_out(b, g):
                        n = GPB * b + g
                        if later(b, g):
                            act.wait_ge(w_spec, 8 * n)
                        for k in range(4):
                            act.wait_ge(wt_spec, 4 * n + k + 1)
                            nc.scalar.activation(wt[:, 0, k, :], ps[:, 4 + TURN[k], :], ACT.Copy, scale=WSCALE).then_inc(wt_hi, 1)

                    def weights_high(b, g, h):
                        m = piece(b, g, h)
                        if not (isinstance(m, int) and m == 0):
                            act.wait_ge(s_wst, 32 * m)
                        act.wait_ge(s_wc, 16 * m + 16)
                        nc.scalar.activation(wch[:, :], wc[:, :], ACT.Copy, scale=w_scale[:, 0:1]).then_inc(wch_ok, 1)

                    def step(b, g, more, lead, far, convert):
                        n = GPB * b + g
                        transposed_out(b, g)
                        if more:
                            high_of_q(*ahead(b, g, 2))
                        if lead:
                            store_spectrum(*ahead(b, g, 1), 1)
                        if convert:
                            weights_high(b, g, 0)
                        if lead:
                            turn_row(*ahead(b, g, 1))
                            corr_to_sbuf(*ahead(b, g, 1))
                        if convert:
                            weights_high(b, g, 1)
                        if more:
                            act.wait_ge(oprod, 9 * n + 9)
                            store_spectrum(*ahead(b, g, 2), 0)
                        if lead:
                            exponentials(*ahead(b, g, 1))
                        if far:
                            normalise(*ahead(b, g, 3))
                        if lead:
                            divide_w(*ahead(b, g, 1))

                    normalise(0, 0)
                    normalise(0, 1)
                    act.wait_ge(s_tabs, 64)
                    high_of_q(0, 0)
                    store_spectrum(0, 0, 0)
                    store_spectrum(0, 0, 1)
                    high_of_q(0, 1)
                    turn_row(0, 0)
                    corr_to_sbuf(0, 0)
                    store_spectrum(0, 1, 0)
                    exponentials(0, 0)
                    normalise(0, 2)
                    divide_w(0, 0)
                    for g in range(GPB):
                        step(0, g, True, True, True, False)
                    with act.Fori(1, B // 2) as b:
                        for g in range(GPB):
                            step(b, g, True, True, True, False)
                    act.wait_ge(scale_ok, 1)
                    for g in range(GPB):
                        step(B // 2, g, True, True, True, True)
                    with act.Fori(B // 2 + 1, B - 1) as b:
                        for g in range(GPB):
                            step(b, g, True, True, True, True)
                    for g in range(GPB):
                        step(B - 1, g, g + 2 < GPB, g + 1 < GPB, g + 3 < GPB, True)

                @block.tensor
                def _(pe):
                    def forward(bank, kind, src):
                        for k in range(2):
                            last = nc.tensor.matmul(ps[:, bank, :], ft[:, k, kind, :], src[k], start=(k == 0), stop=(k == 1))
                        return last

                    def forward_pair(bank, kind, pair, part):
                        for k in range(2):
                            for i, (tab, val) in enumerate(((0, 0), (1, 0), (0, 1))):
                                last = nc.tensor.matmul(ps[:, bank, :], fp[:, tab, k, kind, :], pair[val][:, 2 * part + k, :],
                                                        start=(k == 0 and i == 0), stop=(k == 1 and i == 2))
                        return last

                    def v_spectrum(b, g):
                        m, k = GPB * b + g, g % 2
                        pe.wait_ge(v_fold, 2 * m + 2)
                        for i in range(4):
                            if later(b, g):
                                pe.wait_ge(corr_out, 4 * m - 3 + i)
                            src = (va[:, 0, :], va[:, 1, :]) if i < 2 else (cg[:, k, 0, :], cg[:, k, 1, :])
                            forward(TURN[i], i, src).then_inc(v_spec, 1)

                    def q_spectrum(b, g):
                        m, k = GPB * b + g, g % 2
                        pe.wait_ge(q_lo, 2 * m + 2)
                        pe.wait_ge(v_out, 4 * m + 4)
                        for i in range(4):
                            forward_pair(i, i, (qh, ql[k]), i // 2).then_inc(q_spec, 1)

                    def z_spectrum(b, g):
                        m, k = GPB * b + g, g % 2
                        pe.wait_ge(z_fold, 2 * m + 2)
                        for i in range(4):
                            if later(b, g):
                                pe.wait_ge(wt_lo, 4 * m - 3 + i)
                            src = (zs[:, 0, :], zs[:, 1, :]) if i < 2 else (cg[:, k, 2, :], cg[:, k, 3, :])
                            forward(4 + TURN[i], i, src).then_inc(z_spec, 1)

                    def transpose_w(b, g):
                        n = GPB * b + g
                        pe.wait_ge(w_ready, 4 * n + 4)
                        for k in range(4):
                            if later(b, g):
                                pe.wait_ge(out_add, 4 * n - 3 + k)
                            for j in range(CT):
                                last = nc.tensor.transpose(ps[:, 4 + TURN[k], j * P:(j + 1) * P], wd[:, j, k * P:(k + 1) * P], ident[:, :])
                            last.then_inc(wt_spec, 1)

                    def weight_spectra(b, g, lead):
                        n = GPB * b + g
                        if lead:
                            pe.wait_ge(cprod, 4 * n + 8)
                        pe.wait_ge(wt_lo, 4 * n + 4)
                        for i in range(4):
                            forward_pair(i, (ER, EI)[i % 2], (wt[:, 0], wt[:, 1]), i // 2).then_inc(w_spec, 1)
                        if lead:
                            pe.wait_ge(z_out, 4 * n + 8)
                        for i in range(4):
                            forward_pair(4 + i, (OR, OI)[i % 2], (wt[:, 0], wt[:, 1]), i // 2).then_inc(w_spec, 1)

                    def correlation(b, g):
                        m = GPB * b + g
                        pe.wait_ge(cp_turn, m + 1)
                        for j in range(CT):
                            if later(b, g):
                                pe.wait_ge(oprod, 9 * m - (6 if j < 2 else 4))
                            for h in range(2):
                                for i in range(2):
                                    s = 2 * h + i
                                    last = nc.tensor.matmul(ps[:, TURN[j], h * HALF:(h + 1) * HALF], cp[:, s, j * P:(j + 1) * P],
                                                            it[:, s, :], start=(i == 0), stop=(i == 1))
                            last.then_inc(corr_spec, 1)

                    def output(b, g):
                        n = GPB * b + g
                        pe.wait_ge(oprod, 9 * n + 9)
                        pe.wait_ge(hi_sum, 3 * n + 3)
                        for t in TURN:
                            if t == 0:
                                pe.wait_ge(op_sum, 6 * n + 6)
                            for s in range(4):
                                last = nc.tensor.matmul(ps[:, 4 + t, :], it[:, s, (t % 2) * P:(t % 2 + 1) * P], op[:, t // 2, s, :],
                                                        start=(s == 0), stop=(s == 3))
                            last.then_inc(out_spec, 1)

                    def step(b, g, more, lead):
                        if lead:
                            q_spectrum(*ahead(b, g, 1))
                        transpose_w(b, g)
                        if lead:
                            z_spectrum(*ahead(b, g, 1))
                        weight_spectra(b, g, lead)
                        if lead:
                            correlation(*ahead(b, g, 1))
                        if more:
                            v_spectrum(*ahead(b, g, 2))
                        output(b, g)

                    pe.wait_ge(s_tabs, 64)
                    v_spectrum(0, 0)
                    q_spectrum(0, 0)
                    z_spectrum(0, 0)
                    correlation(0, 0)
                    v_spectrum(0, 1)
                    for g in range(GPB):
                        step(0, g, True, True)
                    with pe.Fori(1, B - 1) as b:
                        for g in range(GPB):
                            step(b, g, True, True)
                    for g in range(GPB):
                        step(B - 1, g, g + 2 < GPB, g + 1 < GPB)

                @block.vector
                def _(dve):
                    def corr_products_even(b, g):
                        m, k = GPB * b + g, g % 2
                        if later(b, g) and later(b, g - 1):
                            dve.wait_ge(op_sum, 6 * m - 6)
                        dve.wait_ge(v_out, 4 * m + 4)
                        dve.wait_ge(q_spec, 4 * m + 2)
                        nc.vector.tensor_tensor(mr[:, 0:2, :], ps[:, 0:2, :], spe[:, k, 0, 0:2, :], ALU.mult).then_inc(cprod, 1)
                        nc.vector.tensor_tensor(mi[:, 0:2, :], ps[:, 0:2, :], spe[:, k, 0, 1:3, :], ALU.mult).then_inc(cprod, 1)

                    def corr_products_odd(b, g):
                        m, k = GPB * b + g, g % 2
                        dve.wait_ge(q_spec, 4 * m + 4)
                        nc.vector.tensor_tensor(mr[:, 2:4, :], ps[:, 2:4, :], spo[:, k, 0, :, :], ALU.mult).then_inc(cprod, 1)
                        nc.vector.tensor_tensor(mi[:, 2:4, :], ps[:, 2:4, :], spo[:, k, 0, ::-1, :], ALU.mult).then_inc(cprod, 1)

                    def weights_rest(b, g, h):
                        dve.wait_ge(wch_ok, piece(b, g, h) + 1)
                        nc.vector.scalar_tensor_tensor(out=wcl, in0=wc[:, :], scalar=w_scale[:, 0:1], in1=wch[:, :],
                                                       op0=ALU.mult, op1=ALU.subtract).then_inc(wcl_ok, 1)

                    def largest_weight(b, g):
                        n = GPB * b + g
                        dst = (wnew if later(b, 0) else wmax)[:, g:g + 1]
                        dve.wait_ge(s_wx, 16 * n + 16)
                        nc.vector.tensor_reduce(dst, xrow[:, :], AXX, ALU.max, apply_absolute_value=True).then_inc(wx_used, 1)
                        if later(b, 0):
                            dve.wait_ge(wx_used, n + 1)
                            nc.vector.tensor_tensor(wmax[:, g:g + 1], wmax[:, g:g + 1], wnew[:, g:g + 1], ALU.max).then_inc(wmax_ok, 1)

                    def weight_scales():
                        dve.sem_clear(own)
                        dve.wait_ge(wmax_ok, KT - GPB)
                        nc.vector.tensor_reduce(wtop[:, 0:1], wmax[:, :], AXX, ALU.max).then_inc(top_ok, 1)
                        dve.wait_ge(topall_ok, 1)
                        nc.vector.tensor_scalar(wtop[:, 1:2], wtop[:, 1:2], 1e-30, None, ALU.max).then_inc(own, 1)
                        dve.wait_ge(own, 1)
                        nc.vector.tensor_scalar(wtop[:, 2:3].bitcast(U32), wtop[:, 1:2].bitcast(U32), 0x7F800000, None, ALU.bitwise_and).then_inc(own, 1)
                        dve.wait_ge(own, 2)
                        nc.vector.reciprocal(wtop[:, 3:4], wtop[:, 2:3]).then_inc(own, 1)
                        nc.vector.tensor_scalar(w_back[:, :], wtop[:, 2:3], 1.0 / (16384.0 * HSCALE), None, ALU.mult)
                        dve.wait_ge(own, 3)
                        nc.vector.tensor_scalar(w_scale[:, :], wtop[:, 3:4], 16384.0, None, ALU.mult).then_inc(scale_ok, 1)

                    def row_statistics(b, g):
                        n = GPB * b + g
                        dve.sem_clear(own)
                        dve.wait_ge(s_xrow, 16 * n + 16)
                        for c in range(4):
                            nc.vector.bn_stats(bn1[:, 6 * c:6 * c + 6], xrow[:, c * 512:(c + 1) * 512]).then_inc(own, 1)
                        dve.wait_ge(own, 4)
                        nc.vector.bn_aggr(mv1[:, g, :], bn1[:, :]).then_inc(row_used, 1)
                        if g == GPB - 1:
                            dve.wait_ge(row_used, n + 1)
                            if later(b, 0):
                                dve.wait_ge(rsn_ok, 2 * b)
                            nc.vector.tensor_scalar(nm1[:, :], mv1[:, :, 0], -1.0, None, ALU.mult)
                            nc.vector.tensor_scalar(ve1[:, :], mv1[:, :, 1], EPS, QSCALE ** -2, ALU.add, ALU.mult).then_inc(ve_ok, 1)

                    def w_rest(b, g):
                        n = GPB * b + g
                        if later(b, g):
                            dve.wait_ge(w_spec, 8 * n)
                        for k in range(4):
                            dve.wait_ge(wt_hi, 4 * n + k + 1)
                            nc.vector.scalar_tensor_tensor(out=wt[:, 1, k, :], in0=ps[:, 4 + TURN[k], :], scalar=WSCALE, in1=wt[:, 0, k, :],
                                                           op0=ALU.mult, op1=ALU.subtract).then_inc(wt_lo, 1)

                    def out_products(b, g, lead, convert):
                        n, k = GPB * b + g, g % 2
                        dve.wait_ge(z_out, 4 * n + 4)
                        for h in range(2):
                            if h == 0:
                                dve.wait_ge(cp_sum, 2 * n + (4 if lead else 2))
                            else:
                                if not convert:
                                    largest_weight(b, g)
                                dve.wait_ge(op_sum, 6 * n + 1)
                            dve.wait_ge(w_spec, 8 * n + 4 * h + 4)
                            split = "p (a r) c -> p a r c"
                            wl, wlh = ps[:, 4 * h:4 * h + 2, :], ps[:, 4 * h:4 * h + 4, :].rearrange(split, a=2)
                            if h == 0:
                                v_r, v_i, z_r, z_i = spe[:, k, :, 0:2, :], spe[:, k, :, 1:3, :], spe[:, k, 1, 0:2, :], spe[:, k, 1, 1:3, :]
                            else:
                                v_r, v_i, z_r, z_i = spo[:, k, :, :, :], spo[:, k, :, ::-1, :], spo[:, k, 1, :, :], spo[:, k, 1, ::-1, :]
                            nc.vector.tensor_tensor(mr[:, :, :].rearrange(split, a=2), wlh, v_r, ALU.mult).then_inc(oprod, 1)
                            if h == 1:
                                dve.wait_ge(op_sum, 6 * n + 2)
                            nc.vector.tensor_tensor(mi[:, :, :].rearrange(split, a=2), wlh, v_i, ALU.mult).then_inc(oprod, 1)
                            if h == 0:
                                dve.wait_ge(s_xr, 32 * n + 32)
                                nc.vector.scalar_tensor_tensor(out=vlast[:, :], in0=ps[0:1, 2, :], scalar=float(L), in1=vlast[:, :],
                                                               op0=ALU.mult, op1=ALU.mult).then_inc(oprod, 1)
                            else:
                                dve.wait_ge(op_sum, 6 * n + 4)
                            nc.vector.tensor_tensor(mhr[:, :, :], wl, z_r, ALU.mult).then_inc(oprod, 1)
                            nc.vector.tensor_tensor(mhi[:, :, :], wl, z_i, ALU.mult).then_inc(oprod, 1)
                        nc.vector.tensor_tensor(op[0:1, 1, ER, :], op[0:1, 1, ER, :], vlast[:, :], ALU.add).then_inc(hi_sum, 1)
                        dve.wait_ge(oprod, 9 * n + 8)
                        nc.vector.tensor_tensor(op[:, 1, OR, :], mhr[:, 0, :], mhr[:, 1, :], ALU.add).then_inc(hi_sum, 1)
                        dve.wait_ge(oprod, 9 * n + 9)
                        nc.vector.tensor_tensor(op[:, 1, OI, :], mhi[:, 0, :], mhi[:, 1, :], ALU.subtract).then_inc(hi_sum, 1)

                    def top_lags(b, g):
                        m = GPB * b + g
                        dve.sem_clear(own)
                        if later(b, g):
                            dve.wait_ge(exp_ok, 4 * m)
                        for j in range(CT):
                            dve.wait_ge(corr_out, 4 * m + j + 1)
                            nc.vector.tensor_tensor(cr[:, j, 0:HALF], eo[:, j, 0:HALF], eo[:, j, HALF:L], ALU.add)
                            nc.vector.tensor_tensor(cr[:, j, HALF:L], eo[:, j, 0:HALF], eo[:, j, HALF:L], ALU.subtract).then_inc(own, 1)
                        for j in range(CT):
                            dve.wait_ge(own, j + 1)
                            nc.vector.max(m16[:, j, 0:8], cr[:, j, :]).then_inc(own, 1)
                        dve.wait_ge(own, 2 * CT)
                        nc.vector.tensor_scalar(nmax[:, :], m16[:, :, 0], -1.0 / (QSCALE * TSCALE), None, ALU.mult).then_inc(nmax_ok, 1)
                        for j in range(CT):
                            nc.vector.match_replace(eo[:, j, :], m16[:, j, 0:8], cr[:, j, :], NEG).then_inc(own, 1)
                        for j in range(CT):
                            dve.wait_ge(own, 2 * CT + j + 1)
                            nc.vector.max(m16[:, j, 8:16], eo[:, j, :]).then_inc(own, 1)
                        dve.wait_ge(own, 4 * CT)
                        nc.vector.memset(m16[:, :, TOPK:16], NEG).then_inc(own, 1)
                        dve.wait_ge(own, 4 * CT + 1)
                        for j in range(CT):
                            nc.vector.match_replace(eo[:, j, :], m16[:, j, 8:16], eo[:, j, :], NEG).then_inc(own, 1)
                        dve.wait_ge(exp_ok, 4 * m + 4)
                        for j in range(CT):
                            dve.wait_ge(own, 4 * CT + j + 2)
                            nc.vector.scalar_tensor_tensor(out=wd[:, j, :], in0=eo[:, j, :], scalar=NEG, in1=wd[:, j, :],
                                                           op0=ALU.is_le, op1=ALU.mult, accum_out=zsum[:, j:j + 1]).then_inc(own, 1)
                        dve.wait_ge(own, 6 * CT + 1)
                        if later(b, g):
                            dve.wait_ge(w_ready, 4 * m)
                        nc.vector.reciprocal(rz[:, :], zsum[:, :]).then_inc(rz_ok, 1)

                    def add_output(b, g):
                        n = GPB * b + g
                        for i, t in enumerate(TURN):
                            dve.wait_ge(out_spec, 4 * n + i + 1)
                            nc.vector.scalar_tensor_tensor(out=xv[:, t, :], in0=ps[:, 4 + t, :], scalar=1.0 / (WSCALE * TSCALE),
                                                           in1=xv[:, t, :], op0=ALU.mult, op1=ALU.add).then_inc(out_add, 1)

                    def step(b, g, lead, rows, convert):
                        if lead:
                            corr_products_even(*ahead(b, g, 1))
                        w_rest(b, g)
                        if lead:
                            corr_products_odd(*ahead(b, g, 1))
                        if rows:
                            row_statistics(b, g)
                        if convert:
                            weights_rest(b, g, 0)
                        out_products(b, g, lead, convert)
                        if convert:
                            weights_rest(b, g, 1)
                        if lead:
                            top_lags(*ahead(b, g, 1))
                        add_output(b, g)

                    corr_products_even(0, 0)
                    corr_products_odd(0, 0)
                    top_lags(0, 0)
                    for g in range(GPB):
                        step(0, g, True, True, False)
                    with dve.Fori(1, B // 2) as b:
                        for g in range(GPB):
                            step(b, g, True, True, False)
                    weight_scales()
                    with dve.Fori(B // 2, B - 2) as b:
                        for g in range(GPB):
                            step(b, g, True, True, True)
                    for g in range(GPB):
                        step(B - 2, g, True, False, True)
                    for g in range(GPB):
                        step(B - 1, g, g + 1 < GPB, False, True)

        mid.close()

        with ExitStack() as st:
            w_hi = sb("w_hi", [P, KT, D], FP16, st)
            w_lo = sb("w_lo", [P, KT, D], FP16, st)
            a_f = sb("a_f", [P, 2, KT, RANK], FP32, st)
            a_hi = sb("a_hi", [P, KT, 2, RANK], FP16, st)
            a_lo = sb("a_lo", [P, KT, 2, RANK], FP16, st)
            xt = sb("xt", [P, 2, D], FP32, st)
            h = sb("h", [P, D], FP32, st)
            h_hi = sb("h_hi", [P, 2, KT, P], FP16, st)
            h_lo = sb("h_lo", [P, 2, KT, P], FP16, st)
            b_f = sb("b_f", [4 * RANK, D], FP32, st)
            b_hi = sb("b_hi", [4 * RANK, D], FP16, st)
            b_lo = sb("b_lo", [2 * RANK, D], FP16, st)
            brow = sb("brow", [P, D], FP32, st)
            bn2 = sb("bn2", [P, 4, 6], FP32, st)
            mv2 = sb("mv2", [P, 2], FP32, st)
            ve2 = sb("ve2", [P, 1], FP32, st)
            rp2 = sb("rp2", [P, 1], FP32, st)
            rs2 = sb("rs2", [P, 1], FP32, st)
            nb2 = sb("nb2", [P, 1], FP32, st)
            ax = sb("ax", [P, 2, 2 * RANK], FP32, st)
            axT = sb("axT", [4 * RANK, P], FP16, st)

            s_row = sem("s_row", st)
            s_brow = sem("s_brow", st)
            s_ab = sem("s_ab", st)
            ab_hi = sem("ab_hi", st)
            ab_lo = sem("ab_lo", st)
            s_w = [sem(f"s_w{k}", st) for k in range(8)]
            s_xt = [sem(f"s_xt{k}", st) for k in range(2)]
            s_out = [sem(f"s_out{k}", st) for k in range(2)]
            own2 = sem("own2", st)
            ve_ok = sem("ve_ok", st)
            rp_ok = sem("rp_ok", st)
            nb_ok = sem("nb_ok", st)
            h_ok = sem("h_ok", st)
            bias_ok = sem("bias_ok", st)
            ht_spec = sem("ht_spec", st)
            hi_ok = sem("hi_ok", st)
            lo_ok = sem("lo_ok", st)
            ax_spec = sem("ax_spec", st)
            ax_ok = sem("ax_ok", st)
            axt_spec = sem("axt_spec", st)
            axt_hi = sem("axt_hi", st)
            axt_lo = sem("axt_lo", st)
            d_spec = sem("d_spec", st)
            d_ok = sem("d_ok", st)
            y_spec = sem("y_spec", st)
            y_ok = sem("y_ok", st)

            with nc.Block() as block:
                out_t = out.rearrange("b (t p) c -> b p t c", p=P)

                @block.sync
                def _(sp):
                    def load(b, t):
                        sp.dma_start(xt[:, t % 2, :], x2_g[b, :, t, :]).then_inc(s_xt[t % 2], 16)

                    def load_ab(b):
                        sp.dma_start(a_f[:, 0, :, :].rearrange("p k r -> p (k r)"), aeff[b]).then_inc(s_ab, 16)
                        for k in (0, 2 * RANK):
                            sp.dma_start(b_f[k:k + RANK, :], beff[bass.ts(b, RANK), :]).then_inc(s_ab, 16)

                    load(0, 0)
                    load_ab(0)
                    sp.dma_start(a_f[:, 1, :, :].rearrange("p k r -> p (k r)"), aeff[B]).then_inc(s_row, 16)
                    for k in (RANK, 3 * RANK):
                        sp.dma_start(b_f[k:k + RANK, :], lora_bsT).then_inc(s_row, 16)
                    for c in range(4):
                        cols = slice(c * 512, (c + 1) * 512)
                        for part in range(2):
                            ks = slice(part * KT // 2, (part + 1) * KT // 2)
                            for a, dst in enumerate((w_hi, w_lo)):
                                sp.dma_start(dst[:, ks, cols], w_pair[a, ks, :, cols].rearrange("k p o -> p k o")).then_inc(s_w[2 * c + part], 16)
                        if c == 0:
                            sp.dma_start(brow[:, :], bias.partition_broadcast(P)).then_inc(s_brow, 16)
                            load(0, 1)

                    def step(b, t, more):
                        n = TT * b + t
                        sp.wait_ge(y_ok, 4 * n + 4)
                        sp.dma_start(out_t[b, :, t, :], xt[:, t % 2, :]).then_inc(s_out[t % 2], 16)
                        if more:
                            if t == 0 and not (isinstance(b, int) and b == B - 1):
                                sp.wait_ge(ab_lo, 2 * b + 2)
                                load_ab(b + 1)
                            sp.wait_ge(s_out[t % 2], 16 * (2 * b + t // 2 + 1))
                            load(*ahead(b, t, 2))

                    for t in range(TT):
                        step(0, t, True)
                    with sp.Fori(1, B - 1) as b:
                        for t in range(TT):
                            step(b, t, True)
                    for t in range(TT):
                        step(B - 1, t, t + 2 < TT)
                    for k in range(2):
                        sp.wait_ge(s_out[k], 16 * NT // 2)

                @block.gpsimd
                def _(pool):
                    def prepare(b, t):
                        n = TT * b + t
                        pool.wait_ge(ve_ok, n + 1)
                        nc.gpsimd.tensor_tensor(rp2[:, :], ve2[:, :], half[:, 0:1], ALU.pow).then_inc(rp_ok, 1)
                        pool.wait_ge(h_ok, n + 1)
                        if not later(b, t):
                            pool.wait_ge(s_brow, 16)
                        nc.gpsimd.tensor_tensor(xt[:, t % 2, :], xt[:, t % 2, :], brow[:, :], ALU.add).then_inc(bias_ok, 1)

                    for t in range(TT):
                        prepare(0, t)
                    with pool.Fori(1, B) as b:
                        for t in range(TT):
                            prepare(b, t)

                @block.scalar
                def _(act):
                    def normalise(b, t):
                        n, k = TT * b + t, t % 2
                        act.wait_ge(s_xt[k], 16 * (2 * b + t // 2 + 1))
                        act.wait_ge(nb_ok, n + 1)
                        if later(b, t):
                            act.wait_ge(ht_spec, 4 * n)
                        nc.scalar.activation(h[:, :], xt[:, k, :], ACT.Identity, bias=nb2[:, 0:1], scale=rs2[:, 0:1]).then_inc(h_ok, 1)

                    def high_of_h(b, t):
                        n, k = TT * b + t, t % 2
                        if later(b, t) and later(b, t - 1):
                            act.wait_ge(y_spec, 4 * n - 4)
                        for q in range(4):
                            act.wait_ge(ht_spec, 4 * n + q + 1)
                            nc.scalar.activation(h_hi[:, k, 4 * q:4 * q + 4, :], ps[:, 4 + q, :].rearrange("p (c t) -> p c t", t=P),
                                                 ACT.Copy).then_inc(hi_ok, 1)

                    def high_of_ax(b, t):
                        n = TT * b + t
                        act.wait_ge(axt_spec, n + 1)
                        if later(b, t):
                            act.wait_ge(d_spec, 4 * n)
                        nc.scalar.activation(axT[:, :], ps[:, 5, 0:P], ACT.Copy).then_inc(axt_hi, 1)

                    def high_of_ab(b):
                        act.wait_ge(s_ab, 48 * b + 48)
                        if later(b, 0):
                            act.wait_ge(ax_spec, TT * b)
                        nc.scalar.activation(a_hi[:, :, :, :].rearrange("p k s r -> p s k r"), a_f[:, :, :, :], ACT.Copy,
                                             scale=a_scale[:, 0:1]).then_inc(ab_hi, 1)
                        if later(b, 0):
                            act.wait_ge(d_spec, 4 * TT * b)
                        nc.scalar.activation(b_hi[:, :], b_f[:, :], ACT.Copy, scale=b_scale[:, 0:1]).then_inc(ab_hi, 1)

                    def step(b, t, more):
                        high_of_ax(b, t)
                        if more:
                            normalise(*ahead(b, t, 1))
                            if t == TT - 1:
                                high_of_ab(b + 1)
                            high_of_h(*ahead(b, t, 1))

                    normalise(0, 0)
                    act.wait_ge(s_row, 48)
                    high_of_ab(0)
                    high_of_h(0, 0)
                    for t in range(TT):
                        step(0, t, True)
                    with act.Fori(1, B - 1) as b:
                        for t in range(TT):
                            step(b, t, True)
                    for t in range(TT):
                        step(B - 1, t, t + 1 < TT)

                @block.tensor
                def _(pe):
                    def transposes(b, t):
                        n = TT * b + t
                        pe.wait_ge(h_ok, n + 1)
                        if later(b, t):
                            pe.wait_ge(d_ok, 4 * n)
                        for q in range(4):
                            for c in range(4):
                                i = 4 * q + c
                                last = nc.tensor.transpose(ps[:, 4 + q, c * P:(c + 1) * P], h[:, i * P:(i + 1) * P], ident[:, :])
                            last.then_inc(ht_spec, 1)

                    def adapter_in(b, t):
                        n, k = TT * b + t, t % 2
                        pe.wait_ge(hi_ok, 4 * n + 4)
                        pe.wait_ge(lo_ok, 4 * n + 4)
                        if t == 0:
                            pe.wait_ge(ab_lo, 2 * b + 1)
                        dst = ps[:, 4, 0:2 * RANK]
                        for i in range(KT):
                            high, rest = (a[:, i, :, :].rearrange("p s r -> p (s r)") for a in (a_hi, a_lo))
                            nc.tensor.matmul(dst, h_hi[:, k, i, :], high, start=(i == 0), stop=False)
                            nc.tensor.matmul(dst, h_hi[:, k, i, :], rest, start=False, stop=False)
                            last = nc.tensor.matmul(dst, h_lo[:, k, i, :], high, start=False, stop=(i == KT - 1))
                        last.then_inc(ax_spec, 1)

                    def chunk(b, t, c):
                        n, k = TT * b + t, t % 2
                        if later(b, t):
                            pe.wait_ge(y_ok, 4 * n)
                        cols = slice(c * 512, (c + 1) * 512)
                        for i in range(KT):
                            if not later(b, t) and i % (KT // 2) == 0:
                                pe.wait_ge(s_w[2 * c + i // (KT // 2)], 32)
                            nc.tensor.matmul(ps[:, c, :], h_hi[:, k, i, :], w_hi[:, i, cols], start=(i == 0), stop=False)
                            nc.tensor.matmul(ps[:, c, :], h_hi[:, k, i, :], w_lo[:, i, cols], start=False, stop=False)
                            last = nc.tensor.matmul(ps[:, c, :], h_lo[:, k, i, :], w_hi[:, i, cols], start=False, stop=(i == KT - 1))
                            if c == 0 and i == KT // 2:
                                pe.wait_ge(ax_ok, n + 1)
                                nc.tensor.transpose(ps[:, 5, 0:P], ax[:, :, :].rearrange("p s r -> p (s r)"), ident[:, :]).then_inc(axt_spec, 1)
                        last.then_inc(y_spec, 1)

                    def adapter_out(b, t):
                        n = TT * b + t
                        pe.wait_ge(axt_lo, n + 1)
                        if t == 0:
                            pe.wait_ge(ab_lo, 2 * b + 2)
                        for c in range(4):
                            cols = slice(c * 512, (c + 1) * 512)
                            nc.tensor.matmul(ps[:, 4 + c, :], axT[:, :], b_hi[:, cols], start=True, stop=False)
                            nc.tensor.matmul(ps[:, 4 + c, :], axT[0:2 * RANK, :], b_lo[:, cols], start=False, stop=True).then_inc(d_spec, 1)

                    def step(b, t, more):
                        nxt = ahead(b, t, 1)
                        chunk(b, t, 0)
                        adapter_out(b, t)
                        chunk(b, t, 1)
                        if more:
                            transposes(*nxt)
                        chunk(b, t, 2)
                        chunk(b, t, 3)
                        if more:
                            adapter_in(*nxt)

                    transposes(0, 0)
                    adapter_in(0, 0)
                    for t in range(TT):
                        step(0, t, True)
                    with pe.Fori(1, B - 1) as b:
                        for t in range(TT):
                            step(b, t, True)
                    for t in range(TT):
                        step(B - 1, t, t + 1 < TT)

                @block.vector
                def _(dve):
                    def statistics(b, t):
                        n, k = TT * b + t, t % 2
                        dve.sem_clear(own2)
                        dve.wait_ge(s_xt[k], 16 * (2 * b + t // 2 + 1))
                        for c in range(4):
                            last = nc.vector.bn_stats(bn2[:, c, :], xt[:, k, c * 512:(c + 1) * 512])
                        last.then_inc(own2, 1)
                        dve.wait_ge(own2, 1)
                        nc.vector.bn_aggr(mv2[:, :], bn2[:, :, :].rearrange("p c s -> p (c s)")).then_inc(own2, 1)
                        dve.wait_ge(own2, 2)
                        nc.vector.tensor_scalar(ve2[:, :], mv2[:, 1:2], EPS, None, ALU.add).then_inc(ve_ok, 1)
                        dve.wait_ge(rp_ok, n + 1)
                        if later(b, t):
                            dve.wait_ge(h_ok, n)
                        nc.vector.tensor_scalar(rs2[:, :], rp2[:, :], HSCALE, None, ALU.mult).then_inc(own2, 1)
                        dve.wait_ge(own2, 3)
                        nc.vector.tensor_scalar(nb2[:, :], mv2[:, 0:1], rs2[:, 0:1], -1.0, ALU.mult, ALU.mult).then_inc(nb_ok, 1)

                    def rest_of_h(b, t):
                        n, k = TT * b + t, t % 2
                        for q in range(4):
                            dve.wait_ge(hi_ok, 4 * n + q + 1)
                            nc.vector.tensor_tensor(h_lo[:, k, 4 * q:4 * q + 4, :], ps[:, 4 + q, :].rearrange("p (c t) -> p c t", t=P),
                                                    h_hi[:, k, 4 * q:4 * q + 4, :], ALU.subtract).then_inc(lo_ok, 1)

                    def adapter(b, t):
                        n = TT * b + t
                        dve.wait_ge(ax_spec, n + 1)
                        if later(b, t):
                            dve.wait_ge(axt_spec, n)
                        nc.vector.tensor_scalar(ax[:, :, :], ps[:, 4, 0:2 * RANK].unsqueeze(1).broadcast_to([P, 2, 2 * RANK]), AXSCALE,
                                                None, ALU.mult).then_inc(ax_ok, 1)

                    def rest_of_ax(b, t):
                        n, rows = TT * b + t, slice(2 * RANK, 4 * RANK)
                        dve.wait_ge(axt_hi, n + 1)
                        nc.vector.tensor_tensor(axT[rows, :], ps[rows, 5, 0:P], axT[rows, :], ALU.subtract).then_inc(axt_lo, 1)

                    def rest_of_ab(b):
                        dve.wait_ge(ab_hi, 2 * b + 1)
                        for s in range(2):
                            last = nc.vector.scalar_tensor_tensor(out=a_lo[:, :, s, :], in0=a_f[:, s, :, :], scalar=a_scale[:, 0:1],
                                                                  in1=a_hi[:, :, s, :], op0=ALU.mult, op1=ALU.subtract)
                        last.then_inc(ab_lo, 1)
                        dve.wait_ge(ab_hi, 2 * b + 2)
                        nc.vector.scalar_tensor_tensor(out=b_lo[:, :], in0=b_f[0:2 * RANK, :], scalar=b_scale[0:2 * RANK, 0:1],
                                                       in1=b_hi[0:2 * RANK, :], op0=ALU.mult, op1=ALU.subtract).then_inc(ab_lo, 1)

                    def add_adapter(b, t):
                        n, k = TT * b + t, t % 2
                        for c in range(4):
                            dve.wait_ge(d_spec, 4 * n + c + 1)
                            cols = slice(c * 512, (c + 1) * 512)
                            nc.vector.scalar_tensor_tensor(out=xt[:, k, cols], in0=ps[:, 4 + c, :], scalar=d_back[:, 0:1],
                                                           in1=xt[:, k, cols], op0=ALU.mult, op1=ALU.add).then_inc(d_ok, 1)

                    def finish(b, t, c):
                        n, k = TT * b + t, t % 2
                        if c == 0:
                            dve.wait_ge(bias_ok, n + 1)
                        dve.wait_ge(y_spec, 4 * n + c + 1)
                        if c:
                            dve.wait_ge(d_ok, 4 * n + c + 1)
                        cols = slice(c * 512, (c + 1) * 512)
                        nc.vector.scalar_tensor_tensor(out=xt[:, k, cols], in0=ps[:, c, :], scalar=w_back[:, 0:1], in1=xt[:, k, cols],
                                                       op0=ALU.mult, op1=ALU.add).then_inc(y_ok, 1)

                    def step(b, t, more):
                        n, nxt = TT * b + t, ahead(b, t, 1)
                        rest_of_ax(b, t)
                        if more:
                            statistics(*nxt)
                        finish(b, t, 0)
                        dve.wait_ge(y_ok, 4 * n + 1)
                        add_adapter(b, t)
                        if more and t == TT - 1:
                            rest_of_ab(b + 1)
                        finish(b, t, 1)
                        if more:
                            rest_of_h(*nxt)
                        finish(b, t, 2)
                        finish(b, t, 3)
                        if more:
                            adapter(*nxt)

                    statistics(0, 0)
                    rest_of_ab(0)
                    rest_of_h(0, 0)
                    adapter(0, 0)
                    for t in range(TT):
                        step(0, t, True)
                    with dve.Fori(1, B - 1) as b:
                        for t in range(TT):
                            step(b, t, True)
                    for t in range(TT):
                        step(B - 1, t, t + 1 < TT)


def kernel(x, ctx_4096, L0_ffn_gate, L0_ffn_kernel, L0_ffn_bias, L0_ffn_lora_A, L0_ffn_lora_B,
           L0_ffn_lora_A_shared, L0_ffn_lora_B_shared):
    import concourse.bacc as bacc
    from concourse.bass_utils import run_bass_kernel_spmd

    fwd_tab, fwd_pair, inv_tab = dft_tables()
    nyq_mask = np.ones((P, 1), np.float32)
    nyq_mask[0] = 0.0
    arrays = {
        "x": np.ascontiguousarray(x),
        "ctx": np.ascontiguousarray(ctx_4096),
        "gateT": np.ascontiguousarray(np.asarray(L0_ffn_gate).T),
        "w": np.ascontiguousarray(L0_ffn_kernel),
        "bias": np.ascontiguousarray(L0_ffn_bias),
        "lora_a": np.ascontiguousarray(np.asarray(L0_ffn_lora_A).reshape(NL * RANK, D)),
        "lora_bT": np.ascontiguousarray(np.asarray(L0_ffn_lora_B).transpose(0, 2, 1).reshape(NL * RANK, D)),
        "lora_as": np.ascontiguousarray(L0_ffn_lora_A_shared),
        "lora_bsT": np.ascontiguousarray(np.asarray(L0_ffn_lora_B_shared).T),
        "fwd_tab": fwd_tab,
        "inv_tab": inv_tab,
        "eye": np.eye(P, dtype=np.float32),
        "rank_sel": np.ascontiguousarray(np.tile(np.eye(RANK, dtype=np.float32), (P // RANK, 1))),
        "nyq_mask": nyq_mask,
        "fwd_pair": fwd_pair,
    }
    nc = bacc.Bacc("TRN2", target_bir_lowering=False, num_devices=1)
    args = [nc.dram_tensor(name, a.shape, mybir.dt.from_np(a.dtype), kind="ExternalInput").ap() for name, a in arrays.items()]
    args.append(nc.dram_tensor("out", (B, L, D), FP32, kind="ExternalOutput").ap())
    build(nc, *args)
    r = run_bass_kernel_spmd(nc, [arrays], core_ids=[0])
    return r.results[0]["out"]
```
